# Optimizing a Trainium2 kernel written in Bass

```python
import numpy as np
import jax
import jax.numpy as jnp

def _softmax(x, axis=-1):
    return jax.nn.softmax(x, axis=axis)

def _gelu(x):
    return jax.nn.gelu(x, approximate=True)

def _silu(x):
    return jax.nn.silu(x)

def _sigmoid(x):
    return jax.nn.sigmoid(x)

def _layernorm(x, axis=-1, eps=1e-05):
    m = jnp.mean(x, axis=axis, keepdims=True)
    v = jnp.var(x, axis=axis, keepdims=True)
    return (x - m) / jnp.sqrt(v + eps)

def _scatter_add(tgt, idx, src, axis=0):
    return tgt.at[idx].add(src)

def _segment_sum(src, seg, n):
    return jax.ops.segment_sum(src, seg, n)
kernel_name = 'mk_xattn_ffn_d2_seqx_r4_a11541'

def setup_inputs(seed: int=0):
    np.random.seed(seed)
    _w = jnp.asarray

    def _rec_inputs():
        import jax
        import jax.numpy as jnp
        _rk = jax.random.key(seed)
        x = -0.0002928 + 1 * jax.random.normal(jax.random.fold_in(_rk, 1), (4, 512, 256), jnp.float32)
        _lenS = 512 - jax.random.randint(jax.random.fold_in(_rk, 7), (4,), 0, max(1, 512 // 4) + 1, jnp.int32)
        _lenS2 = 512 - jax.random.randint(jax.random.fold_in(_rk, 8), (4,), 0, max(1, 512 // 4) + 1, jnp.int32)
        _ctx_1024P = jax.random.normal(jax.random.fold_in(_rk, 11), (4, 16, 256), jnp.float32)
        _ctx_1024c = jax.random.dirichlet(jax.random.fold_in(_rk, 511), 0.3 * jnp.ones((16,), jnp.float32), (4, 512))
        _ctx_1024t = jnp.einsum('bsk,bkd->bsd', _ctx_1024c, _ctx_1024P)
        _ctx_1024t = _ctx_1024t * jax.lax.rsqrt(jnp.mean(jnp.square(_ctx_1024t)) + 1e-12) * 0.953939
        ctx_1024 = -1.39393e-06 + 0.999914 * (_ctx_1024t + 0.3 * jax.random.normal(jax.random.fold_in(_rk, 611), (4, 512, 256), jnp.float32))
        return (x, ctx_1024)
    x, ctx_1024 = _rec_inputs()

    def _L0_xattn_setup():
        import jax, jax.numpy as jnp
        import numpy as np
        import math
        HIDDEN = 256
        HEADS = 16
        HEAD = HIDDEN // HEADS
        SCALE_BASE = 512.0

        def _gammas(heads):
            return 1.0 - jnp.exp(jnp.linspace(math.log(1.0 / 32.0), math.log(1.0 / 512.0), heads))

        def _xpos(x, downscale):
            S, d = (x.shape[2], x.shape[3])
            half = d // 2
            base_scale = (jnp.arange(0, d, 2, dtype=jnp.float32) + 0.4 * d) / (1.4 * d)
            pos = jnp.arange(S, dtype=jnp.float32)
            scale = base_scale[None, :] ** (pos / SCALE_BASE)[:, None]
            if downscale:
                scale = 1.0 / scale
            inv_freq = 1.0 / 10000.0 ** (jnp.arange(half, dtype=jnp.float32) / half)
            sinusoid = pos[:, None] * inv_freq[None, :]
            sin = jnp.repeat(jnp.sin(sinusoid) * scale, 2, axis=-1)
            cos = jnp.repeat(jnp.cos(sinusoid) * scale, 2, axis=-1)
            x1 = x[..., ::2]
            x2 = x[..., 1::2]
            rot = jnp.stack([-x2, x1], axis=-1).reshape(x.shape)
            return x * cos + rot * sin

        def _decay_mask(S, gammas):
            n = jnp.arange(S)[:, None]
            m = jnp.arange(S)[None, :]
            diff = (n - m).astype(jnp.float32)
            mask = n >= m
            pw = jnp.maximum(diff, 0.0)[None, :, :]
            return jnp.where(mask[None, :, :], gammas[:, None, None] ** pw, 0.0)

        def retention_forward(Q, K, V):
            B, S, _ = Q.shape

            def split(x, hd):
                return x.reshape(B, S, HEADS, hd).transpose(0, 2, 1, 3)
            q = _xpos(split(Q, HEAD), downscale=False)
            k = _xpos(split(K, HEAD), downscale=True)
            v = split(V, HEAD)
            D = _decay_mask(S, _gammas(HEADS).astype(Q.dtype))
            scores = jnp.einsum('bhsd,bhtd->bhst', q, k) * D[None]
            out = jnp.einsum('bhst,bhtd->bhsd', scores, v)
            return out.transpose(0, 2, 1, 3).reshape(B, S, HEADS * HEAD)
        key = jax.random.key(seed)
        kq, kk, kv = jax.random.split(key, 3)
        B, S = (2, 512)
        return {'Q': jax.random.normal(kq, (B, S, HIDDEN), dtype=jnp.float32), 'K': jax.random.normal(kk, (B, S, HIDDEN), dtype=jnp.float32), 'V': jax.random.normal(kv, (B, S, HIDDEN), dtype=jnp.float32)}
    _L0_xattn_all = _L0_xattn_setup()
    _L0_xattn_in = {k: v for k, v in _L0_xattn_all.items() if k in ()}
    del _L0_xattn_all

    def _L0_ffn_setup():
        import jax, jax.numpy as jnp
        import numpy as np
        FEATURES = 256
        D_IN = 256

        def fp8_gemm_optimized(x, input_scale, kernel, kernel_scale):
            s_in = input_scale[0]
            s_k = kernel_scale[0]
            x_q = (x.astype(jnp.float32) / s_in).astype(jnp.float8_e4m3fn)
            k_q = (kernel.astype(jnp.float32) / s_k).astype(jnp.float8_e4m3fn)
            y = jnp.dot(x_q.astype(jnp.float32), k_q.astype(jnp.float32), preferred_element_type=jnp.float32)
            return y * (s_in * s_k)
        key = jax.random.key(seed)
        kx, kk, kb = jax.random.split(key, 3)
        x = jax.random.normal(kx, (4, 2048, D_IN), dtype=jnp.float32)
        limit = np.sqrt(6.0 / (D_IN + FEATURES)).astype(np.float32)
        kernel = jax.random.uniform(kk, (D_IN, FEATURES), dtype=jnp.float32, minval=-limit, maxval=limit).astype(jnp.bfloat16)
        input_scale = jnp.ones((1,), dtype=jnp.float32)
        kernel_scale = jnp.ones((1,), dtype=jnp.float32)
        bias = jnp.zeros((FEATURES,), dtype=jnp.bfloat16)
        return {'x': x, 'kernel': kernel, 'input_scale': input_scale, 'kernel_scale': kernel_scale, 'bias': bias}
    _L0_ffn_all = _L0_ffn_setup()
    _L0_ffn_in = {k: v for k, v in _L0_ffn_all.items() if k in ('kernel', 'input_scale', 'kernel_scale', 'bias')}
    del _L0_ffn_all

    def _L1_xattn_setup():
        import jax, jax.numpy as jnp
        import numpy as np
        DIM = 256
        NUM_HEADS = 16
        HEAD_DIM = DIM // NUM_HEADS
        SCALE = HEAD_DIM ** (-0.5)
        B, T1, T2 = (4, 512, 512)
        key = jax.random.key(seed)
        ks = jax.random.split(key, 6)
        s = 0.02
        return {'x': jax.random.normal(ks[0], (B, T1, DIM), dtype=jnp.float32), 'context': jax.random.normal(ks[1], (B, T2, DIM), dtype=jnp.float32), 'Wq': jax.random.normal(ks[2], (DIM, DIM), dtype=jnp.float32) * s, 'Wkv': jax.random.normal(ks[3], (2 * DIM, DIM), dtype=jnp.float32) * s, 'Wproj': jax.random.normal(ks[4], (DIM, DIM), dtype=jnp.float32) * s, 'bproj': jax.random.normal(ks[5], (DIM,), dtype=jnp.float32) * s}
    _L1_xattn_all = _L1_xattn_setup()
    _L1_xattn_in = {k: v for k, v in _L1_xattn_all.items() if k in ('Wq', 'Wkv', 'Wproj', 'bproj')}
    del _L1_xattn_all

    def _L1_ffn_setup():
        import jax, jax.numpy as jnp
        import numpy as np
        SWIGLU_ALPHA = 1.702
        SWIGLU_LIMIT = 7.0
        TOP_K = 4
        key = jax.random.key(seed)
        k = jax.random.split(key, 5)
        B, S, D, E, I = (2, 256, 256, 8, 512)
        return {'hidden_states': jax.random.normal(k[0], (B, S, D), dtype=jnp.float32), 'router_weight': jax.random.normal(k[1], (E, D), dtype=jnp.float32) * 0.02, 'router_bias': jnp.zeros((E,), dtype=jnp.float32), 'gate_up_proj': jax.random.normal(k[2], (E, 2 * I, D), dtype=jnp.float32) * 0.02, 'gate_up_proj_bias': jnp.zeros((E, 2 * I), dtype=jnp.float32), 'down_proj': jax.random.normal(k[3], (E, D, I), dtype=jnp.float32) * 0.02, 'down_proj_bias': jnp.zeros((E, D), dtype=jnp.float32)}
    _L1_ffn_all = _L1_ffn_setup()
    _L1_ffn_in = {k: v for k, v in _L1_ffn_all.items() if k in ('router_weight', 'router_bias', 'gate_up_proj', 'gate_up_proj_bias', 'down_proj', 'down_proj_bias')}
    del _L1_ffn_all
    return {'x': x, 'ctx_1024': ctx_1024, 'L0_ffn_kernel': _L0_ffn_in['kernel'], 'L0_ffn_input_scale': _L0_ffn_in['input_scale'], 'L0_ffn_kernel_scale': _L0_ffn_in['kernel_scale'], 'L0_ffn_bias': _L0_ffn_in['bias'], 'L1_xattn_Wq': _L1_xattn_in['Wq'], 'L1_xattn_Wkv': _L1_xattn_in['Wkv'], 'L1_xattn_Wproj': _L1_xattn_in['Wproj'], 'L1_xattn_bproj': _L1_xattn_in['bproj'], 'L1_ffn_router_weight': _L1_ffn_in['router_weight'], 'L1_ffn_router_bias': _L1_ffn_in['router_bias'], 'L1_ffn_gate_up_proj': _L1_ffn_in['gate_up_proj'], 'L1_ffn_gate_up_proj_bias': _L1_ffn_in['gate_up_proj_bias'], 'L1_ffn_down_proj': _L1_ffn_in['down_proj'], 'L1_ffn_down_proj_bias': _L1_ffn_in['down_proj_bias']}

def reference(x, ctx_1024, L0_ffn_kernel, L0_ffn_input_scale, L0_ffn_kernel_scale, L0_ffn_bias, L1_xattn_Wq, L1_xattn_Wkv, L1_xattn_Wproj, L1_xattn_bproj, L1_ffn_router_weight, L1_ffn_router_bias, L1_ffn_gate_up_proj, L1_ffn_gate_up_proj_bias, L1_ffn_down_proj, L1_ffn_down_proj_bias):
    import jax
    import jax.numpy as jnp

    def _L0_xattn_ref(Q, K, V):
        import jax, jax.numpy as jnp
        import numpy as np
        import math
        HIDDEN = 256
        HEADS = 16
        HEAD = HIDDEN // HEADS
        SCALE_BASE = 512.0

        def _gammas(heads):
            return 1.0 - jnp.exp(jnp.linspace(math.log(1.0 / 32.0), math.log(1.0 / 512.0), heads))

        def _xpos(x, downscale):
            S, d = (x.shape[2], x.shape[3])
            half = d // 2
            base_scale = (jnp.arange(0, d, 2, dtype=jnp.float32) + 0.4 * d) / (1.4 * d)
            pos = jnp.arange(S, dtype=jnp.float32)
            scale = base_scale[None, :] ** (pos / SCALE_BASE)[:, None]
            if downscale:
                scale = 1.0 / scale
            inv_freq = 1.0 / 10000.0 ** (jnp.arange(half, dtype=jnp.float32) / half)
            sinusoid = pos[:, None] * inv_freq[None, :]
            sin = jnp.repeat(jnp.sin(sinusoid) * scale, 2, axis=-1)
            cos = jnp.repeat(jnp.cos(sinusoid) * scale, 2, axis=-1)
            x1 = x[..., ::2]
            x2 = x[..., 1::2]
            rot = jnp.stack([-x2, x1], axis=-1).reshape(x.shape)
            return x * cos + rot * sin

        def _decay_mask(S, gammas):
            n = jnp.arange(S)[:, None]
            m = jnp.arange(S)[None, :]
            diff = (n - m).astype(jnp.float32)
            mask = n >= m
            pw = jnp.maximum(diff, 0.0)[None, :, :]
            return jnp.where(mask[None, :, :], gammas[:, None, None] ** pw, 0.0)

        def retention_forward(Q, K, V):
            B, S, _ = Q.shape

            def split(x, hd):
                return x.reshape(B, S, HEADS, hd).transpose(0, 2, 1, 3)
            q = _xpos(split(Q, HEAD), downscale=False)
            k = _xpos(split(K, HEAD), downscale=True)
            v = split(V, HEAD)
            D = _decay_mask(S, _gammas(HEADS).astype(Q.dtype))
            scores = jnp.einsum('bhsd,bhtd->bhst', q, k) * D[None]
            out = jnp.einsum('bhst,bhtd->bhsd', scores, v)
            return out.transpose(0, 2, 1, 3).reshape(B, S, HEADS * HEAD)
        return retention_forward(Q, K, V)

    def _L0_ffn_ref(x, kernel, input_scale, kernel_scale, bias):
        import jax, jax.numpy as jnp
        import numpy as np
        FEATURES = 256
        D_IN = 256

        def fp8_gemm_optimized(x, input_scale, kernel, kernel_scale):
            s_in = input_scale[0]
            s_k = kernel_scale[0]
            x_q = (x.astype(jnp.float32) / s_in).astype(jnp.float8_e4m3fn)
            k_q = (kernel.astype(jnp.float32) / s_k).astype(jnp.float8_e4m3fn)
            y = jnp.dot(x_q.astype(jnp.float32), k_q.astype(jnp.float32), preferred_element_type=jnp.float32)
            return y * (s_in * s_k)
        dtype = jnp.bfloat16
        x = x.astype(dtype)
        orig_shape = x.shape
        x2 = x.reshape(-1, x.shape[-1])
        y = fp8_gemm_optimized(x2, input_scale, kernel, kernel_scale)
        y = y.astype(dtype) + bias
        return y.reshape(orig_shape[:-1] + (FEATURES,))

    def _L1_xattn_ref(x, context, Wq, Wkv, Wproj, bproj):
        import jax, jax.numpy as jnp
        import numpy as np
        DIM = 256
        NUM_HEADS = 16
        HEAD_DIM = DIM // NUM_HEADS
        SCALE = HEAD_DIM ** (-0.5)
        B, T1, T2 = (4, 512, 512)
        Bx, T1x, C = x.shape
        T2x = context.shape[1]
        q = (x @ Wq.T).reshape(Bx, T1x, NUM_HEADS, HEAD_DIM).transpose(0, 2, 1, 3)
        kv = (context @ Wkv.T).reshape(Bx, T2x, 2, NUM_HEADS, HEAD_DIM)
        kv = kv.transpose(2, 0, 3, 1, 4)
        k, v = (kv[0], kv[1])
        attn = jnp.einsum('bhqd,bhkd->bhqk', q, k) * SCALE
        attn = jax.nn.softmax(attn, axis=-1)
        out = jnp.einsum('bhqk,bhkd->bhqd', attn, v)
        out = out.transpose(0, 2, 1, 3).reshape(Bx, T1x, C)
        return out @ Wproj.T + bproj

    def _L1_ffn_ref(hidden_states, router_weight, router_bias, gate_up_proj, gate_up_proj_bias, down_proj, down_proj_bias):
        import jax, jax.numpy as jnp
        import numpy as np
        SWIGLU_ALPHA = 1.702
        SWIGLU_LIMIT = 7.0
        TOP_K = 4
        B, S, D = hidden_states.shape
        E = router_weight.shape[0]
        x = hidden_states.reshape(-1, D)
        N = x.shape[0]
        logits = x @ router_weight.T + router_bias
        topk_logits, topk_idx = jax.lax.top_k(logits, TOP_K)
        topk_w = jax.nn.softmax(topk_logits.astype(jnp.float32), axis=-1)
        combine = jnp.zeros((N, E), dtype=jnp.float32)
        combine = combine.at[jnp.arange(N)[:, None], topk_idx].set(topk_w)
        gate_up = jnp.einsum('nd,ejd->nej', x, gate_up_proj) + gate_up_proj_bias
        gate, up = jnp.split(gate_up, 2, axis=-1)
        gate = jnp.minimum(gate, SWIGLU_LIMIT)
        up = jnp.clip(up, -SWIGLU_LIMIT, SWIGLU_LIMIT)
        act = (up + 1.0) * gate * jax.nn.sigmoid(SWIGLU_ALPHA * gate)
        out = jnp.einsum('nei,edi->ned', act, down_proj) + down_proj_bias
        y = jnp.einsum('ned,ne->nd', out, combine.astype(out.dtype))
        return y.reshape(B, S, D)
    x = x + _L0_xattn_ref(_layernorm(x, axis=-1), ctx_1024, ctx_1024)
    x = x + _L0_ffn_ref(_layernorm(x, axis=-1), L0_ffn_kernel, L0_ffn_input_scale, L0_ffn_kernel_scale, L0_ffn_bias)
    x = x + _L1_xattn_ref(_layernorm(x, axis=-1), ctx_1024, L1_xattn_Wq, L1_xattn_Wkv, L1_xattn_Wproj, L1_xattn_bproj)
    x = x + _L1_ffn_ref(_layernorm(x, axis=-1), L1_ffn_router_weight, L1_ffn_router_bias, L1_ffn_gate_up_proj, L1_ffn_gate_up_proj_bias, L1_ffn_down_proj, L1_ffn_down_proj_bias)
    return x

_drawn_inputs = setup_inputs


def setup_inputs(seed=0):
    import zlib

    import numpy as np

    out = dict(_drawn_inputs(seed))
    spreads = {'L0_ffn_bias': (0.0, 2.0),
     'L1_ffn_router_bias': (0.0, 2.0),
     'L1_ffn_gate_up_proj_bias': (0.0, 0.8),
     'L1_ffn_down_proj_bias': (0.0, 2.0)}
    factors = {'L0_ffn_kernel': 7.44,
     'L1_xattn_Wq': 8.0,
     'L1_xattn_Wkv': 8.0,
     'L1_xattn_Wproj': 8.0,
     'L1_xattn_bproj': 200.0,
     'L1_ffn_router_weight': 8.0,
     'L1_ffn_gate_up_proj': 8.0,
     'L1_ffn_down_proj': 8.0}
    for name, (base, spread) in spreads.items():
        noise = np.random.default_rng([zlib.crc32(name.encode()), seed]).standard_normal(out[name].shape)
        drawn = base * np.exp(spread * noise) if base else spread * noise
        out[name] = jnp.asarray(drawn.astype(out[name].dtype))
    for name, factor in factors.items():
        out[name] = (out[name] * factor).astype(out[name].dtype)
    return out
```

```python
from contextlib import ExitStack

import concourse.bass as bass
import numpy as np
from concourse import mybir

F32, F16, BF16, I32 = mybir.dt.float32, mybir.dt.float16, mybir.dt.bfloat16, mybir.dt.int32
ALU, ACT, AX = mybir.AluOpType, mybir.ActivationFunctionType, mybir.AxisListType

P = 128
B, S, D = 4, 512, 256
H, HD = 16, 16
T = S // P
KD = D // P
NT = B * T
E, I = 8, 512
IT = I // P
PAIRS = H // 2
HP = PAIRS // 2
HH = H // 2
SR = 3 * HD
KR = 2 * SR
MR = KR + 4
WS = 16.0
LIMIT, EPS = 7.0, 1e-5
QSCALE = float(HD) ** -0.5
TOPK = 4


def need(eng, sem, value):
    if not (isinstance(value, int) and value <= 0):
        eng.wait_ge(sem, value)


def tables():
    pos = np.arange(S, dtype=np.float64)
    base = (np.arange(0, HD, 2) + 0.4 * HD) / (1.4 * HD)
    scale = base[None, :] ** (pos / 512.0)[:, None]
    angle = pos[:, None] / 10000.0 ** (np.arange(HD // 2) / (HD // 2))[None, :]
    gamma = (1.0 - np.exp(np.linspace(np.log(1 / 32), np.log(1 / 512), H))).astype(np.float32).astype(np.float64)
    sign = np.array([-1.0, 1.0])
    within = pos % P
    out = {}
    for name, s, decay in (("q", scale, gamma[None, :] ** within[:, None]),
                           ("k", 1.0 / scale, gamma[None, :] ** -within[:, None])):
        cos = np.repeat(np.cos(angle) * s, 2, axis=-1)
        sin = np.repeat(np.sin(angle) * s, 2, axis=-1) * np.tile(sign, HD // 2)
        for part, t in (("cos", cos), ("sin", sin)):
            full = (decay[:, :, None] * t[:, None, :]).reshape(S, D)
            out[f"{name}_{part}"] = np.ascontiguousarray(full.reshape(T, P, D).transpose(1, 0, 2), np.float32)
    head = np.arange(D) // HD
    block = np.zeros((P, 2, P), np.float32)
    for half in range(2):
        hs = head[half * P:(half + 1) * P]
        block[:, half] = (hs[:, None] == hs[None, :]) * (gamma[hs] ** P)[:, None]
    out["chunk_decay"] = block
    out["causal"] = (np.arange(P)[None, :] >= np.arange(P)[:, None]).astype(np.float32)
    out["ident"] = np.eye(P, dtype=np.float32)
    ones = np.zeros((4, 2, 2 * HP * S), np.float32)
    ones[0:2, 0], ones[2:4, 1] = 1.0, 1.0
    out["max_rows"] = ones.astype(np.float16)
    out["before"] = np.tile((np.arange(E)[None, :] < np.arange(E)[:, None]).astype(np.float32)[None], (P, 1, 1))
    return out


def xattn_ffn_moe_kernel(nc, t, out):
    dram = lambda name, shape, dt: nc.dram_tensor(name, shape, dt, kind="Internal").ap()
    stack0_d = dram("stack0_d", (2, 2, D, S), F16)
    stack1_d = dram("stack1_d", (2, 2, D, S), F16)
    max_d = dram("max_d", (2, 4 * HP, S), F16)
    x_d = dram("x_d", (NT, P, D), F32)
    xt_d = dram("xt_d", (2, B, P, KD, S), F16)

    with ExitStack() as both:
        raw = both.enter_context(nc.sbuf_tensor("raw", [P, KD * 2 * I + IT * D], F32))
        raw_b = both.enter_context(nc.sbuf_tensor("raw_b", [P, 2, 8], F32))
        w_loaded = both.enter_context(nc.semaphore("w_loaded"))
        phase_a(nc, t, stack0_d, stack1_d, max_d, x_d, xt_d)
        phase_m(nc, t, out, x_d, xt_d, raw, raw_b, w_loaded)


def phase_a(nc, t, stack0_d, stack1_d, max_d, x_d, xt_d):
    with ExitStack() as ctx:
        def sb(name, shape, dt=F32):
            return ctx.enter_context(nc.sbuf_tensor(name, shape, dt))

        def sem(name):
            return ctx.enter_context(nc.semaphore(name))

        q_cos, q_sin = sb("q_cos", [P, T, D]), sb("q_sin", [P, T, D])
        k_cos, k_sin = sb("k_cos", [P, T, D]), sb("k_sin", [P, T, D])
        chunk_decay = sb("chunk_decay", [P, 2, P])
        causal, ident = sb("causal", [P, P]), sb("ident", [P, P])
        ident16, ident_bf = sb("ident16", [P, P], F16), sb("ident_bf", [P, P], BF16)
        half_power = sb("half_power", [P, T])
        wq = [sb(f"wq{i}", [P, KD, D], F16) for i in range(2)]
        wkv = [sb(f"wkv{i}", [P, KD, 2 * D], F16) for i in range(2)]
        wp = [sb(f"wp{i}", [P, KD, D], F16) for i in range(2)]
        w8_raw, w8 = sb("w8_raw", [P, KD, D], BF16), sb("w8", [P, KD, D], BF16)
        bias0, biasp = sb("bias0", [P, D], BF16), sb("biasp", [P, D])
        s_in, s_k = sb("s_in", [P, 1]), sb("s_k", [P, 1])
        r_in, r_k, s_both = sb("r_in", [P, 1]), sb("r_k", [P, 1]), sb("s_both", [P, 1])
        ctx_n, ctx_s, ctx_t = sb("ctx_n", [P, T, D]), sb("ctx_s", [P, T, D]), sb("ctx_t", [P, KD, S])
        x_p, x_n = sb("x_p", [P, T, D]), sb("x_n", [P, T, D])
        bn6, mv, ve, rstd = sb("bn6", [P, T, 6]), sb("mv", [P, 4, T]), sb("ve", [P, T]), sb("rstd", [P, T])
        q_r, q_s, k_r = sb("q_r", [P, T, D]), sb("q_s", [P, T, D]), sb("k_r", [P, T, D])
        t0 = [[sb(f"t0_{w}{i}", [P, 2, S], F16) for i in range(2)] for w in "qk"]
        v0 = [sb(f"v0_{i}", [P, T, D], F16) for i in range(2)]
        state = sb("state", [P, T - 1, P])
        state_s = [sb(f"state_s{i}", [P, T - 1, P], F16) for i in range(2)]
        sq0 = sb("sq0", [P, HP, S], F16)
        kz0 = [sb(f"kz0_{i}", [P, HP, S], F16) for i in range(2)]
        rm = sb("rm", [P, 2, 4, P])
        rs = [sb(f"rs{i}", [P, 2, HH, P], F16) for i in range(2)]
        x_b, x_q, xq_t = sb("x_b", [P, T, D], BF16), sb("x_q", [P, T, D], BF16), sb("xq_t", [P, KD, S], BF16)
        y_a, y_b = sb("y_a", [P, 2, D], BF16), sb("y_b", [P, 2, D], BF16)
        x3 = [sb(f"x3_{i}", [P, KD, S], F16) for i in range(2)]
        c3 = [sb(f"c3_{i}", [P, KD, S], F16) for i in range(2)]
        t1 = [sb(f"t1_{i}", [P, 2, S], F16) for i in range(2)]
        v_next = [sb(f"v_next{i}", [P, T, H, HD + 1], F16) for i in range(2)]
        v_cur = [sb(f"v_cur{i}", [P, T, H, HD + 1], F16) for i in range(2)]
        sq1 = sb("sq1", [P, 2, HP, S], F16)
        kz1 = [sb(f"kz1_{i}", [P, 2, HP, S], F16) for i in range(2)]
        neg_max = sb("neg_max", [P, T, 2, HP])
        max16 = sb("max16", [P, T, 2, 2, HP], F16)
        max_t = sb("max_t", [4 * HP, S], F16)
        p32 = sb("p32", [P, 2, 2, S])
        ph, pl = sb("ph", [P, 2, T, S], F16), sb("pl", [P, 2, T, S], F16)
        rden, o_n = sb("rden", [P, 4, T]), sb("o_n", [P, T, D])
        o_t = [sb(f"o_t{i}", [P, KD, S], F16) for i in range(2)]
        x_a = sb("x_a", [P, T, D])
        bn6_a, mv_a, ve_a, rstd_a = sb("bn6_a", [P, T, 6]), sb("mv_a", [P, 4, T]), sb("ve_a", [P, T]), sb("rstd_a", [P, T])

        misc = ctx.enter_context(nc.psum_tensor("misc", [P, 2, 512], F32))
        sc = ctx.enter_context(nc.psum_tensor("sc", [P, 2, 512], F32))
        st = ctx.enter_context(nc.psum_tensor("st", [P, 2, 512], F32))
        pv = ctx.enter_context(nc.psum_tensor("pv", [P, 2, 512], F32))

        wq_raw = q_r[:].rearrange("p t d -> p (t d)")[:, 0:KD * D].rearrange("p (k d) -> p k d", k=KD)
        wp_raw = q_r[:].rearrange("p t d -> p (t d)")[:, KD * D:2 * KD * D].rearrange("p (k d) -> p k d", k=KD)
        wkv_raw = k_r[:].rearrange("p t d -> p (t d)").rearrange("p (k d) -> p k d", k=KD)
        qa, qb = q_r, q_s
        w8a = ctx_s[:].rearrange("p t d -> p (t d)")[:, 0:KD * D]
        w8b = ctx_s[:].rearrange("p t d -> p (t d)")[:, KD * D:2 * KD * D]

        const_in = sem("const_in")
        const_ok = sem("const_ok")
        w8_step = sem("w8_step")
        w16_hi = sem("w16_hi")
        w16_lo = sem("w16_lo")
        zeros_ok = sem("zeros_ok")
        x_in, ctx_in = sem("x_in"), sem("ctx_in")
        ln_bn, ln_mv, ln_ve, ln_rs, ln_out = (sem(f"ln_{n}") for n in ("bn", "mv", "ve", "rs", "out"))
        rot_q = sem("rot_q")
        rot_k = sem("rot_k")
        v0_hi, v0_lo = sem("v0_hi"), sem("v0_lo")
        tr0, t0_hi, t0_lo = sem("tr0"), sem("t0_hi"), sem("t0_lo")
        st0_out, st0_in = sem("st0_out"), sem("st0_in")
        upd = sem("upd")
        state_ok = sem("state_ok")
        state_hi, state_lo = sem("state_hi"), sem("state_lo")
        r_sc, r_mask, r_hi, r_lo = (sem(f"r_{n}") for n in ("sc", "mask", "hi", "lo"))
        r_out, r_add = sem("r_out"), sem("r_add")
        quant = sem("quant")
        xq_tr, xq_cp = sem("xq_tr"), sem("xq_cp")
        ffn_mm, ffn_y, ffn_b, ffn_x = (sem(f"ffn_{n}") for n in ("mm", "y", "b", "x"))
        tr3, t3_hi, t3_lo = sem("tr3"), sem("t3_hi"), sem("t3_lo")
        c3_hi, c3_lo = sem("c3_hi"), sem("c3_lo")
        qk_mm, qk_hi, qk_lo = sem("qk_mm"), sem("qk_hi"), sem("qk_lo")
        v_mm, v_hi, v_lo = sem("v_mm"), sem("v_hi"), sem("v_lo")
        st1_out = [sem(f"st1_out{i}") for i in range(2)]
        rows_in = sem("rows_in")
        st1_in = [sem(f"st1_in{i}") for i in range(2)]
        m_sc, m_max = sem("m_sc"), sem("m_max")
        m_16 = sem("m_16")
        m_tr, m_cp = sem("m_tr"), sem("m_cp")
        m_out = sem("m_out")
        m_in = [sem(f"m_in{i}") for i in range(2)]
        v_cp = sem("v_cp")
        x_cp = sem("x_cp")
        s_mm, s_exp = sem("s_mm"), sem("s_exp")
        p_hi, p_lo = sem("p_hi"), sem("p_lo")
        pv_mm = sem("pv_mm")
        o_rec, o_mul = sem("o_rec"), sem("o_mul")
        o_tr, o_hi, o_lo = sem("o_tr"), sem("o_hi"), sem("o_lo")
        x_bias = sem("x_bias")
        pr_mm, pr_x = sem("pr_mm"), sem("pr_x")
        la_bn, la_mv, la_ve, la_rs, la_out = (sem(f"la_{n}") for n in ("bn", "mv", "ve", "rs", "out"))
        tr4, t4_hi, t4_lo = sem("tr4"), sem("t4_hi"), sem("t4_lo")
        x_out = sem("x_out")

        flat = lambda ap: ap.rearrange("p t d -> p (t d)")
        LAST = B - 1

        def prep_steps(b):
            yield "layernorm", b, 0
            yield "rotate", b, 0
            for half in range(2):
                yield "turn0", b, half
                yield "state", b, half
                for c in range(T):
                    yield "retain", b, (half, c)
            yield "layernorm", b, 1
            yield "quantise", b, 0
            yield "linear", b, 0
            yield "layernorm", b, 2
            yield "project", b, 0

        def batch_steps(b, more):
            prep = list(prep_steps(b + 1)) if more else []
            first, second = prep[:14], prep[14:]
            maxima = [("maxima", b, (1, h)) for h in range(HH)] + [("max_rows", b, 1)]
            after = [("maxima", b + 1, (0, h)) for h in range(HH)] + [("max_rows", b + 1, 0)] if more else []
            before8, before16 = first + maxima, second + after
            yield "hand_over", b, more
            for h in range(H):
                yield "score", b, h
                fill, slot = (before8, h) if h < HH else (before16, h - HH)
                n = len(fill)
                if h < HH - 1:
                    yield from fill[slot * n // (HH - 1):(slot + 1) * n // (HH - 1)]
                elif h >= HH:
                    yield from fill[slot * n // HH:(slot + 1) * n // HH]
                if h:
                    yield "values", b, h - 1
            yield "values", b, H - 1
            yield "out_project", b, 0

        def run(steps, engine, loop=True):
            def emit(order):
                for name, b, arg in order:
                    if name in steps:
                        steps[name](b, arg)
            emit(list(prep_steps(0)) + [("maxima", 0, (0, h)) for h in range(HH)] + [("max_rows", 0, 0)])
            emit(batch_steps(0, True))
            if loop:
                with engine.Fori(1, LAST) as i:
                    emit(batch_steps(i, True))
            else:
                for i in range(1, LAST):
                    emit(batch_steps(i, True))
            emit(batch_steps(LAST, False))

        block = ctx.enter_context(nc.Block())

        @block.sync
        def _(sp):
            n_const = [0]

            def const(dst, src):
                sp.dma_start(dst, src).then_inc(const_in, 16)
                n_const[0] += 1

            def load_x(b):
                sp.dma_start(x_p[:], t["x"].rearrange("(b t p) d -> b p t d", b=B, t=T)[bass.ds(b, 1)]
                             .rearrange("a p t d -> (a p) t d")).then_inc(x_in, 16)

            def load_ctx(b):
                for dst, name in ((ctx_n, "ctx"), (ctx_s, "ctx_swapped")):
                    sp.dma_start(dst[:], t[name].rearrange("(b t p) d -> b p t d", b=B, t=T)[bass.ds(b, 1)]
                                 .rearrange("a p t d -> (a p) t d")).then_inc(ctx_in, 16)
                sp.dma_start(ctx_t[:], t["ctx_t"].rearrange("(k p) (b n) -> b p k n", k=KD, b=B)[bass.ds(b, 1)]
                             .rearrange("a p k n -> (a p) k n")).then_inc(ctx_in, 16)

            load_x(0)
            const(ident[:], t["ident"])
            const(w8_raw[:], t["L0_ffn_kernel"].rearrange("(k p) d -> p k d", k=KD))
            const(s_in[:], t["L0_ffn_input_scale"][None, :].to_broadcast([P, 1]))
            const(s_k[:], t["L0_ffn_kernel_scale"][None, :].to_broadcast([P, 1]))
            const(wq_raw, t["wq_t"].rearrange("(k p) d -> p k d", k=KD))
            const(wp_raw, t["wp_t"].rearrange("(k p) d -> p k d", k=KD))
            const(wkv_raw, t["wkv_t"].rearrange("(k p) d -> p k d", k=KD))
            const(q_cos[:], t["q_cos"])
            const(q_sin[:], t["q_sin"])
            const(k_cos[:], t["k_cos"])
            const(k_sin[:], t["k_sin"])
            const(causal[:], t["causal"])
            const(chunk_decay[:], t["chunk_decay"])
            const(bias0[:], t["L0_ffn_bias"][None, :].to_broadcast([P, D]))
            const(biasp[:], t["L1_xattn_bproj"][None, :].to_broadcast([P, D]))
            assert n_const[0] == N_CONST
            sp.wait_ge(zeros_ok, 4)
            for i in range(2):
                sp.dma_start(kz1[i][KR:MR].rearrange("p a b n -> p (a b n)"), t["max_rows"][:, i]).then_inc(rows_in, 16)
            sp.wait_ge(w8_step, W8_STEPS)
            load_ctx(0)

            def to_stack():
                return [(w, par, j, (0, 0, 1)[j] if w == 0 else (0, 1, 0)[j])
                        for w in range(2) for par in range(2) for j in range(3)]

            def part(stack, w, hl, half, par):
                return stack[w, hl].rearrange("(f q r d) n -> f r d q n", f=2, q=HP, r=2)[half, par]

            def turn0(b, half):
                if half == 0:
                    need(sp, st0_in, b * 2 * 12 * 16)
                for w in range(2):
                    sp.wait_ge(t0_lo, b * 4 + 2 * half + w + 1)
                    for hl in range(2):
                        sp.dma_start(stack0_d[w, hl].rearrange("(f p) n -> f p n", f=2)[half],
                                     t0[w][hl][:, half, :]).then_inc(st0_out, 16)
                sp.wait_ge(st0_out, (b * 2 + half + 1) * 4 * 16)
                if half == 0:
                    sp.wait_ge(zeros_ok, 4)
                need(sp, r_sc, b * 16 + half * 8)
                for w, par, j, hl in to_stack():
                    row = par * SR + j * HD
                    dst = (sq0 if w == 0 else kz0[par])[row:row + HD]
                    sp.dma_start(dst, part(stack0_d, w, hl, half, par)).then_inc(st0_in, 16)

            def project(b, _):
                for half in range(2):
                    need(sp, st1_in[half], b * 12 * 16)
                for n in range(4):
                    w, half = n // 2, n % 2
                    sp.wait_ge(qk_lo, b * 4 + n + 1)
                    for hl in range(2):
                        sp.dma_start(stack1_d[w, hl].rearrange("(f p) n -> f p n", f=2)[half],
                                     t1[hl][:, half, :]).then_inc(st1_out[half], 16)
                for half in range(2):
                    sp.wait_ge(st1_out[half], (b + 1) * 4 * 16)
                need(sp, s_mm, b * 64 - 32)
                stack1(0)

            def stack1(half):
                for w, par, j, hl in to_stack():
                    row = par * SR + j * HD
                    dst = (sq1 if w == 0 else kz1[par])[row:row + HD, half]
                    sp.dma_start(dst, part(stack1_d, w, hl, half, par)).then_inc(st1_in[half], 16)

            def max_rows(b, half):
                sp.wait_ge(m_cp, b * 2 + half + 1)
                need(sp, m_in[half], b * 16)
                sp.dma_start(max_d[half], max_t[:]).then_inc(m_out, 16)
                sp.wait_ge(m_out, (b * 2 + half + 1) * 16)
                need(sp, s_mm, b * 64 - 32 + half * 32)
                sp.dma_start(sq1[KR:MR, half], max_d[half].rearrange("(r q) n -> r q n", r=4)).then_inc(m_in[half], 16)

            def hand_over(b, more):
                need(sp, s_mm, b * 64)
                stack1(1)
                if more:
                    sp.wait_ge(x_cp, b + 1)
                    load_x(b + 1)
                    sp.wait_ge(v0_lo, b + 1)
                    sp.wait_ge(rot_k, (b + 1) * 2)
                    sp.wait_ge(c3_lo, b + 1)
                    sp.wait_ge(upd, (b + 1) * 2)
                    load_ctx(b + 1)

            def out_project(b, _):
                sp.wait_ge(pr_x, (b + 1) * 2)
                sp.dma_start(x_d.rearrange("(b t) p d -> b p t d", b=B)[bass.ds(b, 1)]
                             .rearrange("a p t d -> (a p) t d"), x_a[:]).then_inc(x_out, 16)
                sp.wait_ge(t4_lo, (b + 1) * 2)
                for hl in range(2):
                    sp.dma_start(xt_d[hl][bass.ds(b, 1)].rearrange("a p k n -> (a p) k n"),
                                 o_t[hl][:]).then_inc(x_out, 16)

            run({"turn0": turn0, "project": project, "max_rows": max_rows, "hand_over": hand_over,
                 "out_project": out_project}, sp, loop=False)
            sp.wait_ge(x_out, B * 3 * 16)

        @block.gpsimd
        def _(pool):
            pool.memset(half_power[:], -0.5).then_inc(const_ok, 1)
            for buf in (kz0[0], kz0[1], kz1[0], kz1[1]):
                pool.memset(buf[:], 0.0).then_inc(zeros_ok, 1)
            pool.wait_ge(const_in, N_CONST * 16)
            pool.wait_ge(const_ok, CONSTS)

            def root(ve_t, rs_t, s_ve, s_rs, n):
                pool.wait_ge(s_ve, n)
                pool.tensor_tensor(rs_t[:], ve_t[:], half_power[:], ALU.pow).then_inc(s_rs, 1)

            def layernorm(b, j):
                root(ve, rstd, ln_ve, ln_rs, b * 3 + j + 1)
                if j == 0:
                    pool.wait_ge(ctx_in, (b + 1) * 48)
                    need(pool, tr0, b * 4)
                    need(pool, upd, b * 2)
                    pool.tensor_tensor(k_r[:], ctx_n[:], k_cos[:], ALU.mult)
                    pool.tensor_tensor(ctx_s[:], ctx_s[:], k_sin[:], ALU.mult).then_inc(rot_k, 1)
                    pool.wait_ge(rot_k, b * 2 + 1)
                    pool.tensor_tensor(k_r[:], k_r[:], ctx_s[:], ALU.add).then_inc(rot_k, 1)
                    pool.wait_ge(v0_hi, b + 1)
                    pool.tensor_tensor(v0[1][:], ctx_n[:], v0[0][:], ALU.subtract).then_inc(v0_lo, 1)
                if j == 1:
                    pool.wait_ge(c3_hi, b + 1)
                    pool.tensor_tensor(c3[1][:], ctx_t[:], c3[0][:], ALU.subtract).then_inc(c3_lo, 1)

            def retain(b, arg):
                half, c = arg
                for g in range(2):
                    n = half * 8 + c * 2 + g
                    pool.wait_ge(r_hi, b * 16 + n + 1)
                    pool.tensor_tensor(rs[1][:, c % 2, 4 * g:4 * g + 4, :], rm[:, n % 2],
                                       rs[0][:, c % 2, 4 * g:4 * g + 4, :], ALU.subtract).then_inc(r_lo, 1)

            def score(b, h):
                for g in range(2):
                    n = 2 * h + g
                    pool.wait_ge(p_hi, b * 32 + n + 1)
                    pool.tensor_tensor(pl[:, h % 2, 2 * g:2 * g + 2, :], p32[:, g], ph[:, h % 2, 2 * g:2 * g + 2, :],
                                       ALU.subtract).then_inc(p_lo, 1)

            def out_project(b, _):
                root(ve_a, rstd_a, la_ve, la_rs, b + 1)

            run({"layernorm": layernorm, "retain": retain, "score": score, "out_project": out_project}, pool)

        @block.scalar
        def _(act):
            act.wait_ge(const_in, N_CONST * 16)
            for hl, w_raw in ((wq, wq_raw), (wkv, wkv_raw), (wp, wp_raw)):
                act.activation(hl[0][:], w_raw, ACT.Copy, scale=WS).then_inc(w16_hi, 1)

            def layernorm(b, j):
                if j == 0:
                    act.wait_ge(ctx_in, (b + 1) * 48)
                    need(act, r_out, b * 8)
                    act.activation(v0[0][:], ctx_n[:], ACT.Copy).then_inc(v0_hi, 1)
                    need(act, v_mm, b * 2)
                    act.activation(c3[0][:], ctx_t[:], ACT.Copy).then_inc(c3_hi, 1)

            def turn0(b, half):
                for w in range(2):
                    n = 2 * half + w
                    need(act, st0_out, b * 8 * 16)
                    if w == 0:
                        need(act, r_out, b * 8)
                    act.wait_ge(tr0, b * 4 + n + 1)
                    act.activation(t0[w][0][:, half, :], misc[:, MISC_TURN0[n] % 2, :], ACT.Copy).then_inc(t0_hi, 1)

            def state_(b, half):
                act.wait_ge(state_ok, (b * 2 + half + 1) * 5)
                need(act, r_out, b * 8 + half * 4)
                act.activation(state_s[0][:], state[:], ACT.Copy).then_inc(state_hi, 1)

            def retain(b, arg):
                half, c = arg
                for g in range(2):
                    n = half * 8 + c * 2 + g
                    act.wait_ge(r_mask, b * 16 + n + 1)
                    need(act, r_out, b * 8 + half * 4 + c - 1)
                    act.activation(rs[0][:, c % 2, 4 * g:4 * g + 4, :], rm[:, n % 2], ACT.Copy).then_inc(r_hi, 1)

            def project(b, _):
                for k in range(KD):
                    act.wait_ge(tr3, b * 2 + k + 1)
                    need(act, qk_mm, b * 4)
                    act.activation(x3[0][:, k, :], misc[:, (MISC_X3 + k) % 2, :], ACT.Copy).then_inc(t3_hi, 1)
                for n in range(4):
                    act.wait_ge(qk_mm, b * 4 + n + 1)
                    need(act, st1_out[n % 2], (b * 4 + 2 * (n // 2)) * 16)
                    act.activation(t1[0][:, n % 2, :], misc[:, (MISC_QK + n) % 2, :], ACT.Copy,
                                   scale=1 / WS).then_inc(qk_hi, 1)
                for u in range(2):
                    act.wait_ge(v_mm, b * 2 + u + 1)
                    need(act, v_cp, b * 2)
                    act.activation(v_next[0][:, 2 * u:2 * u + 2, :, 0:HD],
                                   misc[:, (MISC_V + u) % 2, :].rearrange("p (t h d) -> p t h d", t=2, h=H),
                                   ACT.Copy, scale=1 / WS).then_inc(v_hi, 1)

            def score(b, h):
                for kt in range(T):
                    g = kt // 2
                    act.wait_ge(s_mm, b * 64 + h * 4 + kt + 1)
                    if kt % 2 == 0:
                        need(act, p_lo, b * 32 + 2 * h + g - 1)
                    act.activation(p32[:, g, kt % 2, :], st[:, kt % 2, :], ACT.Exp, scale=QSCALE).then_inc(s_exp, 1)

            def out_project(b, _):
                for k in range(KD):
                    act.wait_ge(o_tr, b * 2 + k + 1)
                    need(act, x_out, b * 3 * 16)
                    act.activation(o_t[0][:, k, :], pv[:, (4 + k) % 2, :], ACT.Copy).then_inc(o_hi, 1)
                for k in range(KD):
                    act.wait_ge(tr4, b * 2 + k + 1)
                    act.wait_ge(pr_mm, (b + 1) * 2)
                    act.activation(o_t[0][:, k, :], pv[:, (8 + k) % 2, :], ACT.Copy).then_inc(t4_hi, 1)

            run({"layernorm": layernorm, "turn0": turn0, "state": state_, "retain": retain, "project": project,
                 "score": score, "out_project": out_project}, act)

        @block.vector
        def _(dve):
            def steps(sem_):
                count = [0]

                def done(ins):
                    count[0] += 1
                    ins.then_inc(sem_, 1)
                    dve.wait_ge(sem_, count[0])
                return done, count

            def to_e4m3(v, m, dst, done):
                done(dve.tensor_scalar(m.bitcast(I32), v.bitcast(I32), 0x7F800000, None, ALU.bitwise_and))
                done(dve.tensor_scalar(m, m, 2.0 ** -6, 1.5 * 2.0 ** 20, ALU.max, ALU.mult))
                done(dve.tensor_tensor(v, v, m, ALU.add))
                done(dve.tensor_tensor(v, v, m, ALU.subtract))
                done(dve.tensor_scalar(m, v, 1.1 * 2.0 ** 119, 0.0, ALU.mult, ALU.mult))
                return dve.tensor_tensor(dst, v, m, ALU.add)

            dve.wait_ge(const_in, N_CONST * 16)
            dve.tensor_copy(ident16[:], ident[:]).then_inc(const_ok, 1)
            dve.tensor_copy(ident_bf[:], ident[:]).then_inc(const_ok, 1)
            dve.memset(v_next[0][:, :, :, HD:HD + 1], 1.0).then_inc(const_ok, 1)
            dve.memset(v_next[1][:, :, :, HD:HD + 1], 0.0).then_inc(const_ok, 1)
            done, count = steps(w8_step)
            dve.reciprocal(r_in[:], s_in[:])
            dve.tensor_tensor(s_both[:], s_in[:], s_k[:], ALU.mult)
            done(dve.reciprocal(r_k[:], s_k[:]))
            done(dve.tensor_scalar(w8a, w8_raw[:].rearrange("p k d -> p (k d)"), r_k[:, 0:1], None, ALU.mult))
            done(to_e4m3(w8a, w8b, w8[:].rearrange("p k d -> p (k d)"), done))
            assert count[0] == W8_STEPS
            for n, (hl, w_raw) in enumerate(((wq, wq_raw), (wkv, wkv_raw), (wp, wp_raw))):
                dve.wait_ge(w16_hi, n + 1)
                dve.scalar_tensor_tensor(hl[1][:], w_raw, WS, hl[0][:], ALU.mult, ALU.subtract).then_inc(w16_lo, 1)
            dve.wait_ge(w16_lo, 3)

            def normalise(x, dst, bn6_, mv_, ve_, rs_, s_bn, s_mv, s_ve, s_rs, s_out, n):
                for i in range(T):
                    ins = dve.bn_stats(bn6_[:, i, :], x[:, i, :])
                ins.then_inc(s_bn, 1)
                dve.wait_ge(s_bn, n)
                mean, diff, dev, sq = (mv_[:, i, :] for i in range(4))
                k = (n - 1) * 3
                dve.tensor_tensor(mean, bn6_[:, :, 1], bn6_[:, :, 4], ALU.add)
                dve.tensor_tensor(diff, bn6_[:, :, 1], bn6_[:, :, 4], ALU.subtract)
                dve.tensor_tensor(dev, bn6_[:, :, 2], bn6_[:, :, 5], ALU.add).then_inc(s_mv, 1)
                dve.wait_ge(s_mv, k + 1)
                dve.tensor_tensor(sq, diff, diff, ALU.mult)
                dve.tensor_scalar(mean, mean, 0.5, None, ALU.mult).then_inc(s_mv, 1)
                dve.wait_ge(s_mv, k + 2)
                dve.scalar_tensor_tensor(dev, sq, D / 4.0, dev, ALU.mult, ALU.add).then_inc(s_mv, 1)
                dve.wait_ge(s_mv, k + 3)
                dve.tensor_scalar(ve_[:], dev, 1.0 / D, EPS, ALU.mult, ALU.add).then_inc(s_ve, 1)
                dve.wait_ge(s_rs, n)
                for i in range(T):
                    ins = dve.tensor_scalar(dst[:, i, :], x[:, i, :], mean[:, i:i + 1], rs_[:, i:i + 1],
                                            ALU.subtract, ALU.mult)
                ins.then_inc(s_out, 1)

            def layernorm(b, j):
                if j == 0:
                    dve.wait_ge(x_in, (b + 1) * 16)
                    need(dve, tr3, b * 2)
                if j == 1:
                    dve.wait_ge(r_add, (b + 1) * 8)
                if j == 2:
                    dve.wait_ge(ffn_x, (b + 1) * 2)
                normalise(x_p, x_b if j == 1 else x_n, bn6, mv, ve, rstd, ln_bn, ln_mv, ln_ve,
                          ln_rs, ln_out, b * 3 + j + 1)

            def rotate(b, _):
                dve.wait_ge(ln_out, b * 3 + 1)
                need(dve, tr0, b * 4)
                need(dve, quant, b * QUANT_STEPS)
                two = lambda a: a[:].rearrange("p t (i two) -> p (t i) two", two=2)
                dve.tensor_tensor(q_r[:], x_n[:], q_cos[:], ALU.mult)
                for i in range(2):
                    ins = dve.tensor_tensor(two(q_s)[:, :, i], two(x_n)[:, :, 1 - i], two(q_sin)[:, :, i], ALU.mult)
                ins.then_inc(rot_q, 1)
                dve.wait_ge(rot_q, b * 2 + 1)
                dve.tensor_tensor(q_r[:], q_r[:], q_s[:], ALU.add).then_inc(rot_q, 1)

            def turn0(b, half):
                for w in range(2):
                    n = 2 * half + w
                    dve.wait_ge(t0_hi, b * 4 + n + 1)
                    dve.tensor_tensor(t0[w][1][:, half, :], misc[:, MISC_TURN0[n] % 2, :], t0[w][0][:, half, :],
                                      ALU.subtract).then_inc(t0_lo, 1)

            def state_(b, half):
                n = (b * 2 + half) * 5
                dve.wait_ge(upd, b * 2 + half + 1)
                need(dve, state_hi, b * 2 + half)
                need(dve, state_lo, b * 2 + half)
                u = misc[:, MISC_STATE[half] % 2, :].rearrange("p (c n) -> p c n", c=T)
                dve.tensor_tensor(state[:, 0], u[:, 0], chunk_decay[:, half], ALU.mult).then_inc(state_ok, 1)
                for c in range(1, T - 1):
                    dve.wait_ge(state_ok, n + 2 * c - 1)
                    dve.tensor_tensor(state[:, c], u[:, c], state[:, c - 1], ALU.add).then_inc(state_ok, 1)
                    dve.wait_ge(state_ok, n + 2 * c)
                    dve.tensor_tensor(state[:, c], state[:, c], chunk_decay[:, half], ALU.mult).then_inc(state_ok, 1)
                dve.wait_ge(state_hi, b * 2 + half + 1)
                dve.tensor_tensor(state_s[1][:], state[:], state_s[0][:], ALU.subtract).then_inc(state_lo, 1)

            sc_use = [0]

            def retain(b, arg):
                half, c = arg
                for g in range(2):
                    n = half * 8 + c * 2 + g
                    dve.wait_ge(r_sc, b * 16 + n + 1)
                    need(dve, r_hi, b * 16 + n - 1)
                    need(dve, r_lo, b * 16 + n - 1)
                    dve.tensor_tensor(rm[:, n % 2], sc[:, sc_use[0] % 2, :].rearrange("p (h n) -> p h n", h=4),
                                      causal[:, None, :].to_broadcast([P, 4, P]), ALU.mult).then_inc(r_mask, 1)
                    sc_use[0] += 1
                dve.wait_ge(r_out, b * 8 + half * 4 + c + 1)
                xs = x_p[:, c, half * P:(half + 1) * P]
                dve.tensor_tensor(xs, misc[:, MISC_RET[half * T + c] % 2, 0:P], xs, ALU.add).then_inc(r_add, 1)

            def quantise(b, _):
                dve.wait_ge(ln_out, b * 3 + 2)
                dve.wait_ge(tr0, (b + 1) * 4)
                count = [0]

                def done(ins):
                    count[0] += 1
                    ins.then_inc(quant, 1)
                    dve.wait_ge(quant, b * QUANT_STEPS + count[0])
                need(dve, xq_tr, b * 2)
                done(dve.tensor_scalar(flat(qa[:]), flat(x_b[:]), r_in[:, 0:1], None, ALU.mult))
                done(to_e4m3(flat(qa[:]), flat(qb[:]), flat(x_q[:]), done))
                assert count[0] == QUANT_STEPS

            def linear(b, _):
                for k in range(KD):
                    dve.wait_ge(xq_tr, b * 2 + k + 1)
                    need(dve, ffn_mm, b * 2)
                    dve.tensor_copy(xq_t[:, k, :], misc[:, (MISC_XQ + k) % 2, 0:256].bitcast(BF16)).then_inc(xq_cp, 1)
                for u in range(2):
                    n = b * 2 + u + 1
                    dve.wait_ge(ffn_mm, n)
                    need(dve, ffn_b, n - 1)
                    dve.tensor_scalar(y_a[:].rearrange("p t d -> p (t d)"), misc[:, (MISC_FFN + u) % 2, :],
                                      s_both[:, 0:1], None, ALU.mult).then_inc(ffn_y, 1)
                    dve.wait_ge(ffn_y, n)
                    need(dve, ffn_x, n - 1)
                    dve.tensor_tensor(y_b[:], y_a[:], bias0[:, None, :].to_broadcast([P, 2, D]),
                                      ALU.add).then_inc(ffn_b, 1)
                    dve.wait_ge(ffn_b, n)
                    xs = x_p[:, 2 * u:2 * u + 2, :]
                    dve.tensor_tensor(xs, xs, y_b[:], ALU.add).then_inc(ffn_x, 1)

            def project(b, _):
                for k in range(KD):
                    dve.wait_ge(t3_hi, b * 2 + k + 1)
                    dve.tensor_tensor(x3[1][:, k, :], misc[:, (MISC_X3 + k) % 2, :], x3[0][:, k, :],
                                      ALU.subtract).then_inc(t3_lo, 1)
                for n in range(4):
                    dve.wait_ge(qk_hi, b * 4 + n + 1)
                    dve.scalar_tensor_tensor(t1[1][:, n % 2, :], misc[:, (MISC_QK + n) % 2, :], 1 / WS,
                                             t1[0][:, n % 2, :], ALU.mult, ALU.subtract).then_inc(qk_lo, 1)
                for u in range(2):
                    dve.wait_ge(v_hi, b * 2 + u + 1)
                    view = lambda a: a[:, 2 * u:2 * u + 2, :, 0:HD].rearrange("p t h d -> p (t h) d")
                    dve.scalar_tensor_tensor(view(v_next[1]),
                                             misc[:, (MISC_V + u) % 2, :].rearrange("p (a d) -> p a d", d=HD), 1 / WS,
                                             view(v_next[0]), ALU.mult, ALU.subtract).then_inc(v_lo, 1)

            def maxima(b, arg):
                half, h = arg
                for qt in range(T):
                    n = half * 32 + h * T + qt
                    dve.wait_ge(m_sc, b * 64 + n + 1)
                    if h == 0 and qt == 0:
                        need(dve, m_16, b * 4 + half * 2)
                    dve.tensor_reduce(neg_max[:, qt, h % 2, h // 2:h // 2 + 1], sc[:, sc_use[0] % 2, :], AX.X,
                                      ALU.max, negate=True).then_inc(m_max, 1)
                    sc_use[0] += 1

            def max_rows(b, half):
                dve.wait_ge(m_max, b * 64 + half * 32 + 32)
                need(dve, m_tr, b * 2 + half)
                dve.tensor_copy(max16[:, :, :, 0, :], neg_max[:]).then_inc(m_16, 1)
                dve.wait_ge(m_16, b * 4 + half * 2 + 1)
                dve.tensor_tensor(max16[:, :, :, 1, :], neg_max[:], max16[:, :, :, 0, :],
                                  ALU.subtract).then_inc(m_16, 1)
                dve.wait_ge(m_tr, b * 2 + half + 1)
                need(dve, m_out, (b * 2 + half) * 16)
                dve.tensor_copy(max_t[:], sc[0:4 * HP, sc_use[0] % 2, 0:256].bitcast(F16)).then_inc(m_cp, 1)
                sc_use[0] += 1

            def hand_over(b, more):
                need(dve, pv_mm, b * 16)
                dve.wait_ge(v_lo, (b + 1) * 2)
                for hl in range(2):
                    dve.tensor_copy(v_cur[hl][:], v_next[hl][:]).then_inc(v_cp, 1)
                need(dve, x_out, b * 3 * 16)
                dve.wait_ge(ln_out, (b + 1) * 3)
                dve.tensor_copy(x_a[:], x_p[:]).then_inc(x_cp, 1)

            def score(b, h):
                for g in range(2):
                    n = 2 * h + g
                    dve.wait_ge(s_exp, b * 64 + 2 * n + 2)
                    need(dve, pv_mm, b * 16 + h - 1)
                    dve.tensor_copy(ph[:, h % 2, 2 * g:2 * g + 2, :], p32[:, g]).then_inc(p_hi, 1)

            def values(b, h):
                if h % 4 != 3:
                    return
                g = h // 4
                dve.wait_ge(pv_mm, b * 16 + h + 1)
                need(dve, o_mul, b * 4 + g)
                o = pv[:, g % 2, 0:4 * T * (HD + 1)].rearrange("p (h q d) -> p h q d", h=4, q=T)
                dve.reciprocal(rden[:], o[:, :, :, HD]).then_inc(o_rec, 1)
                if g == 0:
                    need(dve, tr4, b * 2)
                dve.wait_ge(o_rec, b * 4 + g + 1)
                dst = o_n[:].rearrange("p q (g h d) -> p g h q d", g=4, h=4)[:, g]
                dve.tensor_tensor(dst, o[:, :, :, 0:HD], rden[:, :, :, None].to_broadcast([P, 4, T, HD]),
                                  ALU.mult).then_inc(o_mul, 1)

            def out_project(b, _):
                for k in range(KD):
                    dve.wait_ge(o_hi, b * 2 + k + 1)
                    dve.tensor_tensor(o_t[1][:, k, :], pv[:, (4 + k) % 2, :], o_t[0][:, k, :],
                                      ALU.subtract).then_inc(o_lo, 1)
                dve.wait_ge(x_cp, b + 1)
                dve.tensor_tensor(x_a[:], x_a[:], biasp[:, None, :].to_broadcast([P, T, D]), ALU.add).then_inc(x_bias, 1)
                dve.wait_ge(x_bias, b + 1)
                for u in range(2):
                    dve.wait_ge(pr_mm, b * 2 + u + 1)
                    xs = x_a[:, 2 * u:2 * u + 2, :].rearrange("p t d -> p (t d)")
                    dve.scalar_tensor_tensor(xs, pv[:, (6 + u) % 2, :], 1 / WS, xs, ALU.mult, ALU.add).then_inc(pr_x, 1)
                dve.wait_ge(pr_x, (b + 1) * 2)
                dve.wait_ge(o_tr, (b + 1) * 2)
                normalise(x_a, o_n, bn6_a, mv_a, ve_a, rstd_a, la_bn, la_mv, la_ve, la_rs, la_out, b + 1)
                for k in range(KD):
                    dve.wait_ge(t4_hi, b * 2 + k + 1)
                    dve.tensor_tensor(o_t[1][:, k, :], pv[:, (8 + k) % 2, :], o_t[0][:, k, :],
                                      ALU.subtract).then_inc(t4_lo, 1)

            run({"layernorm": layernorm, "rotate": rotate, "turn0": turn0, "state": state_, "retain": retain,
                 "quantise": quantise, "linear": linear, "project": project, "maxima": maxima, "max_rows": max_rows,
                 "hand_over": hand_over, "score": score, "values": values, "out_project": out_project}, dve)

        @block.tensor
        def _(pe):
            pe.wait_ge(const_ok, CONSTS)
            pe.wait_ge(w16_lo, 3)
            pe.wait_ge(w8_step, W8_STEPS)

            THREE = ((0, 0), (0, 1), (1, 0))

            misc_read = [None, None]
            sc_read = [None, None]
            sc_use = [0]

            def misc_bank(n, b, read_by):
                before = misc_read[0]
                if before is None:
                    need(pe, v_lo, b * 2 - (2 - n) + 1)
                else:
                    pe.wait_ge(*before)
                misc_read[:] = [misc_read[1], read_by]
                return misc[:, n % 2, :]

            def sc_bank(read_by):
                if sc_read[0] is not None:
                    pe.wait_ge(*sc_read[0])
                sc_read[:] = [sc_read[1], read_by]
                sc_use[0] += 1
                return sc[:, (sc_use[0] - 1) % 2, :]

            def layernorm(b, j):
                if j == 0:
                    misc_read[:] = [None, None]

            def turn(bank, src, col):
                for i in range(T):
                    ins = pe.transpose(bank[:, i * P:(i + 1) * P], src[:, i, col * P:(col + 1) * P], ident[:])
                return ins

            def turn0(b, half):
                for w in range(2):
                    n = 2 * half + w
                    bank = misc_bank(MISC_TURN0[n], b, (t0_lo, b * 4 + n + 1))
                    pe.wait_ge(rot_q if w == 0 else rot_k, (b + 1) * 2)
                    turn(bank, q_r if w == 0 else k_r, half).then_inc(tr0, 1)

            def state_(b, half):
                bank = misc_bank(MISC_STATE[half], b, (state_ok, (b * 2 + half) * 5 + 5))
                for c in range(T - 1):
                    cols = slice(half * P, (half + 1) * P)
                    ins = pe.matmul(bank[:, c * P:(c + 1) * P], k_r[:, c, cols], ctx_n[:, c, cols],
                                    start=True, stop=True)
                ins.then_inc(upd, 1)

            def retain(b, arg):
                half, c = arg
                if c == 0:
                    pe.wait_ge(st0_in, (b * 2 + half + 1) * 12 * 16)
                tok = slice(c * P, (c + 1) * P)
                for g in range(2):
                    n = half * 8 + c * 2 + g
                    bank = sc_bank((r_mask, b * 16 + n + 1))
                    for i in range(4):
                        pair, par = 2 * g + i // 2, i % 2
                        ins = pe.matmul(bank[:, i * P:(i + 1) * P], kz0[par][0:KR, pair, tok], sq0[0:KR, pair, tok],
                                        start=True, stop=True)
                    ins.then_inc(r_sc, 1)
                bank = misc_bank(MISC_RET[half * T + c], b, (r_add, b * 8 + half * 4 + c + 1))
                first = True
                if c:
                    pe.wait_ge(state_lo, b * 2 + half + 1)
                    for qi, si in THREE:
                        pe.matmul(bank[:, 0:P], t0[0][qi][:, half, tok], state_s[si][:, c - 1, :],
                                  start=first, stop=False, skip_group_check=True)
                        first = False
                if c == 0 and half == 0:
                    pe.wait_ge(v0_lo, b + 1)
                for h in range(HH):
                    if h % 4 == 0:
                        pe.wait_ge(r_lo, b * 16 + half * 8 + c * 2 + h // 4 + 1)
                    col = half * P + h * HD
                    for si, vi in THREE:
                        ins = pe.matmul(bank[:, h * HD:(h + 1) * HD], rs[si][:, c % 2, h, :],
                                        v0[vi][:, c, col:col + HD], start=first, stop=True, skip_group_check=True)
                        first = False
                ins.then_inc(r_out, 1)

            def linear(b, _):
                for k in range(KD):
                    bank = misc_bank(MISC_XQ + k, b, (xq_cp, b * 2 + k + 1))
                    pe.wait_ge(quant, (b + 1) * QUANT_STEPS)
                    for i in range(T):
                        ins = pe.transpose(bank[:, i * 64:(i + 1) * 64].bitcast(BF16), x_q[:, i, k * P:(k + 1) * P],
                                           ident_bf[:])
                    ins.then_inc(xq_tr, 1)
                for u in range(2):
                    bank = misc_bank(MISC_FFN + u, b, (ffn_y, b * 2 + u + 1))
                    pe.wait_ge(xq_cp, (b + 1) * 2)
                    for i in range(2):
                        tok = slice((2 * u + i) * P, (2 * u + i + 1) * P)
                        for k in range(KD):
                            ins = pe.matmul(bank[:, i * D:(i + 1) * D], xq_t[:, k, tok], w8[:, k, :],
                                            start=(k == 0), stop=(k == KD - 1))
                    ins.then_inc(ffn_mm, 1)

            def project(b, _):
                for k in range(KD):
                    bank = misc_bank(MISC_X3 + k, b, (t3_lo, b * 2 + k + 1))
                    pe.wait_ge(ln_out, (b + 1) * 3)
                    turn(bank, x_n, k).then_inc(tr3, 1)
                for n in range(4):
                    w, m = n // 2, n % 2
                    bank = misc_bank(MISC_QK + n, b, (qk_lo, b * 4 + n + 1))
                    pe.wait_ge(*((t3_lo, (b + 1) * 2) if w == 0 else (c3_lo, b + 1)))
                    src, wt = (x3, wq) if w == 0 else (c3, wkv)
                    for j, (wi, xi) in enumerate(THREE):
                        for k in range(KD):
                            ins = pe.matmul(bank, wt[wi][:, k, m * P:(m + 1) * P], src[xi][:, k, :],
                                            start=(j == 0 and k == 0), stop=(j == 2 and k == KD - 1))
                    ins.then_inc(qk_mm, 1)
                for u in range(2):
                    bank = misc_bank(MISC_V + u, b, (v_lo, b * 2 + u + 1))
                    for i in range(2):
                        tok = slice((2 * u + i) * P, (2 * u + i + 1) * P)
                        for j, (xi, wi) in enumerate(THREE):
                            for k in range(KD):
                                ins = pe.matmul(bank[:, i * D:(i + 1) * D], c3[xi][:, k, tok], wkv[wi][:, k, D:2 * D],
                                                start=(j == 0 and k == 0), stop=(j == 2 and k == KD - 1))
                    ins.then_inc(v_mm, 1)

            def maxima(b, arg):
                half, h = arg
                if h == 0:
                    pe.wait_ge(st1_in[half], (b + 1) * 12 * 16)
                for qt in range(T):
                    bank = sc_bank((m_max, b * 64 + half * 32 + h * T + qt + 1))
                    pe.matmul(bank, sq1[0:KR, half, h // 2, qt * P:(qt + 1) * P], kz1[h % 2][0:KR, half, h // 2, :],
                              start=True, stop=True).then_inc(m_sc, 1)

            def max_rows(b, half):
                bank = sc_bank((m_cp, b * 2 + half + 1))
                pe.wait_ge(m_16, b * 4 + half * 2 + 2)
                for qt in range(T):
                    ins = pe.transpose(bank[0:4 * HP, qt * 64:(qt + 1) * 64].bitcast(F16),
                                       max16[:, qt].rearrange("p r l q -> p (r l q)"), ident16[:])
                ins.then_inc(m_tr, 1)

            def hand_over(b, more):
                sc_read[:] = [(m_max, b * 64 + 32), (m_cp, b * 2 + 1)]

            def score(b, h):
                half, pair, par = h // HH, (h % HH) // 2, h % 2
                if h % HH == 0:
                    pe.wait_ge(m_in[half], (b + 1) * 16)
                    if half == 0:
                        pe.wait_ge(rows_in, 2 * 16)
                for kt in range(T):
                    need(pe, s_exp, b * 64 + h * 4 + kt - 1)
                    pe.matmul(st[:, kt % 2, :], kz1[par][0:MR, half, pair, kt * P:(kt + 1) * P],
                              sq1[0:MR, half, pair, :], start=True, stop=True).then_inc(s_mm, 1)

            def pv_bank(n, b):
                readers = ([(o_mul, b * 4 + g + 1) for g in range(4)] + [(o_lo, b * 2 + 1), (o_lo, b * 2 + 2)]
                           + [(pr_x, b * 2 + 1), (pr_x, b * 2 + 2)])
                if n < 2:
                    need(pe, t4_lo, b * 2 + n - 1)
                else:
                    pe.wait_ge(*readers[n - 2])
                return pv[:, n % 2, :]

            def values(b, h):
                g = h // 4
                if h % 4 == 0:
                    pv_bank(g, b)
                if h == 0:
                    pe.wait_ge(v_cp, (b + 1) * 2)
                pe.wait_ge(p_lo, b * 32 + 2 * h + 2)
                o = pv[:, g % 2, 0:4 * T * (HD + 1)].rearrange("p (h q d) -> p h q d", h=4, q=T)
                parts = (ph, pl)
                for qt in range(T):
                    for kt in range(T):
                        for j, (pi, vi) in enumerate(THREE):
                            ins = pe.matmul(o[:, h % 4, qt, :], parts[pi][:, h % 2, kt, qt * P:(qt + 1) * P],
                                            v_cur[vi][:, kt, h, :], start=(kt == 0 and j == 0),
                                            stop=(kt == T - 1 and j == 2))
                ins.then_inc(pv_mm, 1)

            def out_project(b, _):
                for k in range(KD):
                    bank = pv_bank(4 + k, b)
                    pe.wait_ge(o_mul, (b + 1) * 4)
                    turn(bank, o_n, k).then_inc(o_tr, 1)
                for u in range(2):
                    bank = pv_bank(6 + u, b)
                    pe.wait_ge(o_lo, (b + 1) * 2)
                    for i in range(2):
                        tok = slice((2 * u + i) * P, (2 * u + i + 1) * P)
                        for j, (oi, wi) in enumerate(THREE):
                            for k in range(KD):
                                ins = pe.matmul(bank[:, i * D:(i + 1) * D], o_t[oi][:, k, tok], wp[wi][:, k, :],
                                                start=(j == 0 and k == 0), stop=(j == 2 and k == KD - 1))
                    ins.then_inc(pr_mm, 1)
                for k in range(KD):
                    bank = pv_bank(8 + k, b)
                    pe.wait_ge(la_out, b + 1)
                    turn(bank, o_n, k).then_inc(tr4, 1)

            run({"layernorm": layernorm, "turn0": turn0, "state": state_, "retain": retain, "linear": linear,
                 "project": project, "maxima": maxima, "max_rows": max_rows, "hand_over": hand_over, "score": score,
                 "values": values, "out_project": out_project}, pe)


MISC_TURN0 = [0, 1, 7, 8]
MISC_STATE = [2, 9]
MISC_RET = [3, 4, 5, 6, 10, 11, 12, 13]
MISC_XQ, MISC_FFN, MISC_X3, MISC_QK, MISC_V = 14, 16, 18, 20, 24
N_CONST = 15
CONSTS = 5
W8_STEPS = 8
QUANT_STEPS = 7


def phase_m(nc, t, out, x_d, xt_d, raw, raw_b, w_loaded):
    with ExitStack() as ctx:
        def sb(name, shape, dt=F32):
            return ctx.enter_context(nc.sbuf_tensor(name, shape, dt))

        def sem(name):
            return ctx.enter_context(nc.semaphore(name))

        N = B * S
        CH = N // 512
        U = CH * IT
        GU, DN = KD * 2 * I, IT * D
        WSTEP = 1024
        WP = (GU + DN) // WSTEP
        LAG = 2

        x_all = sb("x_all", [P, NT, D])
        xt = [sb(f"xt{i}", [P, B, KD, S], F16) for i in range(2)]
        ident, before = sb("ident_m", [P, P]), sb("before", [P, E, E])
        wr_raw = sb("wr_raw", [P, KD, E])
        wr = [sb(f"wr{i}", [P, KD, E], F16) for i in range(2)]
        bias_r, bias_d = sb("bias_r", [P, E]), sb("bias_d", [E, D])
        logit = sb("logit", [P, NT, E])
        above, equal = sb("above", [P, NT, E * E]), sb("equal", [P, NT, E * E])
        rank, top, expo = sb("rank", [P, NT, E]), sb("top", [P, NT]), sb("expo", [P, NT, E])
        total, combine = sb("total", [P, NT]), sb("combine", [P, NT, E])
        scaled = sb("scaled", [P, E, NT])
        combine_t = sb("combine_t", [E, N])
        w = [[sb(f"w_{e}{i}", [P, GU + DN], F16) for i in range(2)] for e in range(2)]
        bias16, share = sb("bias16", [P, 2, 8]), sb("share", [P, 2, NT])
        gate, up = sb("gate", [P, 2, 512]), sb("up", [P, 2, 512])
        glu, prod = sb("glu", [P, 2, 512]), sb("prod", [P, 2, 512])
        h16 = [sb(f"h16_{i}", [P, 4, 512], F16) for i in range(2)]

        gu_ps = ctx.enter_context(nc.psum_tensor("gu_ps", [P, 4, 512], F32))
        dn_ps = ctx.enter_context(nc.psum_tensor("dn_ps", [P, 4, 512], F32))

        const_in = sem("m_const_in")
        x_in = sem("m_x_in")
        wr_hi, wr_lo = sem("wr_hi"), sem("wr_lo")
        rt_mm = sem("rt_mm")
        rt = sem("rt")
        rt_exp = sem("rt_exp")
        ct_tr, ct_cp = sem("ct_tr"), sem("ct_cp")
        bd_mm, bd_x = sem("bd_mm"), sem("bd_x")
        w_in = sem("w_in")
        w_hi, w_lo = sem("w_hi"), sem("w_lo")
        w_bias, w_share = sem("w_bias"), sem("w_share")
        gate_mm, up_mm = sem("gate_mm"), sem("up_mm")
        gate_ok, glu_ok, up_ok, prod_ok = sem("gate_ok"), sem("glu_ok"), sem("up_ok"), sem("prod_ok")
        h_hi, h_lo = sem("h_hi"), sem("h_lo")
        dn_mm, dn_x = sem("dn_mm"), sem("dn_x")
        y_out = sem("y_out")
        N_CONST_M = 6

        def moe(run_expert):
            def emit(engine, loop=True):
                for k in range(2):
                    run_expert(k, k, False)
                if loop:
                    with engine.Fori(1, E // 2 - 1) as i:
                        for k in range(2):
                            run_expert(2 * i + k, k, False)
                else:
                    for e in range(2, E - 2):
                        run_expert(e, e % 2, False)
                for k in range(2):
                    run_expert(E - 2 + k, k, k == 1)
            return emit

        block = ctx.enter_context(nc.Block())

        @block.sync
        def _(sp):
            def load_w(e):
                gu = t["gate_up_t"].rearrange("e (k p) j -> e p k j", k=KD)[bass.ds(e, 1)].rearrange("a p k j -> (a p) k j")
                sp.dma_start(raw[:, 0:GU].rearrange("p (k j) -> p k j", k=KD), gu).then_inc(w_in, 16)
                dn = t["down_t"].rearrange("e (k p) d -> e p k d", k=IT)[bass.ds(e, 1)].rearrange("a p k d -> (a p) k d")
                sp.dma_start(raw[:, GU:].rearrange("p (k d) -> p k d", k=IT), dn).then_inc(w_in, 16)
                sp.dma_start(raw_b[:, 0, :], t["gate_up_bias_t"][bass.ds(e, 1)].rearrange("a p j -> (a p) j")).then_inc(w_in, 16)

            sp.dma_start(ident[:], t["ident"]).then_inc(const_in, 16)
            sp.dma_start(before[:], t["before"]).then_inc(const_in, 16)
            sp.dma_start(wr_raw[:], t["wr_t"].rearrange("(k p) e -> p k e", k=KD)).then_inc(const_in, 16)
            sp.dma_start(bias_r[:], t["L1_ffn_router_bias"][None, :].to_broadcast([P, E])).then_inc(const_in, 16)
            sp.dma_start(bias_d[:], t["L1_ffn_down_proj_bias"]).then_inc(const_in, 16)
            for hl in range(2):
                sp.dma_start(xt[hl][:], xt_d[hl].rearrange("b p k n -> p b k n")).then_inc(x_in, 16)
            load_w(0)
            sp.dma_start(x_all[:], x_d.rearrange("t p d -> p t d")).then_inc(const_in, 16)

            def after(e):
                sp.wait_ge(w_lo, (e + 1) * WP)
                sp.wait_ge(w_bias, (e + 1) * 2)

            def expert(e, k, last):
                if not last:
                    after(e)
                    load_w(e + 1)

            moe(expert)(sp, loop=False)
            for c in range(CH):
                sp.wait_ge(dn_x, (E - 1) * NT + 4 * c + 4)
                sp.dma_start(out.rearrange("(c t p) d -> c p t d", c=CH, t=4)[c],
                             x_all[:, 4 * c:4 * c + 4, :]).then_inc(y_out, 16)
            sp.wait_ge(y_out, CH * 16)

        def pieces():
            return [slice(i * WSTEP, (i + 1) * WSTEP) for i in range(WP)]

        @block.scalar
        def _(act):
            act.wait_ge(const_in, N_CONST_M * 16)
            act.activation(wr[0][:], wr_raw[:], ACT.Copy, scale=WS).then_inc(wr_hi, 1)
            act.wait_ge(rt, RT_SUB)
            act.activation(expo[:], expo[:], ACT.Exp).then_inc(rt_exp, 1)

            def split(e, k, i):
                if i == 0:
                    act.wait_ge(w_in, (e + 1) * 3 * 16)
                    need(act, dn_mm, (e - 1) * U)
                act.activation(w[k][0][:, pieces()[i]], raw[:, pieces()[i]], ACT.Copy, scale=WS).then_inc(w_hi, 1)

            def unit(e, k, u):
                n = e * U + u
                act.wait_ge(gate_ok, n + 1)
                need(act, prod_ok, n - 1)
                act.activation(glu[:, u % 2, :], gate[:, u % 2, :], ACT.Gelu_apprx_sigmoid,
                               scale=1 / WS).then_inc(glu_ok, 1)
                act.wait_ge(prod_ok, n + 1)
                need(act, dn_mm, n - 3)
                act.activation(h16[0][:, u % 4, :], prod[:, u % 2, :], ACT.Copy).then_inc(h_hi, 1)

            for i in range(WP):
                split(0, 0, i)
            for u in range(LAG):
                unit(0, 0, u)

            def expert(e, k, last):
                for u in range(U):
                    if not last and u in SPLIT_AT:
                        split(e + 1, 1 - k, SPLIT_AT.index(u))
                    if u + LAG < U:
                        unit(e, k, u + LAG)
                    elif not last:
                        unit(e + 1, 1 - k, u + LAG - U)

            moe(expert)(act)

        @block.gpsimd
        def _(pool):
            def unit(e, k, u):
                n = e * U + u
                pool.wait_ge(h_hi, n + 1)
                pool.tensor_tensor(h16[1][:, u % 4, :], prod[:, u % 2, :], h16[0][:, u % 4, :],
                                   ALU.subtract).then_inc(h_lo, 1)

            for u in range(LAG):
                unit(0, 0, u)

            def expert(e, k, last):
                for u in range(U):
                    if u + LAG < U:
                        unit(e, k, u + LAG)
                    elif not last:
                        unit(e + 1, 1 - k, u + LAG - U)

            moe(expert)(pool)

        @block.vector
        def _(dve):
            count = [0]

            def done(ins):
                count[0] += 1
                ins.then_inc(rt, 1)
                dve.wait_ge(rt, count[0])

            dve.wait_ge(wr_hi, 1)
            dve.scalar_tensor_tensor(wr[1][:], wr_raw[:], WS, wr[0][:], ALU.mult, ALU.subtract).then_inc(wr_lo, 1)

            dve.wait_ge(const_in, N_CONST_M * 16)
            dve.wait_ge(rt_mm, 1)
            flat = lambda a: a[:].rearrange("p t e -> p (t e)")
            per_expert = lambda a: a[:].to_broadcast([P, NT, E])
            done(dve.tensor_scalar(flat(logit), dn_ps[:, 0, 0:NT * E], 1 / WS, None, ALU.mult))
            done(dve.tensor_tensor(logit[:], logit[:], bias_r[:, None, :].to_broadcast([P, NT, E]), ALU.add))
            square = lambda a: a[:].rearrange("p t (i j) -> p t i j", i=E)
            this, other = logit[:, :, :, None].to_broadcast([P, NT, E, E]), logit[:, :, None, :].to_broadcast([P, NT, E, E])
            dve.tensor_tensor(square(above), other, this, ALU.is_gt)
            done(dve.tensor_tensor(square(equal), other, this, ALU.is_equal))
            done(dve.tensor_tensor(equal[:], equal[:], before[:].rearrange("p i j -> p (i j)")[:, None, :]
                                   .to_broadcast([P, NT, E * E]), ALU.mult))
            done(dve.tensor_tensor(above[:], above[:], equal[:], ALU.add))
            done(dve.tensor_reduce(rank[:], square(above), AX.X, ALU.add))
            dve.tensor_scalar(rank[:], rank[:], TOPK - 0.5, None, ALU.is_lt)
            done(dve.tensor_reduce(top[:], logit[:], AX.X, ALU.max))
            done(dve.tensor_tensor(expo[:], logit[:], top[:, :, None].to_broadcast([P, NT, E]), ALU.subtract))
            assert count[0] == RT_SUB
            dve.wait_ge(rt_exp, 1)
            done(dve.tensor_tensor(expo[:], expo[:], rank[:], ALU.mult))
            done(dve.tensor_reduce(total[:], expo[:], AX.X, ALU.add))
            done(dve.reciprocal(total[:], total[:]))
            done(dve.tensor_tensor(combine[:], expo[:], total[:, :, None].to_broadcast([P, NT, E]), ALU.mult))
            done(dve.tensor_scalar(scaled[:].rearrange("p e t -> p t e"), combine[:], 1 / (WS * WS), None, ALU.mult))
            assert count[0] == RT_STEPS
            for c in range(4):
                dve.wait_ge(ct_tr, c + 1)
                dve.tensor_copy(combine_t[:, c * 512:(c + 1) * 512], dn_ps[0:E, c, :]).then_inc(ct_cp, 1)
            for u in range(NT // 2):
                dve.wait_ge(bd_mm, u + 1)
                xs = x_all[:, 2 * u:2 * u + 2, :].rearrange("p t d -> p (t d)")
                dve.tensor_tensor(xs, dn_ps[:, u % 4, :], xs, ALU.add).then_inc(bd_x, 1)
            dve.wait_ge(bd_x, NT // 2)

            def split(e, k, i):
                dve.wait_ge(w_hi, e * WP + i + 1)
                dve.scalar_tensor_tensor(w[k][1][:, pieces()[i]], raw[:, pieces()[i]], WS, w[k][0][:, pieces()[i]],
                                         ALU.mult, ALU.subtract).then_inc(w_lo, 1)
                if i == 0:
                    need(dve, up_ok, (e - 1) * U)
                    dve.tensor_scalar(bias16[:, k, 0:4], raw_b[:, 0, 0:4], WS, None, ALU.mult).then_inc(w_bias, 1)
                    dve.tensor_scalar(bias16[:, k, 4:8], raw_b[:, 0, 4:8], WS, WS, ALU.mult, ALU.add).then_inc(w_bias, 1)
                    dve.tensor_copy(share[:, k:k + 1, :], scaled[:, bass.ds(e, 1), :]).then_inc(w_share, 1)

            def unit(e, k, u):
                n = e * U + u
                it = u % IT
                dve.wait_ge(gate_mm, n + 1)
                if u == 0:
                    dve.wait_ge(w_bias, (e + 1) * 2)
                need(dve, glu_ok, n - 1)
                dve.tensor_scalar(gate[:, u % 2, :], gu_ps[:, 2 * (u % 2), :], bias16[:, k, it:it + 1], WS * LIMIT,
                                  ALU.add, ALU.min).then_inc(gate_ok, 1)
                dve.wait_ge(up_mm, n + 1)
                dve.tensor_scalar(up[:, u % 2, :], gu_ps[:, 2 * (u % 2) + 1, :], bias16[:, k, 4 + it:5 + it],
                                  WS * (LIMIT + 1), ALU.add, ALU.min).then_inc(up_ok, 1)
                dve.wait_ge(up_ok, n + 1)
                dve.wait_ge(glu_ok, n + 1)
                need(dve, h_hi, n - 1)
                need(dve, h_lo, n - 1)
                dve.scalar_tensor_tensor(prod[:, u % 2, :], up[:, u % 2, :], WS * (1 - LIMIT), glu[:, u % 2, :],
                                         ALU.max, ALU.mult).then_inc(prod_ok, 1)

            def collect(e, k, c):
                dve.wait_ge(dn_mm, e * U + IT * (c + 1))
                if c == 0:
                    dve.wait_ge(w_share, e + 1)
                    need(dve, dn_x, e * NT)
                for i in range(4):
                    tile = 4 * c + i
                    xs = x_all[:, tile, :]
                    dve.scalar_tensor_tensor(xs, dn_ps[:, 2 * (c % 2) + i // 2, (i % 2) * D:(i % 2 + 1) * D],
                                             share[:, k, tile:tile + 1], xs, ALU.mult, ALU.add).then_inc(dn_x, 1)

            for i in range(WP):
                split(0, 0, i)
            for u in range(LAG):
                unit(0, 0, u)

            def expert(e, k, last):
                for u in range(U):
                    if not last and u in SPLIT_AT:
                        split(e + 1, 1 - k, SPLIT_AT.index(u))
                    if u + LAG < U:
                        unit(e, k, u + LAG)
                    elif not last:
                        unit(e + 1, 1 - k, u + LAG - U)
                    if u % IT == IT - 1:
                        collect(e, k, u // IT)

            moe(expert)(dve)

        @block.tensor
        def _(pe):
            THREE = ((0, 0), (0, 1), (1, 0))
            pe.wait_ge(x_in, 2 * 16)
            pe.wait_ge(wr_lo, 1)
            for tile in range(NT):
                b, tok = tile // T, slice((tile % T) * P, (tile % T + 1) * P)
                for j, (xi, wi) in enumerate(THREE):
                    for k in range(KD):
                        ins = pe.matmul(dn_ps[:, 0, tile * E:(tile + 1) * E], xt[xi][:, b, k, tok], wr[wi][:, k, :],
                                        start=(j == 0 and k == 0), stop=(j == 2 and k == KD - 1))
            ins.then_inc(rt_mm, 1)
            pe.wait_ge(rt, RT_STEPS)
            for c in range(4):
                for i in range(4):
                    ins = pe.transpose(dn_ps[0:E, c, i * P:(i + 1) * P], combine[:, 4 * c + i, :], ident[:])
                ins.then_inc(ct_tr, 1)
            for u in range(NT // 2):
                if u < 4:
                    pe.wait_ge(ct_cp, 4)
                else:
                    pe.wait_ge(bd_x, u - 3)
                for i in range(2):
                    tile = 2 * u + i
                    ins = pe.matmul(dn_ps[:, u % 4, i * D:(i + 1) * D], combine_t[:, tile * P:(tile + 1) * P], bias_d[:],
                                    start=True, stop=True)
                ins.then_inc(bd_mm, 1)

            def gate_up(e, k, u):
                n = e * U + u
                c, it = u // IT, u % IT
                if u == 0:
                    pe.wait_ge(w_lo, (e + 1) * WP)
                for g, (mm, ok) in enumerate(((gate_mm, gate_ok), (up_mm, up_ok))):
                    need(pe, ok, n - 1)
                    for j, (wi, xi) in enumerate(THREE):
                        for kd in range(KD):
                            col = kd * 2 * I + g * I + it * P
                            ins = pe.matmul(gu_ps[:, 2 * (u % 2) + g, :], w[k][wi][:, col:col + P], xt[xi][:, c, kd, :],
                                            start=(j == 0 and kd == 0), stop=(j == 2 and kd == KD - 1))
                    ins.then_inc(mm, 1)

            def down(e, k, u):
                c, it = u // IT, u % IT
                pe.wait_ge(h_lo, e * U + u + 1)
                if it == 0:
                    need(pe, dn_x, e * NT + 4 * (c - 1))
                    if isinstance(e, int) and e == 0 or c == 0:
                        pe.wait_ge(bd_x, NT // 2)
                for i in range(4):
                    for j, (hi, wi) in enumerate(THREE):
                        ins = pe.matmul(dn_ps[:, 2 * (c % 2) + i // 2, (i % 2) * D:(i % 2 + 1) * D],
                                        h16[hi][:, u % 4, i * P:(i + 1) * P],
                                        w[k][wi][:, GU + it * D:GU + (it + 1) * D],
                                        start=(it == 0 and j == 0 and i % 2 == 0), stop=(it == IT - 1 and j == 2),
                                        skip_group_check=True)
                ins.then_inc(dn_mm, 1)

            for u in range(LAG):
                gate_up(0, 0, u)

            def expert(e, k, last):
                for u in range(U):
                    if u + LAG < U:
                        gate_up(e, k, u + LAG)
                    elif not last:
                        gate_up(e + 1, 1 - k, u + LAG - U)
                    down(e, k, u)

            moe(expert)(pe)


RT_SUB, RT_STEPS = 8, 13
SPLIT_AT = [3, 6, 9]


_INS = ["x", "ctx", "ctx_swapped", "ctx_t", "L0_ffn_kernel", "L0_ffn_input_scale", "L0_ffn_kernel_scale",
        "L0_ffn_bias", "wq_t", "wkv_t", "wp_t", "L1_xattn_bproj", "wr_t", "L1_ffn_router_bias", "gate_up_t",
        "gate_up_bias_t", "down_t", "L1_ffn_down_proj_bias"]


def kernel(**inputs):
    import concourse.bacc as bacc
    from concourse.bass_utils import run_bass_kernel_spmd

    a = {k: np.asarray(v) for k, v in inputs.items()}
    flat = a["ctx_1024"].reshape(B * S, D)
    a["x"] = a["x"].reshape(B * S, D)
    a["ctx"] = flat
    a["ctx_swapped"] = flat.reshape(B * S, D // 2, 2)[:, :, ::-1].reshape(B * S, D)
    a["ctx_t"] = flat.T
    a["wq_t"], a["wkv_t"], a["wp_t"] = a["L1_xattn_Wq"].T, a["L1_xattn_Wkv"].T, a["L1_xattn_Wproj"].T
    a["wr_t"] = a["L1_ffn_router_weight"].T
    a["gate_up_t"] = a["L1_ffn_gate_up_proj"].transpose(0, 2, 1)
    a["gate_up_bias_t"] = a["L1_ffn_gate_up_proj_bias"].reshape(E, 8, P).transpose(0, 2, 1)
    a["down_t"] = a["L1_ffn_down_proj"].transpose(0, 2, 1)
    arrays = {name: np.ascontiguousarray(a[name]) for name in _INS}
    arrays.update(tables())
    nc = bacc.Bacc("TRN2", target_bir_lowering=False, num_devices=1)
    aps = {name: nc.dram_tensor(f"in_{name}", v.shape, mybir.dt.from_np(v.dtype), kind="ExternalInput").ap()
           for name, v in arrays.items()}
    out = nc.dram_tensor("out", (B * S, D), F32, kind="ExternalOutput").ap()
    xattn_ffn_moe_kernel(nc, aps, out)
    r = run_bass_kernel_spmd(nc, [{f"in_{name}": v for name, v in arrays.items()}], core_ids=[0])
    return r.results[0]["out"].reshape(B, S, D)
```

```python
from contextlib import ExitStack

import concourse.bass as bass
import numpy as np
from concourse import mybir

F32, F16, BF16, I32 = mybir.dt.float32, mybir.dt.float16, mybir.dt.bfloat16, mybir.dt.int32
ALU, ACT, AX = mybir.AluOpType, mybir.ActivationFunctionType, mybir.AxisListType

P = 128
B, S, D = 4, 512, 256
H, HD = 16, 16
T = S // P
KD = D // P
NT = B * T
E, I = 8, 512
IT = I // P
PAIRS = H // 2
HP = PAIRS // 2
HH = H // 2
SR = 3 * HD
KR = 2 * SR
MR = KR + 4
WS = 16.0
LIMIT, EPS = 7.0, 1e-5
QSCALE = float(HD) ** -0.5
TOPK = 4


def need(eng, sem, value):
    if not (isinstance(value, int) and value <= 0):
        eng.wait_ge(sem, value)


def tables():
    pos = np.arange(S, dtype=np.float64)
    base = (np.arange(0, HD, 2) + 0.4 * HD) / (1.4 * HD)
    scale = base[None, :] ** (pos / 512.0)[:, None]
    angle = pos[:, None] / 10000.0 ** (np.arange(HD // 2) / (HD // 2))[None, :]
    gamma = (1.0 - np.exp(np.linspace(np.log(1 / 32), np.log(1 / 512), H))).astype(np.float32).astype(np.float64)
    sign = np.array([-1.0, 1.0])
    within = pos % P
    out = {}
    for name, s, decay in (("q", scale, gamma[None, :] ** within[:, None]),
                           ("k", 1.0 / scale, gamma[None, :] ** -within[:, None])):
        cos = np.repeat(np.cos(angle) * s, 2, axis=-1)
        sin = np.repeat(np.sin(angle) * s, 2, axis=-1) * np.tile(sign, HD // 2)
        for part, t in (("cos", cos), ("sin", sin)):
            full = (decay[:, :, None] * t[:, None, :]).reshape(S, D)
            out[f"{name}_{part}"] = np.ascontiguousarray(full.reshape(T, P, D).transpose(1, 0, 2), np.float32)
    head = np.arange(D) // HD
    block = np.zeros((P, 2, P), np.float32)
    for half in range(2):
        hs = head[half * P:(half + 1) * P]
        block[:, half] = (hs[:, None] == hs[None, :]) * (gamma[hs] ** P)[:, None]
    out["chunk_decay"] = block
    out["causal"] = (np.arange(P)[None, :] >= np.arange(P)[:, None]).astype(np.float32)
    out["ident"] = np.eye(P, dtype=np.float32)
    ones = np.zeros((4, 2, 2 * HP * S), np.float32)
    ones[0:2, 0], ones[2:4, 1] = 1.0, 1.0
    out["max_rows"] = ones.astype(np.float16)
    out["before"] = np.tile((np.arange(E)[None, :] < np.arange(E)[:, None]).astype(np.float32)[None], (P, 1, 1))
    return out


def xattn_ffn_moe_kernel(nc, t, out):
    dram = lambda name, shape, dt: nc.dram_tensor(name, shape, dt, kind="Internal").ap()
    stack0_d = dram("stack0_d", (2, 2, D, S), F16)
    stack1_d = dram("stack1_d", (2, 2, D, S), F16)
    max_d = dram("max_d", (2, 4 * HP, S), F16)
    x_d = dram("x_d", (NT, P, D), F32)
    xt_d = dram("xt_d", (2, B, P, KD, S), F16)

    with ExitStack() as both:
        raw = both.enter_context(nc.sbuf_tensor("raw", [P, KD * 2 * I + IT * D], F32))
        raw_b = both.enter_context(nc.sbuf_tensor("raw_b", [P, 2, 8], F32))
        w_loaded = both.enter_context(nc.semaphore("w_loaded"))
        phase_a(nc, t, stack0_d, stack1_d, max_d, x_d, xt_d)
        phase_m(nc, t, out, x_d, xt_d, raw, raw_b, w_loaded)


def phase_a(nc, t, stack0_d, stack1_d, max_d, x_d, xt_d):
    with ExitStack() as ctx:
        def sb(name, shape, dt=F32):
            return ctx.enter_context(nc.sbuf_tensor(name, shape, dt))

        def sem(name):
            return ctx.enter_context(nc.semaphore(name))

        q_cos, q_sin = sb("q_cos", [P, T, D]), sb("q_sin", [P, T, D])
        k_cos, k_sin = sb("k_cos", [P, T, D]), sb("k_sin", [P, T, D])
        chunk_decay = sb("chunk_decay", [P, 2, P])
        causal, ident = sb("causal", [P, P]), sb("ident", [P, P])
        ident16, ident_bf = sb("ident16", [P, P], F16), sb("ident_bf", [P, P], BF16)
        half_power = sb("half_power", [P, T])
        wq = [sb(f"wq{i}", [P, KD, D], F16) for i in range(2)]
        wkv = [sb(f"wkv{i}", [P, KD, 2 * D], F16) for i in range(2)]
        wp = [sb(f"wp{i}", [P, KD, D], F16) for i in range(2)]
        w8_raw, w8 = sb("w8_raw", [P, KD, D], BF16), sb("w8", [P, KD, D], BF16)
        bias0, biasp = sb("bias0", [P, D], BF16), sb("biasp", [P, D])
        s_in, s_k = sb("s_in", [P, 1]), sb("s_k", [P, 1])
        r_in, r_k, s_both = sb("r_in", [P, 1]), sb("r_k", [P, 1]), sb("s_both", [P, 1])
        ctx_n, ctx_s, ctx_t = sb("ctx_n", [P, T, D]), sb("ctx_s", [P, T, D]), sb("ctx_t", [P, KD, S])
        x_p, x_n = sb("x_p", [P, T, D]), sb("x_n", [P, T, D])
        bn6, mv, ve, rstd = sb("bn6", [P, T, 6]), sb("mv", [P, 4, T]), sb("ve", [P, T]), sb("rstd", [P, T])
        q_r, q_s, k_r = sb("q_r", [P, T, D]), sb("q_s", [P, T, D]), sb("k_r", [P, T, D])
        t0 = [[sb(f"t0_{w}{i}", [P, 2, S], F16) for i in range(2)] for w in "qk"]
        v0 = [sb(f"v0_{i}", [P, T, D], F16) for i in range(2)]
        state = sb("state", [P, T - 1, P])
        state_s = [sb(f"state_s{i}", [P, T - 1, P], F16) for i in range(2)]
        sq0 = sb("sq0", [P, HP, S], F16)
        kz0 = [sb(f"kz0_{i}", [P, HP, S], F16) for i in range(2)]
        rm = sb("rm", [P, 2, 4, P])
        rs = [sb(f"rs{i}", [P, 2, HH, P], F16) for i in range(2)]
        x_b, x_q, xq_t = sb("x_b", [P, T, D], BF16), sb("x_q", [P, T, D], BF16), sb("xq_t", [P, KD, S], BF16)
        y_a, y_b = sb("y_a", [P, 2, D], BF16), sb("y_b", [P, 2, D], BF16)
        x3 = [sb(f"x3_{i}", [P, KD, S], F16) for i in range(2)]
        c3 = [sb(f"c3_{i}", [P, KD, S], F16) for i in range(2)]
        t1 = [sb(f"t1_{i}", [P, 2, S], F16) for i in range(2)]
        v_next = [sb(f"v_next{i}", [P, T, H, HD + 1], F16) for i in range(2)]
        v_cur = [sb(f"v_cur{i}", [P, T, H, HD + 1], F16) for i in range(2)]
        sq1 = sb("sq1", [P, 2, HP, S], F16)
        kz1 = [sb(f"kz1_{i}", [P, 2, HP, S], F16) for i in range(2)]
        neg_max = sb("neg_max", [P, T, 2, HP])
        max16 = sb("max16", [P, T, 2, 2, HP], F16)
        max_t = sb("max_t", [4 * HP, S], F16)
        p32 = sb("p32", [P, 2, 2, S])
        ph, pl = sb("ph", [P, 2, T, S], F16), sb("pl", [P, 2, T, S], F16)
        rden, o_n = sb("rden", [P, 4, T]), sb("o_n", [P, T, D])
        o_t = [sb(f"o_t{i}", [P, KD, S], F16) for i in range(2)]
        x_a = sb("x_a", [P, T, D])
        bn6_a, mv_a, ve_a, rstd_a = sb("bn6_a", [P, T, 6]), sb("mv_a", [P, 4, T]), sb("ve_a", [P, T]), sb("rstd_a", [P, T])

        misc = ctx.enter_context(nc.psum_tensor("misc", [P, 2, 512], F32))
        sc = ctx.enter_context(nc.psum_tensor("sc", [P, 2, 512], F32))
        st = ctx.enter_context(nc.psum_tensor("st", [P, 2, 512], F32))
        pv = ctx.enter_context(nc.psum_tensor("pv", [P, 2, 512], F32))

        wq_raw = q_r[:].rearrange("p t d -> p (t d)")[:, 0:KD * D].rearrange("p (k d) -> p k d", k=KD)
        wp_raw = q_r[:].rearrange("p t d -> p (t d)")[:, KD * D:2 * KD * D].rearrange("p (k d) -> p k d", k=KD)
        wkv_raw = k_r[:].rearrange("p t d -> p (t d)").rearrange("p (k d) -> p k d", k=KD)
        qa, qb = q_r, q_s
        w8a = ctx_s[:].rearrange("p t d -> p (t d)")[:, 0:KD * D]
        w8b = ctx_s[:].rearrange("p t d -> p (t d)")[:, KD * D:2 * KD * D]

        const_in = sem("const_in")
        const_ok = sem("const_ok")
        w8_step = sem("w8_step")
        w16_hi = sem("w16_hi")
        w16_lo = sem("w16_lo")
        zeros_ok = sem("zeros_ok")
        x_in, ctx_in = sem("x_in"), sem("ctx_in")
        ln_bn, ln_mv, ln_ve, ln_rs, ln_out = (sem(f"ln_{n}") for n in ("bn", "mv", "ve", "rs", "out"))
        rot_q = sem("rot_q")
        rot_k = sem("rot_k")
        v0_hi, v0_lo = sem("v0_hi"), sem("v0_lo")
        tr0, t0_hi, t0_lo = sem("tr0"), sem("t0_hi"), sem("t0_lo")
        st0_out = [sem(f"st0_out{i}") for i in range(2)]
        st0_in = sem("st0_in")
        upd = sem("upd")
        state_ok = sem("state_ok")
        state_hi, state_lo = sem("state_hi"), sem("state_lo")
        r_sc, r_mask, r_hi, r_lo = (sem(f"r_{n}") for n in ("sc", "mask", "hi", "lo"))
        r_out, r_add = sem("r_out"), sem("r_add")
        quant = sem("quant")
        xq_tr, xq_cp = sem("xq_tr"), sem("xq_cp")
        ffn_mm, ffn_y, ffn_b, ffn_x = (sem(f"ffn_{n}") for n in ("mm", "y", "b", "x"))
        tr3, t3_hi, t3_lo = sem("tr3"), sem("t3_hi"), sem("t3_lo")
        c3_hi, c3_lo = sem("c3_hi"), sem("c3_lo")
        qk_mm, qk_hi, qk_lo = sem("qk_mm"), sem("qk_hi"), sem("qk_lo")
        v_mm, v_hi, v_lo = sem("v_mm"), sem("v_hi"), sem("v_lo")
        st1_out = [sem(f"st1_out{i}") for i in range(2)]
        rows_in = sem("rows_in")
        st1_in = [sem(f"st1_in{i}") for i in range(2)]
        m_sc, m_max = sem("m_sc"), sem("m_max")
        m_16 = sem("m_16")
        m_tr, m_cp = sem("m_tr"), sem("m_cp")
        m_out = sem("m_out")
        m_in = [sem(f"m_in{i}") for i in range(2)]
        v_cp = sem("v_cp")
        x_mid = sem("x_mid")
        x_back = sem("x_back")
        s_mm, s_exp = sem("s_mm"), sem("s_exp")
        p_hi, p_lo = sem("p_hi"), sem("p_lo")
        pv_mm = sem("pv_mm")
        o_rec, o_mul = sem("o_rec"), sem("o_mul")
        o_tr, o_hi, o_lo = sem("o_tr"), sem("o_hi"), sem("o_lo")
        x_bias = sem("x_bias")
        pr_mm, pr_x = sem("pr_mm"), sem("pr_x")
        la_bn, la_mv, la_ve, la_rs, la_out = (sem(f"la_{n}") for n in ("bn", "mv", "ve", "rs", "out"))
        tr4, t4_hi, t4_lo = sem("tr4"), sem("t4_hi"), sem("t4_lo")
        x_out = sem("x_out")

        flat = lambda ap: ap.rearrange("p t d -> p (t d)")
        LAST = B - 1
        SLOTS = 2 * H

        def prep_plan(b):
            yield 0.0, ("stats", b, 0)
            yield 0.1, ("rotate_k", b, 0)
            yield 0.6, ("normalise", b, 0)
            yield 0.7, ("split_ctx", b, 0)
            yield 1.1, ("rotate", b, 0)
            for (half, w), turn, low in (((0, 0), 1.9, 2.4), ((0, 1), 2.1, 2.6), ((1, 0), 3.2, 3.6), ((1, 1), 3.3, 3.7)):
                yield turn, ("turn0", b, (half, w))
                yield low, ("turn0_low", b, (half, w))
            for half, time in ((0, 3.9), (1, 8.0)):
                yield time, ("state", b, half)
                yield time + 0.55, ("state_sum", b, half)
                yield time + 1.0, ("state_low", b, half)
            for n, time in enumerate((4.45, 8.3, 17.0, 17.1)):
                yield time, ("qk", b, n)
                yield time + 0.5, ("qk_low", b, n)
            for half, first in enumerate((4.5, 8.0)):
                for c in range(T):
                    time = first + 0.75 * c
                    yield time, ("r_scores", b, (half, c))
                    yield time + 1.0, ("r_outs", b, (half, c))
                    yield time + 1.5, ("r_add", b, (half, c))
            yield 7.0, ("stack0", b, 1)
            for u, time in enumerate((9.4, 10.9)):
                yield time, ("v", b, u)
                yield time + 0.5, ("v_low", b, u)
            yield 11.8, ("stats", b, 1)
            yield 12.3, ("normalise", b, 1)
            for i in range(3):
                yield 12.6 + i / 2, ("quantise", b, i)
            yield 14.0, ("turn_q", b, 0)
            yield 14.6, ("copy_q", b, 0)
            yield 14.7, ("linear", b, 0)
            yield 15.3, ("linear_add", b, 0)
            yield 15.6, ("stats", b, 2)
            yield 16.1, ("normalise", b, 2)
            for k in range(KD):
                yield 16.3 + k / 10, ("turn3", b, k)
                yield 16.8 + k / 10, ("turn3_low", b, k)
            yield 17.9, ("stack1", b, 0)
            yield 17.9, ("next_inputs", b, 0)

        def maxima_plan(b, half, first, last, rows):
            n = 2 * HH
            for i in range(n):
                yield first + i * (last - first) / n, ("maxima", b, (half, i // 2, i % 2))
            yield rows, ("max_split", b, half)
            yield rows + 0.3, ("max_turn", b, half)
            yield rows + 0.8, ("max_copy", b, half)

        def out_plan(b):
            yield 0.0, ("x_back", b, 0)
            yield 1.8, ("x_bias", b, 0)
            yield 2.0, ("divide", b, 3)
            for k in range(KD):
                yield 2.65 + k / 20, ("o_turn", b, k)
                yield 3.1 + k / 20, ("o_low", b, k)
            for u, time in enumerate((3.8, 4.35)):
                yield time, ("o_proj", b, u)
                yield time + 0.5, ("o_add", b, u)
            yield 4.9, ("stats_a", b, 0)
            yield 5.4, ("normalise_a", b, 0)
            for k, time in enumerate((5.9, 6.5)):
                yield time, ("turn4", b, k)
                yield time + 0.45, ("turn4_low", b, k)
            yield 7.5, ("out_store", b, 0)

        def in_order(*plans):
            yield from (step for _, step in sorted((s for plan in plans for s in plan), key=lambda s: s[0]))

        MAX1, MAX0 = (1.3, 12.5, 12.6), (19.0, 28.2, 28.5)

        def batch_steps(b, before, more):
            def attention():
                yield -0.3, ("stack1", b, 1)
                yield -0.2, ("banks", b, 0)
                for slot in range(SLOTS):
                    h, g = slot // 2, slot % 2
                    yield slot - 0.1, ("score", b, (h, g))
                    if h:
                        yield slot + 0.5, ("values", b, (h - 1, g))
                    elif before:
                        yield slot + 0.5, ("values", b - 1, (H - 1, g))
                yield 1.7, ("take_v", b, 0)
                for g in range(3):
                    yield 8 * g + 10.0, ("divide", b, g)
            plans = [attention(), maxima_plan(b, 1, *MAX1)]
            if more:
                plans += [prep_plan(b + 1), maxima_plan(b + 1, 0, *MAX0)]
            if before:
                plans.append(out_plan(b - 1))
            return in_order(*plans)

        def end_steps(b):
            for g in range(2):
                yield "values", b, (H - 1, g)
            yield from in_order(out_plan(b))

        def start_steps():
            return in_order(prep_plan(0), maxima_plan(0, 0, *MAX0))

        BANKS = {"turn0": ("misc", 1), "state": ("misc", 1), "r_outs": ("misc", 1), "turn_q": ("misc", 2),
                 "linear": ("misc", 2), "turn3": ("misc", 1), "qk": ("misc", 1), "v": ("misc", 1),
                 "o_turn": ("misc", 1), "o_proj": ("misc", 1), "turn4": ("misc", 1),
                 "r_scores": ("sc", 2), "maxima": ("sc", 2), "max_turn": ("sc", 1)}
        bank_no = {}

        def bank(name, arg, i=0):
            pair, n = bank_no[name, arg]
            return (misc if pair == "misc" else sc)[:, (n + i) % 2, :]

        def run(steps, engine, loop=True):
            used = {"misc": 0, "sc": 0}

            def emit(order):
                for name, b, arg in order:
                    if name in BANKS:
                        pair, n = BANKS[name]
                        bank_no[name, arg] = (pair, used[pair])
                        used[pair] += n
                    if name in steps:
                        steps[name](b, arg)
            emit(start_steps())
            emit(batch_steps(0, False, True))
            if loop:
                with engine.Fori(1, LAST) as i:
                    emit(batch_steps(i, True, True))
            else:
                for i in range(1, LAST):
                    emit(batch_steps(i, True, True))
            emit(batch_steps(LAST, True, False))
            emit(end_steps(LAST))

        block = ctx.enter_context(nc.Block())

        @block.sync
        def _(sp):
            n_const = [0]

            def const(dst, src):
                sp.dma_start(dst, src).then_inc(const_in, 16)
                n_const[0] += 1

            def load_x(b):
                sp.dma_start(x_p[:], t["x"].rearrange("(b t p) d -> b p t d", b=B, t=T)[b]).then_inc(x_in, 16)

            def load_ctx(b):
                for dst, name in ((ctx_n, "ctx"), (ctx_s, "ctx_swapped")):
                    sp.dma_start(dst[:], t[name].rearrange("(b t p) d -> b p t d", b=B, t=T)[b]).then_inc(ctx_in, 16)
                sp.dma_start(ctx_t[:], t["ctx_t"].rearrange("(k p) (b n) -> b p k n", k=KD, b=B)[b]).then_inc(ctx_in, 16)

            load_x(0)
            const(ident[:], t["ident"])
            const(w8_raw[:], t["L0_ffn_kernel"].rearrange("(k p) d -> p k d", k=KD))
            const(s_in[:], t["L0_ffn_input_scale"][None, :].to_broadcast([P, 1]))
            const(s_k[:], t["L0_ffn_kernel_scale"][None, :].to_broadcast([P, 1]))
            const(wq_raw, t["wq_t"].rearrange("(k p) d -> p k d", k=KD))
            const(wp_raw, t["wp_t"].rearrange("(k p) d -> p k d", k=KD))
            const(wkv_raw, t["wkv_t"].rearrange("(k p) d -> p k d", k=KD))
            const(q_cos[:], t["q_cos"])
            const(q_sin[:], t["q_sin"])
            const(k_cos[:], t["k_cos"])
            const(k_sin[:], t["k_sin"])
            const(causal[:], t["causal"])
            const(chunk_decay[:], t["chunk_decay"])
            const(bias0[:], t["L0_ffn_bias"][None, :].to_broadcast([P, D]))
            const(biasp[:], t["L1_xattn_bproj"][None, :].to_broadcast([P, D]))
            assert n_const[0] == N_CONST
            sp.wait_ge(zeros_ok, 4)
            for i in range(2):
                sp.dma_start(kz1[i][KR:MR].rearrange("p a b n -> p (a b n)"), t["max_rows"][:, i]).then_inc(rows_in, 16)
            sp.wait_ge(w8_step, W8_STEPS)
            load_ctx(0)

            def to_stack():
                return [(w, par, j, (0, 0, 1)[j] if w == 0 else (0, 1, 0)[j])
                        for w in range(2) for par in range(2) for j in range(3)]

            def part(stack, w, hl, half, par):
                return stack[w, hl].rearrange("(f q r d) n -> f r d q n", f=2, q=HP, r=2)[half, par]

            def turn0_low(b, arg):
                half, w = arg
                if (half, w) == (0, 0):
                    need(sp, st0_in, b * 2 * 12 * 16)
                sp.wait_ge(t0_lo, b * 4 + 2 * half + w + 1)
                for hl in range(2):
                    sp.dma_start(stack0_d[w, hl].rearrange("(f p) n -> f p n", f=2)[half],
                                 t0[w][hl][:, half, :]).then_inc(st0_out[half], 16)
                if (half, w) == (0, 1):
                    stack0(b, 0)

            def stack0(b, half):
                sp.wait_ge(st0_out[half], (b + 1) * 4 * 16)
                need(sp, r_sc, b * 16 + half * 8)
                for w, par, j, hl in to_stack():
                    row = par * SR + j * HD
                    dst = (sq0 if w == 0 else kz0[par])[row:row + HD]
                    sp.dma_start(dst, part(stack0_d, w, hl, half, par)).then_inc(st0_in, 16)

            def qk_low(b, n):
                if n == 0:
                    for half in range(2):
                        need(sp, st1_in[half], b * 12 * 16)
                w, half = 1 - n // 2, n % 2
                sp.wait_ge(qk_lo, b * 4 + n + 1)
                for hl in range(2):
                    sp.dma_start(stack1_d[w, hl].rearrange("(f p) n -> f p n", f=2)[half],
                                 t1[hl][:, half, :]).then_inc(st1_out[half], 16)

            def stack1(b, half):
                sp.wait_ge(st1_out[half], (b + 1) * 4 * 16)
                need(sp, s_mm, b * 64 - 32 + half * 32)
                for w, par, j, hl in to_stack():
                    row = par * SR + j * HD
                    dst = (sq1 if w == 0 else kz1[par])[row:row + HD, half]
                    sp.dma_start(dst, part(stack1_d, w, hl, half, par)).then_inc(st1_in[half], 16)

            def max_copy(b, half):
                sp.wait_ge(m_cp, b * 2 + half + 1)
                need(sp, m_in[half], b * 16)
                sp.dma_start(max_d[half], max_t[:]).then_inc(m_out, 16)
                sp.wait_ge(m_out, (b * 2 + half + 1) * 16)
                need(sp, s_mm, b * 64 - 32 + half * 32)
                sp.dma_start(sq1[KR:MR, half], max_d[half].rearrange("(r q) n -> r q n", r=4)).then_inc(m_in[half], 16)

            def next_inputs(b, _):
                sp.wait_ge(ffn_x, (b + 1) * 2)
                sp.dma_start(x_d.rearrange("(b t) p d -> b p t d", b=B)[b], x_p[:]).then_inc(x_mid, 16)
                if b < LAST:
                    sp.wait_ge(v0_lo, b + 1)
                    sp.wait_ge(rot_k, (b + 1) * 2)
                    sp.wait_ge(c3_lo, b + 1)
                    sp.wait_ge(upd, (b + 1) * 2)
                    load_ctx(b + 1)
                    sp.wait_ge(ln_out, (b + 1) * 3)
                    sp.wait_ge(x_mid, (b + 1) * 16)
                    load_x(b + 1)

            def x_back_(b, _):
                sp.wait_ge(x_mid, (b + 1) * 16)
                need(sp, x_out, b * 3 * 16)
                sp.dma_start(x_a[:], x_d.rearrange("(b t) p d -> b p t d", b=B)[b]).then_inc(x_back, 16)

            def out_store(b, _):
                sp.wait_ge(pr_x, (b + 1) * 2)
                sp.dma_start(x_d.rearrange("(b t) p d -> b p t d", b=B)[b], x_a[:]).then_inc(x_out, 16)
                sp.wait_ge(t4_lo, (b + 1) * 2)
                for hl in range(2):
                    sp.dma_start(xt_d[hl][b], o_t[hl][:]).then_inc(x_out, 16)

            run({"turn0_low": turn0_low, "stack0": stack0, "qk_low": qk_low, "stack1": stack1, "max_copy": max_copy,
                 "next_inputs": next_inputs, "x_back": x_back_, "out_store": out_store}, sp, loop=False)
            sp.wait_ge(x_out, B * 3 * 16)

        @block.gpsimd
        def _(pool):
            pool.memset(half_power[:], -0.5).then_inc(const_ok, 1)
            for buf in (kz0[0], kz0[1], kz1[0], kz1[1]):
                pool.memset(buf[:], 0.0).then_inc(zeros_ok, 1)
            pool.wait_ge(const_in, N_CONST * 16)
            pool.wait_ge(const_ok, CONSTS)

            def root(ve_t, rs_t, s_ve, s_rs, n):
                pool.wait_ge(s_ve, n)
                pool.tensor_tensor(rs_t[:], ve_t[:], half_power[:], ALU.pow).then_inc(s_rs, 1)

            def stats(b, j):
                root(ve, rstd, ln_ve, ln_rs, b * 3 + j + 1)

            def rotate_k(b, _):
                pool.wait_ge(ctx_in, (b + 1) * 48)
                need(pool, tr0, b * 4)
                need(pool, upd, b * 2)
                pool.tensor_tensor(k_r[:], ctx_n[:], k_cos[:], ALU.mult)
                pool.tensor_tensor(ctx_s[:], ctx_s[:], k_sin[:], ALU.mult).then_inc(rot_k, 1)
                pool.wait_ge(rot_k, b * 2 + 1)
                pool.tensor_tensor(k_r[:], k_r[:], ctx_s[:], ALU.add).then_inc(rot_k, 1)

            def split_ctx(b, _):
                pool.wait_ge(v0_hi, b + 1)
                pool.tensor_tensor(v0[1][:], ctx_n[:], v0[0][:], ALU.subtract).then_inc(v0_lo, 1)
                pool.wait_ge(c3_hi, b + 1)
                pool.tensor_tensor(c3[1][:], ctx_t[:], c3[0][:], ALU.subtract).then_inc(c3_lo, 1)

            def r_scores(b, arg):
                half, c = arg
                for g in range(2):
                    n = half * 8 + c * 2 + g
                    pool.wait_ge(r_hi, b * 16 + n + 1)
                    pool.tensor_tensor(rs[1][:, c % 2, 4 * g:4 * g + 4, :], rm[:, n % 2],
                                       rs[0][:, c % 2, 4 * g:4 * g + 4, :], ALU.subtract).then_inc(r_lo, 1)

            def score(b, arg):
                h, g = arg
                pool.wait_ge(p_hi, b * 32 + 2 * h + g + 1)
                pool.tensor_tensor(pl[:, h % 2, 2 * g:2 * g + 2, :], p32[:, g], ph[:, h % 2, 2 * g:2 * g + 2, :],
                                   ALU.subtract).then_inc(p_lo, 1)

            def stats_a(b, _):
                root(ve_a, rstd_a, la_ve, la_rs, b + 1)

            run({"stats": stats, "rotate_k": rotate_k, "split_ctx": split_ctx, "r_scores": r_scores, "score": score,
                 "stats_a": stats_a}, pool)

        @block.scalar
        def _(act):
            act.wait_ge(const_in, N_CONST * 16)
            for hl, w_raw in ((wq, wq_raw), (wkv, wkv_raw), (wp, wp_raw)):
                act.activation(hl[0][:], w_raw, ACT.Copy, scale=WS).then_inc(w16_hi, 1)

            def split_ctx(b, _):
                act.wait_ge(ctx_in, (b + 1) * 48)
                need(act, r_out, b * 8)
                act.activation(v0[0][:], ctx_n[:], ACT.Copy).then_inc(v0_hi, 1)
                need(act, v_mm, b * 2)
                act.activation(c3[0][:], ctx_t[:], ACT.Copy).then_inc(c3_hi, 1)

            def turn0(b, arg):
                half, w = arg
                if half == 0:
                    need(act, st0_out[0], b * 4 * 16)
                    need(act, st0_out[1], b * 4 * 16)
                    need(act, r_out, b * 8)
                act.wait_ge(tr0, b * 4 + 2 * half + w + 1)
                act.activation(t0[w][0][:, half, :], bank("turn0", arg), ACT.Copy).then_inc(t0_hi, 1)

            def state_low(b, half):
                act.wait_ge(state_ok, (b * 2 + half + 1) * 5)
                need(act, r_out, b * 8 + half * 4)
                act.activation(state_s[0][:], state[:], ACT.Copy).then_inc(state_hi, 1)

            def r_scores(b, arg):
                half, c = arg
                for g in range(2):
                    n = half * 8 + c * 2 + g
                    act.wait_ge(r_mask, b * 16 + n + 1)
                    need(act, r_out, b * 8 + half * 4 + c - 1)
                    act.activation(rs[0][:, c % 2, 4 * g:4 * g + 4, :], rm[:, n % 2], ACT.Copy).then_inc(r_hi, 1)

            def turn3(b, k):
                act.wait_ge(tr3, b * 2 + k + 1)
                need(act, qk_mm, b * 4)
                act.activation(x3[0][:, k, :], bank("turn3", k), ACT.Copy).then_inc(t3_hi, 1)

            def qk(b, n):
                act.wait_ge(qk_mm, b * 4 + n + 1)
                need(act, st1_out[n % 2], (b * 4 + 2 * (n // 2)) * 16)
                act.activation(t1[0][:, n % 2, :], bank("qk", n), ACT.Copy, scale=1 / WS).then_inc(qk_hi, 1)

            def v(b, u):
                act.wait_ge(v_mm, b * 2 + u + 1)
                need(act, v_cp, b * 2)
                act.activation(v_next[0][:, 2 * u:2 * u + 2, :, 0:HD],
                               bank("v", u).rearrange("p (t h d) -> p t h d", t=2, h=H),
                               ACT.Copy, scale=1 / WS).then_inc(v_hi, 1)

            def score(b, arg):
                h, g = arg
                for kt in range(2 * g, 2 * g + 2):
                    act.wait_ge(s_mm, b * 64 + h * 4 + kt + 1)
                    if kt % 2 == 0:
                        need(act, p_lo, b * 32 + 2 * h + g - 1)
                    act.activation(p32[:, g, kt % 2, :], st[:, kt % 2, :], ACT.Exp, scale=QSCALE).then_inc(s_exp, 1)
                act.wait_ge(s_exp, b * 64 + h * 4 + 2 * g + 2)
                need(act, pv_mm, b * 16 + h - 1)
                act.activation(ph[:, h % 2, 2 * g:2 * g + 2, :], p32[:, g], ACT.Copy).then_inc(p_hi, 1)

            def o_turn(b, k):
                act.wait_ge(x_back, (b + 1) * 16)
                act.wait_ge(o_tr, b * 2 + k + 1)
                act.activation(o_t[0][:, k, :], bank("o_turn", k), ACT.Copy).then_inc(o_hi, 1)

            def turn4(b, k):
                act.wait_ge(tr4, b * 2 + k + 1)
                act.wait_ge(pr_mm, (b + 1) * 2)
                act.activation(o_t[0][:, k, :], bank("turn4", k), ACT.Copy).then_inc(t4_hi, 1)

            run({"split_ctx": split_ctx, "turn0": turn0, "state_low": state_low, "r_scores": r_scores,
                 "turn3": turn3, "qk": qk, "v": v, "score": score, "o_turn": o_turn, "turn4": turn4}, act)

        @block.vector
        def _(dve):
            def steps(sem_):
                count = [0]

                def done(ins):
                    count[0] += 1
                    ins.then_inc(sem_, 1)
                    dve.wait_ge(sem_, count[0])
                return done, count

            def to_e4m3(v, m, dst, done):
                done(dve.tensor_scalar(m.bitcast(I32), v.bitcast(I32), 0x7F800000, None, ALU.bitwise_and))
                done(dve.tensor_scalar(m, m, 2.0 ** -6, 1.5 * 2.0 ** 20, ALU.max, ALU.mult))
                done(dve.tensor_tensor(v, v, m, ALU.add))
                done(dve.tensor_tensor(v, v, m, ALU.subtract))
                done(dve.tensor_scalar(m, v, 1.1 * 2.0 ** 119, 0.0, ALU.mult, ALU.mult))
                return dve.tensor_tensor(dst, v, m, ALU.add)

            dve.wait_ge(const_in, N_CONST * 16)
            dve.tensor_copy(ident16[:], ident[:]).then_inc(const_ok, 1)
            dve.tensor_copy(ident_bf[:], ident[:]).then_inc(const_ok, 1)
            dve.memset(v_next[0][:, :, :, HD:HD + 1], 1.0).then_inc(const_ok, 1)
            dve.memset(v_next[1][:, :, :, HD:HD + 1], 0.0).then_inc(const_ok, 1)
            done, count = steps(w8_step)
            dve.reciprocal(r_in[:], s_in[:])
            dve.tensor_tensor(s_both[:], s_in[:], s_k[:], ALU.mult)
            done(dve.reciprocal(r_k[:], s_k[:]))
            done(dve.tensor_scalar(w8a, w8_raw[:].rearrange("p k d -> p (k d)"), r_k[:, 0:1], None, ALU.mult))
            done(to_e4m3(w8a, w8b, w8[:].rearrange("p k d -> p (k d)"), done))
            assert count[0] == W8_STEPS
            for n, (hl, w_raw) in enumerate(((wq, wq_raw), (wkv, wkv_raw), (wp, wp_raw))):
                dve.wait_ge(w16_hi, n + 1)
                dve.scalar_tensor_tensor(hl[1][:], w_raw, WS, hl[0][:], ALU.mult, ALU.subtract).then_inc(w16_lo, 1)
            dve.wait_ge(w16_lo, 3)

            def variance(x, bn6_, mv_, ve_, s_bn, s_mv, s_ve, n):
                for i in range(T):
                    ins = dve.bn_stats(bn6_[:, i, :], x[:, i, :])
                ins.then_inc(s_bn, 1)
                dve.wait_ge(s_bn, n)
                mean, diff, dev, sq = (mv_[:, i, :] for i in range(4))
                k = (n - 1) * 3
                dve.tensor_tensor(mean, bn6_[:, :, 1], bn6_[:, :, 4], ALU.add)
                dve.tensor_tensor(diff, bn6_[:, :, 1], bn6_[:, :, 4], ALU.subtract)
                dve.tensor_tensor(dev, bn6_[:, :, 2], bn6_[:, :, 5], ALU.add).then_inc(s_mv, 1)
                dve.wait_ge(s_mv, k + 1)
                dve.tensor_tensor(sq, diff, diff, ALU.mult)
                dve.tensor_scalar(mean, mean, 0.5, None, ALU.mult).then_inc(s_mv, 1)
                dve.wait_ge(s_mv, k + 2)
                dve.scalar_tensor_tensor(dev, sq, D / 4.0, dev, ALU.mult, ALU.add).then_inc(s_mv, 1)
                dve.wait_ge(s_mv, k + 3)
                dve.tensor_scalar(ve_[:], dev, 1.0 / D, EPS, ALU.mult, ALU.add).then_inc(s_ve, 1)

            def centre(x, dst, mv_, rs_, s_rs, s_out, n):
                dve.wait_ge(s_rs, n)
                for i in range(T):
                    ins = dve.tensor_scalar(dst[:, i, :], x[:, i, :], mv_[:, 0, i:i + 1], rs_[:, i:i + 1],
                                            ALU.subtract, ALU.mult)
                ins.then_inc(s_out, 1)

            def stats(b, j):
                if j == 0:
                    dve.wait_ge(x_in, (b + 1) * 16)
                    need(dve, ln_out, b * 3)
                if j == 1:
                    dve.wait_ge(r_add, (b + 1) * 8)
                if j == 2:
                    dve.wait_ge(ffn_x, (b + 1) * 2)
                variance(x_p, bn6, mv, ve, ln_bn, ln_mv, ln_ve, b * 3 + j + 1)

            def normalise(b, j):
                if j == 0:
                    need(dve, tr3, b * 2)
                if j == 2:
                    dve.wait_ge(rot_q, (b + 1) * 2)
                    need(dve, tr4, (b - 1) * 2)
                centre(x_p, x_b if j == 1 else x_n, mv, rstd, ln_rs, ln_out, b * 3 + j + 1)

            def rotate(b, _):
                dve.wait_ge(ln_out, b * 3 + 1)
                need(dve, tr0, b * 4)
                need(dve, quant, b * QUANT_STEPS)
                two = lambda a: a[:].rearrange("p t (i two) -> p (t i) two", two=2)
                dve.tensor_tensor(q_r[:], x_n[:], q_cos[:], ALU.mult)
                for i in range(2):
                    ins = dve.tensor_tensor(two(q_s)[:, :, i], two(x_n)[:, :, 1 - i], two(q_sin)[:, :, i], ALU.mult)
                ins.then_inc(rot_q, 1)
                dve.wait_ge(rot_q, b * 2 + 1)
                dve.tensor_tensor(q_r[:], q_r[:], q_s[:], ALU.add).then_inc(rot_q, 1)

            def turn0_low(b, arg):
                half, w = arg
                dve.wait_ge(t0_hi, b * 4 + 2 * half + w + 1)
                dve.tensor_tensor(t0[w][1][:, half, :], bank("turn0", arg), t0[w][0][:, half, :],
                                  ALU.subtract).then_inc(t0_lo, 1)

            def state_sum(b, half):
                n = (b * 2 + half) * 5
                dve.wait_ge(upd, b * 2 + half + 1)
                need(dve, state_hi, b * 2 + half)
                need(dve, state_lo, b * 2 + half)
                u = bank("state", half).rearrange("p (c n) -> p c n", c=T)
                dve.tensor_tensor(state[:, 0], u[:, 0], chunk_decay[:, half], ALU.mult).then_inc(state_ok, 1)
                for c in range(1, T - 1):
                    dve.wait_ge(state_ok, n + 2 * c - 1)
                    dve.tensor_tensor(state[:, c], u[:, c], state[:, c - 1], ALU.add).then_inc(state_ok, 1)
                    dve.wait_ge(state_ok, n + 2 * c)
                    dve.tensor_tensor(state[:, c], state[:, c], chunk_decay[:, half], ALU.mult).then_inc(state_ok, 1)

            def state_low(b, half):
                dve.wait_ge(state_hi, b * 2 + half + 1)
                dve.tensor_tensor(state_s[1][:], state[:], state_s[0][:], ALU.subtract).then_inc(state_lo, 1)

            def r_scores(b, arg):
                half, c = arg
                for g in range(2):
                    n = half * 8 + c * 2 + g
                    dve.wait_ge(r_sc, b * 16 + n + 1)
                    need(dve, r_hi, b * 16 + n - 1)
                    need(dve, r_lo, b * 16 + n - 1)
                    dve.tensor_tensor(rm[:, n % 2], bank("r_scores", arg, g).rearrange("p (h n) -> p h n", h=4),
                                      causal[:, None, :].to_broadcast([P, 4, P]), ALU.mult).then_inc(r_mask, 1)

            def r_add_(b, arg):
                half, c = arg
                dve.wait_ge(r_out, b * 8 + half * 4 + c + 1)
                xs = x_p[:, c, half * P:(half + 1) * P]
                dve.tensor_tensor(xs, bank("r_outs", arg)[:, 0:P], xs, ALU.add).then_inc(r_add, 1)

            def quantise(b, i):
                count = [(0, 3, 5)[i]]

                def done(ins):
                    count[0] += 1
                    ins.then_inc(quant, 1)
                    dve.wait_ge(quant, b * QUANT_STEPS + count[0])
                v, m = flat(qa[:]), flat(qb[:])
                if i == 0:
                    dve.wait_ge(ln_out, b * 3 + 2)
                    dve.wait_ge(tr0, (b + 1) * 4)
                    done(dve.tensor_scalar(v, flat(x_b[:]), r_in[:, 0:1], None, ALU.mult))
                    done(dve.tensor_scalar(m.bitcast(I32), v.bitcast(I32), 0x7F800000, None, ALU.bitwise_and))
                    done(dve.tensor_scalar(m, m, 2.0 ** -6, 1.5 * 2.0 ** 20, ALU.max, ALU.mult))
                if i == 1:
                    done(dve.tensor_tensor(v, v, m, ALU.add))
                    done(dve.tensor_tensor(v, v, m, ALU.subtract))
                if i == 2:
                    done(dve.tensor_scalar(m, v, 1.1 * 2.0 ** 119, 0.0, ALU.mult, ALU.mult))
                    need(dve, xq_tr, b * 2)
                    done(dve.tensor_tensor(flat(x_q[:]), v, m, ALU.add))
                    assert count[0] == QUANT_STEPS

            def copy_q(b, _):
                for k in range(KD):
                    dve.wait_ge(xq_tr, b * 2 + k + 1)
                    need(dve, ffn_mm, b * 2)
                    dve.tensor_copy(xq_t[:, k, :], bank("turn_q", 0, k)[:, 0:256].bitcast(BF16)).then_inc(xq_cp, 1)

            def linear_add(b, _):
                for u in range(2):
                    n = b * 2 + u + 1
                    dve.wait_ge(ffn_mm, n)
                    need(dve, ffn_b, n - 1)
                    dve.tensor_scalar(y_a[:].rearrange("p t d -> p (t d)"), bank("linear", 0, u),
                                      s_both[:, 0:1], None, ALU.mult).then_inc(ffn_y, 1)
                    dve.wait_ge(ffn_y, n)
                    need(dve, ffn_x, n - 1)
                    dve.tensor_tensor(y_b[:], y_a[:], bias0[:, None, :].to_broadcast([P, 2, D]),
                                      ALU.add).then_inc(ffn_b, 1)
                    dve.wait_ge(ffn_b, n)
                    xs = x_p[:, 2 * u:2 * u + 2, :]
                    dve.tensor_tensor(xs, xs, y_b[:], ALU.add).then_inc(ffn_x, 1)

            def turn3_low(b, k):
                dve.wait_ge(t3_hi, b * 2 + k + 1)
                dve.tensor_tensor(x3[1][:, k, :], bank("turn3", k), x3[0][:, k, :], ALU.subtract).then_inc(t3_lo, 1)

            def qk_low(b, n):
                dve.wait_ge(qk_hi, b * 4 + n + 1)
                dve.scalar_tensor_tensor(t1[1][:, n % 2, :], bank("qk", n), 1 / WS, t1[0][:, n % 2, :],
                                         ALU.mult, ALU.subtract).then_inc(qk_lo, 1)

            def v_low(b, u):
                dve.wait_ge(v_hi, b * 2 + u + 1)
                view = lambda a: a[:, 2 * u:2 * u + 2, :, 0:HD].rearrange("p t h d -> p (t h) d")
                dve.scalar_tensor_tensor(view(v_next[1]), bank("v", u).rearrange("p (a d) -> p a d", d=HD), 1 / WS,
                                         view(v_next[0]), ALU.mult, ALU.subtract).then_inc(v_lo, 1)

            def maxima(b, arg):
                half, h, g = arg
                for i in range(2):
                    qt = 2 * g + i
                    dve.wait_ge(m_sc, b * 64 + half * 32 + h * T + qt + 1)
                    if h == 0 and qt == 0:
                        need(dve, m_16, b * 4 + half * 2)
                    dve.tensor_reduce(neg_max[:, qt, h % 2, h // 2:h // 2 + 1], bank("maxima", arg, i), AX.X,
                                      ALU.max, negate=True).then_inc(m_max, 1)

            def max_split(b, half):
                dve.wait_ge(m_max, b * 64 + half * 32 + 32)
                need(dve, m_tr, b * 2 + half)
                dve.tensor_copy(max16[:, :, :, 0, :], neg_max[:]).then_inc(m_16, 1)
                dve.wait_ge(m_16, b * 4 + half * 2 + 1)
                dve.tensor_tensor(max16[:, :, :, 1, :], neg_max[:], max16[:, :, :, 0, :],
                                  ALU.subtract).then_inc(m_16, 1)

            def max_copy(b, half):
                dve.wait_ge(m_tr, b * 2 + half + 1)
                need(dve, m_out, (b * 2 + half) * 16)
                dve.tensor_copy(max_t[:], bank("max_turn", half)[0:4 * HP, 0:256].bitcast(F16)).then_inc(m_cp, 1)

            def take_v(b, _):
                need(dve, pv_mm, b * 16)
                dve.wait_ge(v_lo, (b + 1) * 2)
                for hl in range(2):
                    dve.tensor_copy(v_cur[hl][:], v_next[hl][:]).then_inc(v_cp, 1)

            def divide(b, g):
                dve.wait_ge(pv_mm, b * 16 + 4 * g + 4)
                need(dve, o_mul, b * 4 + g)
                o = pv[:, g % 2, 0:4 * T * (HD + 1)].rearrange("p (h q d) -> p h q d", h=4, q=T)
                dve.reciprocal(rden[:], o[:, :, :, HD]).then_inc(o_rec, 1)
                if g == 0:
                    need(dve, o_tr, b * 2)
                dve.wait_ge(o_rec, b * 4 + g + 1)
                dst = o_n[:].rearrange("p q (g h d) -> p g h q d", g=4, h=4)[:, g]
                dve.tensor_tensor(dst, o[:, :, :, 0:HD], rden[:, :, :, None].to_broadcast([P, 4, T, HD]),
                                  ALU.mult).then_inc(o_mul, 1)

            def x_bias_(b, _):
                dve.wait_ge(x_back, (b + 1) * 16)
                dve.tensor_tensor(x_a[:], x_a[:], biasp[:, None, :].to_broadcast([P, T, D]), ALU.add).then_inc(x_bias, 1)

            def o_low(b, k):
                dve.wait_ge(o_hi, b * 2 + k + 1)
                dve.tensor_tensor(o_t[1][:, k, :], bank("o_turn", k), o_t[0][:, k, :], ALU.subtract).then_inc(o_lo, 1)

            def o_add(b, u):
                dve.wait_ge(x_bias, b + 1)
                dve.wait_ge(pr_mm, b * 2 + u + 1)
                xs = x_a[:, 2 * u:2 * u + 2, :].rearrange("p t d -> p (t d)")
                dve.scalar_tensor_tensor(xs, bank("o_proj", u), 1 / WS, xs, ALU.mult, ALU.add).then_inc(pr_x, 1)

            def stats_a(b, _):
                dve.wait_ge(pr_x, (b + 1) * 2)
                variance(x_a, bn6_a, mv_a, ve_a, la_bn, la_mv, la_ve, b + 1)

            def normalise_a(b, _):
                if not (isinstance(b, int) and b + 2 > LAST):
                    dve.wait_ge(rot_q, (b + 3) * 2)
                centre(x_a, x_n, mv_a, rstd_a, la_rs, la_out, b + 1)

            def turn4_low(b, k):
                dve.wait_ge(t4_hi, b * 2 + k + 1)
                dve.tensor_tensor(o_t[1][:, k, :], bank("turn4", k), o_t[0][:, k, :], ALU.subtract).then_inc(t4_lo, 1)

            run({"stats": stats, "normalise": normalise, "rotate": rotate, "turn0_low": turn0_low,
                 "state_sum": state_sum, "state_low": state_low, "r_scores": r_scores, "r_add": r_add_,
                 "quantise": quantise, "copy_q": copy_q, "linear_add": linear_add, "turn3_low": turn3_low,
                 "qk_low": qk_low, "v_low": v_low, "maxima": maxima, "max_split": max_split, "max_copy": max_copy,
                 "take_v": take_v, "divide": divide, "x_bias": x_bias_, "o_low": o_low, "o_add": o_add,
                 "stats_a": stats_a, "normalise_a": normalise_a, "turn4_low": turn4_low}, dve)

        @block.tensor
        def _(pe):
            pe.wait_ge(const_ok, CONSTS)
            pe.wait_ge(w16_lo, 3)
            pe.wait_ge(w8_step, W8_STEPS)

            THREE = ((0, 0), (0, 1), (1, 0))

            read = {"misc": [None, None], "sc": [None, None]}

            def take(name, arg, read_by, i=0):
                last = read[bank_no[name, arg][0]]
                if last[0] is not None:
                    pe.wait_ge(*last[0])
                last[:] = [last[1], read_by]
                return bank(name, arg, i)

            def banks(b, _):
                read["misc"][:] = [(qk_lo, b * 4 + 3), (qk_lo, b * 4 + 4)]
                read["sc"][:] = [(m_max, b * 64 + 32), (m_cp, b * 2 + 1)]

            def turn(to, src, col):
                for i in range(T):
                    ins = pe.transpose(to[:, i * P:(i + 1) * P], src[:, i, col * P:(col + 1) * P], ident[:])
                return ins

            def turn0(b, arg):
                half, w = arg
                to = take("turn0", arg, (t0_lo, b * 4 + 2 * half + w + 1))
                pe.wait_ge(rot_q if w == 0 else rot_k, (b + 1) * 2)
                turn(to, q_r if w == 0 else k_r, half).then_inc(tr0, 1)

            def state_(b, half):
                to = take("state", half, (state_ok, (b * 2 + half) * 5 + 5))
                pe.wait_ge(rot_k, (b + 1) * 2)
                for c in range(T - 1):
                    cols = slice(half * P, (half + 1) * P)
                    ins = pe.matmul(to[:, c * P:(c + 1) * P], k_r[:, c, cols], ctx_n[:, c, cols],
                                    start=True, stop=True)
                ins.then_inc(upd, 1)

            def r_scores(b, arg):
                half, c = arg
                if c == 0:
                    pe.wait_ge(st0_in, (b * 2 + half + 1) * 12 * 16)
                tok = slice(c * P, (c + 1) * P)
                for g in range(2):
                    n = half * 8 + c * 2 + g
                    to = take("r_scores", arg, (r_mask, b * 16 + n + 1), g)
                    for i in range(4):
                        pair, par = 2 * g + i // 2, i % 2
                        ins = pe.matmul(to[:, i * P:(i + 1) * P], kz0[par][0:KR, pair, tok], sq0[0:KR, pair, tok],
                                        start=True, stop=True)
                    ins.then_inc(r_sc, 1)

            def r_outs(b, arg):
                half, c = arg
                tok = slice(c * P, (c + 1) * P)
                to = take("r_outs", arg, (r_add, b * 8 + half * 4 + c + 1))
                first = True
                if c:
                    pe.wait_ge(state_lo, b * 2 + half + 1)
                    for qi, si in THREE:
                        pe.matmul(to[:, 0:P], t0[0][qi][:, half, tok], state_s[si][:, c - 1, :],
                                  start=first, stop=False, skip_group_check=True)
                        first = False
                if c == 0 and half == 0:
                    pe.wait_ge(v0_lo, b + 1)
                for h in range(HH):
                    if h % 4 == 0:
                        pe.wait_ge(r_lo, b * 16 + half * 8 + c * 2 + h // 4 + 1)
                    col = half * P + h * HD
                    for si, vi in THREE:
                        ins = pe.matmul(to[:, h * HD:(h + 1) * HD], rs[si][:, c % 2, h, :],
                                        v0[vi][:, c, col:col + HD], start=first, stop=True, skip_group_check=True)
                        first = False
                ins.then_inc(r_out, 1)

            def turn_q(b, _):
                pe.wait_ge(quant, (b + 1) * QUANT_STEPS)
                for k in range(KD):
                    to = take("turn_q", 0, (xq_cp, b * 2 + k + 1), k)
                    for i in range(T):
                        ins = pe.transpose(to[:, i * 64:(i + 1) * 64].bitcast(BF16), x_q[:, i, k * P:(k + 1) * P],
                                           ident_bf[:])
                    ins.then_inc(xq_tr, 1)

            def linear(b, _):
                for u in range(2):
                    to = take("linear", 0, (ffn_y, b * 2 + u + 1), u)
                    pe.wait_ge(xq_cp, (b + 1) * 2)
                    for i in range(2):
                        tok = slice((2 * u + i) * P, (2 * u + i + 1) * P)
                        for k in range(KD):
                            ins = pe.matmul(to[:, i * D:(i + 1) * D], xq_t[:, k, tok], w8[:, k, :],
                                            start=(k == 0), stop=(k == KD - 1))
                    ins.then_inc(ffn_mm, 1)

            def turn3(b, k):
                to = take("turn3", k, (t3_lo, b * 2 + k + 1))
                pe.wait_ge(ln_out, (b + 1) * 3)
                turn(to, x_n, k).then_inc(tr3, 1)

            def qk(b, n):
                w, m = 1 - n // 2, n % 2
                to = take("qk", n, (qk_lo, b * 4 + n + 1))
                pe.wait_ge(*((t3_lo, (b + 1) * 2) if w == 0 else (c3_lo, b + 1)))
                src, wt = (x3, wq) if w == 0 else (c3, wkv)
                for j, (wi, xi) in enumerate(THREE):
                    for k in range(KD):
                        ins = pe.matmul(to, wt[wi][:, k, m * P:(m + 1) * P], src[xi][:, k, :],
                                        start=(j == 0 and k == 0), stop=(j == 2 and k == KD - 1))
                ins.then_inc(qk_mm, 1)

            def v(b, u):
                to = take("v", u, (v_lo, b * 2 + u + 1))
                for i in range(2):
                    tok = slice((2 * u + i) * P, (2 * u + i + 1) * P)
                    for j, (xi, wi) in enumerate(THREE):
                        for k in range(KD):
                            ins = pe.matmul(to[:, i * D:(i + 1) * D], c3[xi][:, k, tok], wkv[wi][:, k, D:2 * D],
                                            start=(j == 0 and k == 0), stop=(j == 2 and k == KD - 1))
                ins.then_inc(v_mm, 1)

            def maxima(b, arg):
                half, h, g = arg
                if h == 0 and g == 0:
                    pe.wait_ge(st1_in[half], (b + 1) * 12 * 16)
                for i in range(2):
                    qt = 2 * g + i
                    to = take("maxima", arg, (m_max, b * 64 + half * 32 + h * T + qt + 1), i)
                    pe.matmul(to, sq1[0:KR, half, h // 2, qt * P:(qt + 1) * P], kz1[h % 2][0:KR, half, h // 2, :],
                              start=True, stop=True).then_inc(m_sc, 1)

            def max_turn(b, half):
                to = take("max_turn", half, (m_cp, b * 2 + half + 1))
                pe.wait_ge(m_16, b * 4 + half * 2 + 2)
                for qt in range(T):
                    ins = pe.transpose(to[0:4 * HP, qt * 64:(qt + 1) * 64].bitcast(F16),
                                       max16[:, qt].rearrange("p r l q -> p (r l q)"), ident16[:])
                ins.then_inc(m_tr, 1)

            def score(b, arg):
                h, g = arg
                half, pair, par = h // HH, (h % HH) // 2, h % 2
                if h % HH == 0 and g == 0:
                    pe.wait_ge(m_in[half], (b + 1) * 16)
                    if half == 0:
                        pe.wait_ge(rows_in, 2 * 16)
                for kt in range(2 * g, 2 * g + 2):
                    need(pe, s_exp, b * 64 + h * 4 + kt - 1)
                    pe.matmul(st[:, kt % 2, :], kz1[par][0:MR, half, pair, kt * P:(kt + 1) * P],
                              sq1[0:MR, half, pair, :], start=True, stop=True).then_inc(s_mm, 1)

            def values(b, arg):
                h, part = arg
                g = h // 4
                if h % 4 == 0 and part == 0:
                    need(pe, o_mul, b * 4 + g - 1)
                if h == 0 and part == 0:
                    pe.wait_ge(v_cp, (b + 1) * 2)
                if part == 0:
                    pe.wait_ge(p_lo, b * 32 + 2 * h + 2)
                o = pv[:, g % 2, 0:4 * T * (HD + 1)].rearrange("p (h q d) -> p h q d", h=4, q=T)
                parts = (ph, pl)
                for qt in range(2 * part, 2 * part + 2):
                    for kt in range(T):
                        for j, (pi, vi) in enumerate(THREE):
                            ins = pe.matmul(o[:, h % 4, qt, :], parts[pi][:, h % 2, kt, qt * P:(qt + 1) * P],
                                            v_cur[vi][:, kt, h, :], start=(kt == 0 and j == 0),
                                            stop=(kt == T - 1 and j == 2))
                if part == 1:
                    ins.then_inc(pv_mm, 1)

            def o_turn(b, k):
                to = take("o_turn", k, (o_lo, b * 2 + k + 1))
                pe.wait_ge(o_mul, (b + 1) * 4)
                turn(to, o_n, k).then_inc(o_tr, 1)

            def o_proj(b, u):
                to = take("o_proj", u, (pr_x, b * 2 + u + 1))
                pe.wait_ge(o_lo, (b + 1) * 2)
                for i in range(2):
                    tok = slice((2 * u + i) * P, (2 * u + i + 1) * P)
                    for j, (oi, wi) in enumerate(THREE):
                        for k in range(KD):
                            ins = pe.matmul(to[:, i * D:(i + 1) * D], o_t[oi][:, k, tok], wp[wi][:, k, :],
                                            start=(j == 0 and k == 0), stop=(j == 2 and k == KD - 1))
                ins.then_inc(pr_mm, 1)

            def turn4(b, k):
                to = take("turn4", k, (t4_lo, b * 2 + k + 1))
                pe.wait_ge(la_out, b + 1)
                turn(to, x_n, k).then_inc(tr4, 1)

            run({"banks": banks, "turn0": turn0, "state": state_, "r_scores": r_scores, "r_outs": r_outs,
                 "turn_q": turn_q, "linear": linear, "turn3": turn3, "qk": qk, "v": v, "maxima": maxima,
                 "max_turn": max_turn, "score": score, "values": values, "o_turn": o_turn, "o_proj": o_proj,
                 "turn4": turn4}, pe)


N_CONST = 15
CONSTS = 5
W8_STEPS = 8
QUANT_STEPS = 7


def phase_m(nc, t, out, x_d, xt_d, raw, raw_b, w_loaded):
    with ExitStack() as ctx:
        def sb(name, shape, dt=F32):
            return ctx.enter_context(nc.sbuf_tensor(name, shape, dt))

        def sem(name):
            return ctx.enter_context(nc.semaphore(name))

        N = B * S
        CH = N // 512
        U = CH * IT
        GU, DN = KD * 2 * I, IT * D
        WSTEP = 1024
        WP = (GU + DN) // WSTEP
        LAG = 2

        x_all = sb("x_all", [P, NT, D])
        xt = [sb(f"xt{i}", [P, B, KD, S], F16) for i in range(2)]
        ident, before = sb("ident_m", [P, P]), sb("before", [P, E, E])
        wr_raw = sb("wr_raw", [P, KD, E])
        wr = [sb(f"wr{i}", [P, KD, E], F16) for i in range(2)]
        bias_r, bias_d = sb("bias_r", [P, E]), sb("bias_d", [E, D])
        logit = sb("logit", [P, NT, E])
        above, equal = sb("above", [P, NT, E * E]), sb("equal", [P, NT, E * E])
        rank, top, expo = sb("rank", [P, NT, E]), sb("top", [P, NT]), sb("expo", [P, NT, E])
        total, combine = sb("total", [P, NT]), sb("combine", [P, NT, E])
        scaled = sb("scaled", [P, E, NT])
        combine_t = sb("combine_t", [E, N])
        w = [[sb(f"w_{e}{i}", [P, GU + DN], F16) for i in range(2)] for e in range(2)]
        bias16, share = sb("bias16", [P, 2, 8]), sb("share", [P, 2, NT])
        gate, up = sb("gate", [P, 2, 512]), sb("up", [P, 2, 512])
        glu, prod = sb("glu", [P, 2, 512]), sb("prod", [P, 2, 512])
        h16 = [sb(f"h16_{i}", [P, 4, 512], F16) for i in range(2)]

        gu_ps = ctx.enter_context(nc.psum_tensor("gu_ps", [P, 4, 512], F32))
        dn_ps = ctx.enter_context(nc.psum_tensor("dn_ps", [P, 4, 512], F32))

        const_in = sem("m_const_in")
        x_in = sem("m_x_in")
        wr_hi, wr_lo = sem("wr_hi"), sem("wr_lo")
        rt_mm = sem("rt_mm")
        rt = sem("rt")
        rt_exp = sem("rt_exp")
        ct_tr, ct_cp = sem("ct_tr"), sem("ct_cp")
        bd_mm, bd_x = sem("bd_mm"), sem("bd_x")
        w_in = sem("w_in")
        w_hi, w_lo = sem("w_hi"), sem("w_lo")
        w_bias, w_share = sem("w_bias"), sem("w_share")
        gate_mm, up_mm = sem("gate_mm"), sem("up_mm")
        gate_ok, glu_ok, up_ok, prod_ok = sem("gate_ok"), sem("glu_ok"), sem("up_ok"), sem("prod_ok")
        h_hi, h_lo = sem("h_hi"), sem("h_lo")
        dn_mm, dn_x = sem("dn_mm"), sem("dn_x")
        y_out = sem("y_out")
        N_CONST_M = 6

        def moe(run_expert):
            def emit(engine, loop=True):
                for k in range(2):
                    run_expert(k, k, False)
                if loop:
                    with engine.Fori(1, E // 2 - 1) as i:
                        for k in range(2):
                            run_expert(2 * i + k, k, False)
                else:
                    for e in range(2, E - 2):
                        run_expert(e, e % 2, False)
                for k in range(2):
                    run_expert(E - 2 + k, k, k == 1)
            return emit

        block = ctx.enter_context(nc.Block())

        @block.sync
        def _(sp):
            def load_w(e):
                gu = t["gate_up_t"].rearrange("e (k p) j -> e p k j", k=KD)[bass.ds(e, 1)].rearrange("a p k j -> (a p) k j")
                sp.dma_start(raw[:, 0:GU].rearrange("p (k j) -> p k j", k=KD), gu).then_inc(w_in, 16)
                dn = t["down_t"].rearrange("e (k p) d -> e p k d", k=IT)[bass.ds(e, 1)].rearrange("a p k d -> (a p) k d")
                sp.dma_start(raw[:, GU:].rearrange("p (k d) -> p k d", k=IT), dn).then_inc(w_in, 16)
                sp.dma_start(raw_b[:, 0, :], t["gate_up_bias_t"][bass.ds(e, 1)].rearrange("a p j -> (a p) j")).then_inc(w_in, 16)

            sp.dma_start(ident[:], t["ident"]).then_inc(const_in, 16)
            sp.dma_start(before[:], t["before"]).then_inc(const_in, 16)
            sp.dma_start(wr_raw[:], t["wr_t"].rearrange("(k p) e -> p k e", k=KD)).then_inc(const_in, 16)
            sp.dma_start(bias_r[:], t["L1_ffn_router_bias"][None, :].to_broadcast([P, E])).then_inc(const_in, 16)
            sp.dma_start(bias_d[:], t["L1_ffn_down_proj_bias"]).then_inc(const_in, 16)
            for hl in range(2):
                sp.dma_start(xt[hl][:], xt_d[hl].rearrange("b p k n -> p b k n")).then_inc(x_in, 16)
            load_w(0)
            sp.dma_start(x_all[:], x_d.rearrange("t p d -> p t d")).then_inc(const_in, 16)

            def after(e):
                sp.wait_ge(w_lo, (e + 1) * WP)
                sp.wait_ge(w_bias, (e + 1) * 2)

            def expert(e, k, last):
                if not last:
                    after(e)
                    load_w(e + 1)

            moe(expert)(sp, loop=False)
            for c in range(CH):
                sp.wait_ge(dn_x, (E - 1) * NT + 4 * c + 4)
                sp.dma_start(out.rearrange("(c t p) d -> c p t d", c=CH, t=4)[c],
                             x_all[:, 4 * c:4 * c + 4, :]).then_inc(y_out, 16)
            sp.wait_ge(y_out, CH * 16)

        def pieces():
            return [slice(i * WSTEP, (i + 1) * WSTEP) for i in range(WP)]

        @block.scalar
        def _(act):
            act.wait_ge(const_in, N_CONST_M * 16)
            act.activation(wr[0][:], wr_raw[:], ACT.Copy, scale=WS).then_inc(wr_hi, 1)
            act.wait_ge(rt, RT_SUB)
            act.activation(expo[:], expo[:], ACT.Exp).then_inc(rt_exp, 1)

            def split(e, k, i):
                if i == 0:
                    act.wait_ge(w_in, (e + 1) * 3 * 16)
                    need(act, dn_mm, (e - 1) * U)
                act.activation(w[k][0][:, pieces()[i]], raw[:, pieces()[i]], ACT.Copy, scale=WS).then_inc(w_hi, 1)

            def unit(e, k, u):
                n = e * U + u
                act.wait_ge(gate_ok, n + 1)
                need(act, prod_ok, n - 1)
                act.activation(glu[:, u % 2, :], gate[:, u % 2, :], ACT.Gelu_apprx_sigmoid,
                               scale=1 / WS).then_inc(glu_ok, 1)
                act.wait_ge(prod_ok, n + 1)
                need(act, dn_mm, n - 3)
                act.activation(h16[0][:, u % 4, :], prod[:, u % 2, :], ACT.Copy).then_inc(h_hi, 1)

            for i in range(WP):
                split(0, 0, i)
            for u in range(LAG):
                unit(0, 0, u)

            def expert(e, k, last):
                for u in range(U):
                    if not last and u in SPLIT_AT:
                        split(e + 1, 1 - k, SPLIT_AT.index(u))
                    if u + LAG < U:
                        unit(e, k, u + LAG)
                    elif not last:
                        unit(e + 1, 1 - k, u + LAG - U)

            moe(expert)(act)

        @block.gpsimd
        def _(pool):
            def unit(e, k, u):
                n = e * U + u
                pool.wait_ge(h_hi, n + 1)
                pool.tensor_tensor(h16[1][:, u % 4, :], prod[:, u % 2, :], h16[0][:, u % 4, :],
                                   ALU.subtract).then_inc(h_lo, 1)

            for u in range(LAG):
                unit(0, 0, u)

            def expert(e, k, last):
                for u in range(U):
                    if u + LAG < U:
                        unit(e, k, u + LAG)
                    elif not last:
                        unit(e + 1, 1 - k, u + LAG - U)

            moe(expert)(pool)

        @block.vector
        def _(dve):
            count = [0]

            def done(ins):
                count[0] += 1
                ins.then_inc(rt, 1)
                dve.wait_ge(rt, count[0])

            dve.wait_ge(wr_hi, 1)
            dve.scalar_tensor_tensor(wr[1][:], wr_raw[:], WS, wr[0][:], ALU.mult, ALU.subtract).then_inc(wr_lo, 1)

            dve.wait_ge(const_in, N_CONST_M * 16)
            dve.wait_ge(rt_mm, 1)
            flat = lambda a: a[:].rearrange("p t e -> p (t e)")
            per_expert = lambda a: a[:].to_broadcast([P, NT, E])
            done(dve.tensor_scalar(flat(logit), dn_ps[:, 0, 0:NT * E], 1 / WS, None, ALU.mult))
            done(dve.tensor_tensor(logit[:], logit[:], bias_r[:, None, :].to_broadcast([P, NT, E]), ALU.add))
            square = lambda a: a[:].rearrange("p t (i j) -> p t i j", i=E)
            this, other = logit[:, :, :, None].to_broadcast([P, NT, E, E]), logit[:, :, None, :].to_broadcast([P, NT, E, E])
            dve.tensor_tensor(square(above), other, this, ALU.is_gt)
            done(dve.tensor_tensor(square(equal), other, this, ALU.is_equal))
            done(dve.tensor_tensor(equal[:], equal[:], before[:].rearrange("p i j -> p (i j)")[:, None, :]
                                   .to_broadcast([P, NT, E * E]), ALU.mult))
            done(dve.tensor_tensor(above[:], above[:], equal[:], ALU.add))
            done(dve.tensor_reduce(rank[:], square(above), AX.X, ALU.add))
            dve.tensor_scalar(rank[:], rank[:], TOPK - 0.5, None, ALU.is_lt)
            done(dve.tensor_reduce(top[:], logit[:], AX.X, ALU.max))
            done(dve.tensor_tensor(expo[:], logit[:], top[:, :, None].to_broadcast([P, NT, E]), ALU.subtract))
            assert count[0] == RT_SUB
            dve.wait_ge(rt_exp, 1)
            done(dve.tensor_tensor(expo[:], expo[:], rank[:], ALU.mult))
            done(dve.tensor_reduce(total[:], expo[:], AX.X, ALU.add))
            done(dve.reciprocal(total[:], total[:]))
            done(dve.tensor_tensor(combine[:], expo[:], total[:, :, None].to_broadcast([P, NT, E]), ALU.mult))
            done(dve.tensor_scalar(scaled[:].rearrange("p e t -> p t e"), combine[:], 1 / (WS * WS), None, ALU.mult))
            assert count[0] == RT_STEPS
            for c in range(4):
                dve.wait_ge(ct_tr, c + 1)
                dve.tensor_copy(combine_t[:, c * 512:(c + 1) * 512], dn_ps[0:E, c, :]).then_inc(ct_cp, 1)
            for u in range(NT // 2):
                dve.wait_ge(bd_mm, u + 1)
                xs = x_all[:, 2 * u:2 * u + 2, :].rearrange("p t d -> p (t d)")
                dve.tensor_tensor(xs, dn_ps[:, u % 4, :], xs, ALU.add).then_inc(bd_x, 1)
            dve.wait_ge(bd_x, NT // 2)

            def split(e, k, i):
                dve.wait_ge(w_hi, e * WP + i + 1)
                dve.scalar_tensor_tensor(w[k][1][:, pieces()[i]], raw[:, pieces()[i]], WS, w[k][0][:, pieces()[i]],
                                         ALU.mult, ALU.subtract).then_inc(w_lo, 1)
                if i == 0:
                    need(dve, up_ok, (e - 1) * U)
                    dve.tensor_scalar(bias16[:, k, 0:4], raw_b[:, 0, 0:4], WS, None, ALU.mult).then_inc(w_bias, 1)
                    dve.tensor_scalar(bias16[:, k, 4:8], raw_b[:, 0, 4:8], WS, WS, ALU.mult, ALU.add).then_inc(w_bias, 1)
                    dve.tensor_copy(share[:, k:k + 1, :], scaled[:, bass.ds(e, 1), :]).then_inc(w_share, 1)

            def unit(e, k, u):
                n = e * U + u
                it = u % IT
                dve.wait_ge(gate_mm, n + 1)
                if u == 0:
                    dve.wait_ge(w_bias, (e + 1) * 2)
                need(dve, glu_ok, n - 1)
                dve.tensor_scalar(gate[:, u % 2, :], gu_ps[:, 2 * (u % 2), :], bias16[:, k, it:it + 1], WS * LIMIT,
                                  ALU.add, ALU.min).then_inc(gate_ok, 1)
                dve.wait_ge(up_mm, n + 1)
                dve.tensor_scalar(up[:, u % 2, :], gu_ps[:, 2 * (u % 2) + 1, :], bias16[:, k, 4 + it:5 + it],
                                  WS * (LIMIT + 1), ALU.add, ALU.min).then_inc(up_ok, 1)
                dve.wait_ge(up_ok, n + 1)
                dve.wait_ge(glu_ok, n + 1)
                need(dve, h_hi, n - 1)
                need(dve, h_lo, n - 1)
                dve.scalar_tensor_tensor(prod[:, u % 2, :], up[:, u % 2, :], WS * (1 - LIMIT), glu[:, u % 2, :],
                                         ALU.max, ALU.mult).then_inc(prod_ok, 1)

            def collect(e, k, c):
                dve.wait_ge(dn_mm, e * U + IT * (c + 1))
                if c == 0:
                    dve.wait_ge(w_share, e + 1)
                    need(dve, dn_x, e * NT)
                for i in range(4):
                    tile = 4 * c + i
                    xs = x_all[:, tile, :]
                    dve.scalar_tensor_tensor(xs, dn_ps[:, 2 * (c % 2) + i // 2, (i % 2) * D:(i % 2 + 1) * D],
                                             share[:, k, tile:tile + 1], xs, ALU.mult, ALU.add).then_inc(dn_x, 1)

            for i in range(WP):
                split(0, 0, i)
            for u in range(LAG):
                unit(0, 0, u)

            def expert(e, k, last):
                for u in range(U):
                    if not last and u in SPLIT_AT:
                        split(e + 1, 1 - k, SPLIT_AT.index(u))
                    if u + LAG < U:
                        unit(e, k, u + LAG)
                    elif not last:
                        unit(e + 1, 1 - k, u + LAG - U)
                    if u % IT == IT - 1:
                        collect(e, k, u // IT)

            moe(expert)(dve)

        @block.tensor
        def _(pe):
            THREE = ((0, 0), (0, 1), (1, 0))
            pe.wait_ge(x_in, 2 * 16)
            pe.wait_ge(wr_lo, 1)
            for tile in range(NT):
                b, tok = tile // T, slice((tile % T) * P, (tile % T + 1) * P)
                for j, (xi, wi) in enumerate(THREE):
                    for k in range(KD):
                        ins = pe.matmul(dn_ps[:, 0, tile * E:(tile + 1) * E], xt[xi][:, b, k, tok], wr[wi][:, k, :],
                                        start=(j == 0 and k == 0), stop=(j == 2 and k == KD - 1))
            ins.then_inc(rt_mm, 1)
            pe.wait_ge(rt, RT_STEPS)
            for c in range(4):
                for i in range(4):
                    ins = pe.transpose(dn_ps[0:E, c, i * P:(i + 1) * P], combine[:, 4 * c + i, :], ident[:])
                ins.then_inc(ct_tr, 1)
            for u in range(NT // 2):
                if u < 4:
                    pe.wait_ge(ct_cp, 4)
                else:
                    pe.wait_ge(bd_x, u - 3)
                for i in range(2):
                    tile = 2 * u + i
                    ins = pe.matmul(dn_ps[:, u % 4, i * D:(i + 1) * D], combine_t[:, tile * P:(tile + 1) * P], bias_d[:],
                                    start=True, stop=True)
                ins.then_inc(bd_mm, 1)

            def gate_up(e, k, u):
                n = e * U + u
                c, it = u // IT, u % IT
                if u == 0:
                    pe.wait_ge(w_lo, (e + 1) * WP)
                for g, (mm, ok) in enumerate(((gate_mm, gate_ok), (up_mm, up_ok))):
                    need(pe, ok, n - 1)
                    for j, (wi, xi) in enumerate(THREE):
                        for kd in range(KD):
                            col = kd * 2 * I + g * I + it * P
                            ins = pe.matmul(gu_ps[:, 2 * (u % 2) + g, :], w[k][wi][:, col:col + P], xt[xi][:, c, kd, :],
                                            start=(j == 0 and kd == 0), stop=(j == 2 and kd == KD - 1))
                    ins.then_inc(mm, 1)

            def down(e, k, u):
                c, it = u // IT, u % IT
                pe.wait_ge(h_lo, e * U + u + 1)
                if it == 0:
                    need(pe, dn_x, e * NT + 4 * (c - 1))
                    if isinstance(e, int) and e == 0 or c == 0:
                        pe.wait_ge(bd_x, NT // 2)
                for i in range(4):
                    for j, (hi, wi) in enumerate(THREE):
                        ins = pe.matmul(dn_ps[:, 2 * (c % 2) + i // 2, (i % 2) * D:(i % 2 + 1) * D],
                                        h16[hi][:, u % 4, i * P:(i + 1) * P],
                                        w[k][wi][:, GU + it * D:GU + (it + 1) * D],
                                        start=(it == 0 and j == 0 and i % 2 == 0), stop=(it == IT - 1 and j == 2),
                                        skip_group_check=True)
                ins.then_inc(dn_mm, 1)

            for u in range(LAG):
                gate_up(0, 0, u)

            def expert(e, k, last):
                for u in range(U):
                    if u + LAG < U:
                        gate_up(e, k, u + LAG)
                    elif not last:
                        gate_up(e + 1, 1 - k, u + LAG - U)
                    down(e, k, u)

            moe(expert)(pe)


RT_SUB, RT_STEPS = 8, 13
SPLIT_AT = [3, 6, 9]


_INS = ["x", "ctx", "ctx_swapped", "ctx_t", "L0_ffn_kernel", "L0_ffn_input_scale", "L0_ffn_kernel_scale",
        "L0_ffn_bias", "wq_t", "wkv_t", "wp_t", "L1_xattn_bproj", "wr_t", "L1_ffn_router_bias", "gate_up_t",
        "gate_up_bias_t", "down_t", "L1_ffn_down_proj_bias"]


def kernel(**inputs):
    import concourse.bacc as bacc
    from concourse.bass_utils import run_bass_kernel_spmd

    a = {k: np.asarray(v) for k, v in inputs.items()}
    flat = a["ctx_1024"].reshape(B * S, D)
    a["x"] = a["x"].reshape(B * S, D)
    a["ctx"] = flat
    a["ctx_swapped"] = flat.reshape(B * S, D // 2, 2)[:, :, ::-1].reshape(B * S, D)
    a["ctx_t"] = flat.T
    a["wq_t"], a["wkv_t"], a["wp_t"] = a["L1_xattn_Wq"].T, a["L1_xattn_Wkv"].T, a["L1_xattn_Wproj"].T
    a["wr_t"] = a["L1_ffn_router_weight"].T
    a["gate_up_t"] = a["L1_ffn_gate_up_proj"].transpose(0, 2, 1)
    a["gate_up_bias_t"] = a["L1_ffn_gate_up_proj_bias"].reshape(E, 8, P).transpose(0, 2, 1)
    a["down_t"] = a["L1_ffn_down_proj"].transpose(0, 2, 1)
    arrays = {name: np.ascontiguousarray(a[name]) for name in _INS}
    arrays.update(tables())
    nc = bacc.Bacc("TRN2", target_bir_lowering=False, num_devices=1)
    aps = {name: nc.dram_tensor(f"in_{name}", v.shape, mybir.dt.from_np(v.dtype), kind="ExternalInput").ap()
           for name, v in arrays.items()}
    out = nc.dram_tensor("out", (B * S, D), F32, kind="ExternalOutput").ap()
    xattn_ffn_moe_kernel(nc, aps, out)
    r = run_bass_kernel_spmd(nc, [{f"in_{name}": v for name, v in arrays.items()}], core_ids=[0])
    return r.results[0]["out"].reshape(B, S, D)
```

```python
from contextlib import ExitStack

import concourse.bass as bass
import numpy as np
from concourse import mybir

F32, F16, BF16, I32 = mybir.dt.float32, mybir.dt.float16, mybir.dt.bfloat16, mybir.dt.int32
ALU, ACT, AX = mybir.AluOpType, mybir.ActivationFunctionType, mybir.AxisListType

P = 128
B, S, D = 4, 512, 256
H, HD = 16, 16
T = S // P
KD = D // P
NT = B * T
E, I = 8, 512
IT = I // P
PAIRS = H // 2
HP = PAIRS // 2
HH = H // 2
VW = 2 * HD + 1
SR = 3 * HD
KR = 2 * SR
MR = KR + 4
WS = 16.0
LIMIT, EPS = 7.0, 1e-5
QSCALE = float(HD) ** -0.5
TOPK = 4


def need(eng, sem, value):
    if not (isinstance(value, int) and value <= 0):
        eng.wait_ge(sem, value)


def tables():
    pos = np.arange(S, dtype=np.float64)
    base = (np.arange(0, HD, 2) + 0.4 * HD) / (1.4 * HD)
    scale = base[None, :] ** (pos / 512.0)[:, None]
    angle = pos[:, None] / 10000.0 ** (np.arange(HD // 2) / (HD // 2))[None, :]
    gamma = (1.0 - np.exp(np.linspace(np.log(1 / 32), np.log(1 / 512), H))).astype(np.float32).astype(np.float64)
    sign = np.array([-1.0, 1.0])
    within = pos % P
    out = {}
    for name, s, decay in (("q", scale, gamma[None, :] ** within[:, None]),
                           ("k", 1.0 / scale, gamma[None, :] ** -within[:, None])):
        cos = np.repeat(np.cos(angle) * s, 2, axis=-1)
        sin = np.repeat(np.sin(angle) * s, 2, axis=-1) * np.tile(sign, HD // 2)
        for part, t in (("cos", cos), ("sin", sin)):
            full = (decay[:, :, None] * t[:, None, :]).reshape(S, D)
            out[f"{name}_{part}"] = np.ascontiguousarray(full.reshape(T, P, D).transpose(1, 0, 2), np.float32)
    head = np.arange(D) // HD
    block = np.zeros((P, 2, P), np.float32)
    for half in range(2):
        hs = head[half * P:(half + 1) * P]
        block[:, half] = (hs[:, None] == hs[None, :]) * (gamma[hs] ** P)[:, None]
    out["chunk_decay"] = block
    out["causal"] = (np.arange(P)[None, :] >= np.arange(P)[:, None]).astype(np.float32)
    out["ident"] = np.eye(P, dtype=np.float32)
    ones = np.zeros((4, 2, 2 * HP * S), np.float32)
    ones[0:2, 0], ones[2:4, 1] = 1.0, 1.0
    out["max_rows"] = ones.astype(np.float16)
    out["before"] = np.tile((np.arange(E)[None, :] < np.arange(E)[:, None]).astype(np.float32)[None], (P, 1, 1))
    return out


def xattn_ffn_moe_kernel(nc, t, out):
    dram = lambda name, shape, dt: nc.dram_tensor(name, shape, dt, kind="Internal").ap()
    stack0_d = dram("stack0_d", (2, 2, D, S), F16)
    stack1_d = dram("stack1_d", (2, 2, D, S), F16)
    max_d = dram("max_d", (2, 4 * HP, S), F16)
    x_d = dram("x_d", (NT, P, D), F32)
    xt_d = dram("xt_d", (2, B, P, KD, S), F16)

    with ExitStack() as both:
        raw = both.enter_context(nc.sbuf_tensor("raw", [P, KD * 2 * I + IT * D], F32))
        raw_b = both.enter_context(nc.sbuf_tensor("raw_b", [P, 2, 8], F32))
        w_in = both.enter_context(nc.semaphore("w_in"))
        load_w = lambda sp, e: load_expert(sp, t, raw, raw_b, w_in, e)
        phase_a(nc, t, stack0_d, stack1_d, max_d, x_d, xt_d, load_w)
        phase_m(nc, t, out, x_d, xt_d, raw, raw_b, w_in, load_w)


def load_expert(sp, t, raw, raw_b, w_in, e):
    gu = t["gate_up_t"].rearrange("e (k p) j -> e p k j", k=KD)[e]
    sp.dma_start(raw[:, 0:KD * 2 * I].rearrange("p (k j) -> p k j", k=KD), gu).then_inc(w_in, 16)
    dn = t["down_t"].rearrange("e (k p) d -> e p k d", k=IT)[e]
    sp.dma_start(raw[:, KD * 2 * I:].rearrange("p (k d) -> p k d", k=IT), dn).then_inc(w_in, 16)
    sp.dma_start(raw_b[:, 0, :], t["gate_up_bias_t"][e]).then_inc(w_in, 16)


def phase_a(nc, t, stack0_d, stack1_d, max_d, x_d, xt_d, load_w):
    with ExitStack() as ctx:
        def sb(name, shape, dt=F32):
            return ctx.enter_context(nc.sbuf_tensor(name, shape, dt))

        def sem(name):
            return ctx.enter_context(nc.semaphore(name))

        q_cos, q_sin = sb("q_cos", [P, T, D]), sb("q_sin", [P, T, D])
        k_cos, k_sin = sb("k_cos", [P, T, D]), sb("k_sin", [P, T, D])
        chunk_decay = sb("chunk_decay", [P, 2, P])
        causal, ident = sb("causal", [P, P]), sb("ident", [P, P])
        ident16, ident_bf = sb("ident16", [P, P], F16), sb("ident_bf", [P, P], BF16)
        half_power = sb("half_power", [P, T])
        wq = [sb(f"wq{i}", [P, KD, D], F16) for i in range(2)]
        wkv = [sb(f"wkv{i}", [P, KD, 2 * D], F16) for i in range(2)]
        wp = [sb(f"wp{i}", [P, KD, D], F16) for i in range(2)]
        w8_raw, w8 = sb("w8_raw", [P, KD, D], BF16), sb("w8", [P, KD, D], BF16)
        bias0, biasp = sb("bias0", [P, D], BF16), sb("biasp", [P, D])
        s_in, s_k = sb("s_in", [P, 1]), sb("s_k", [P, 1])
        r_in, r_k, s_both = sb("r_in", [P, 1]), sb("r_k", [P, 1]), sb("s_both", [P, 1])
        ctx_n, ctx_s, ctx_t = sb("ctx_n", [P, T, D]), sb("ctx_s", [P, T, D]), sb("ctx_t", [P, KD, S])
        x_p, x_n = sb("x_p", [P, T, D]), sb("x_n", [P, T, D])
        bn6, mv, ve, rstd = sb("bn6", [P, T, 6]), sb("mv", [P, 4, T]), sb("ve", [P, T]), sb("rstd", [P, T])
        q_r, q_s, k_r = sb("q_r", [P, T, D]), sb("q_s", [P, T, D]), sb("k_r", [P, T, D])
        t0 = [[sb(f"t0_{w}{i}", [P, 2, S], F16) for i in range(2)] for w in "qk"]
        v0 = sb("v0", [P, T, 2, D], F16)
        state = sb("state", [P, T - 1, P])
        state_s = [sb(f"state_s{i}", [P, T - 1, P], F16) for i in range(2)]
        sq0 = sb("sq0", [P, HP, S], F16)
        kz0 = [sb(f"kz0_{i}", [P, HP, S], F16) for i in range(2)]
        rm = sb("rm", [P, 2, 4, P])
        rs = [sb(f"rs{i}", [P, 2, HH, P], F16) for i in range(2)]
        x_b, x_q, xq_t = sb("x_b", [P, T, D], BF16), sb("x_q", [P, T, D], BF16), sb("xq_t", [P, KD, S], BF16)
        y_a, y_b = sb("y_a", [P, 2, D], BF16), sb("y_b", [P, 2, D], BF16)
        x3 = [sb(f"x3_{i}", [P, KD, S], F16) for i in range(2)]
        c3 = [sb(f"c3_{i}", [P, KD, S], F16) for i in range(2)]
        t1 = [sb(f"t1_{i}", [P, 2, S], F16) for i in range(2)]
        v_next = sb("v_next", [P, T, H, VW], F16)
        v_cur = sb("v_cur", [P, T, H, VW], F16)
        sq1 = sb("sq1", [P, 2, HP, S], F16)
        kz1 = [sb(f"kz1_{i}", [P, 2, HP, S], F16) for i in range(2)]
        neg_max = sb("neg_max", [P, T, 2, HP])
        max16 = sb("max16", [P, T, 2, 2, HP], F16)
        max_t = sb("max_t", [4 * HP, S], F16)
        p32 = sb("p32", [P, 2, 2, S])
        ph, pl = sb("ph", [P, 2, T, S], F16), sb("pl", [P, 2, T, S], F16)
        rden, o_n, o_part = sb("rden", [P, 2, T]), sb("o_n", [P, T, D]), sb("o_part", [P, 2, T, HD])
        o_t = [sb(f"o_t{i}", [P, KD, S], F16) for i in range(2)]
        x_a = sb("x_a", [P, T, D])
        bn6_a, mv_a, ve_a, rstd_a = sb("bn6_a", [P, T, 6]), sb("mv_a", [P, 4, T]), sb("ve_a", [P, T]), sb("rstd_a", [P, T])

        misc = ctx.enter_context(nc.psum_tensor("misc", [P, 2, 512], F32))
        sc = ctx.enter_context(nc.psum_tensor("sc", [P, 2, 512], F32))
        st = ctx.enter_context(nc.psum_tensor("st", [P, 2, 512], F32))
        pv = ctx.enter_context(nc.psum_tensor("pv", [P, 2, 512], F32))

        staging = p32[:].rearrange("p a b n -> p (a b n)")
        wkv_raw = staging[:, 0:KD * 2 * D].rearrange("p (k d) -> p k d", k=KD)
        wq_raw = staging[:, 2 * KD * D:3 * KD * D].rearrange("p (k d) -> p k d", k=KD)
        wp_raw = staging[:, 3 * KD * D:4 * KD * D].rearrange("p (k d) -> p k d", k=KD)
        w8a = x_a[:].rearrange("p t d -> p (t d)")[:, 0:KD * D]
        w8b = x_a[:].rearrange("p t d -> p (t d)")[:, KD * D:2 * KD * D]
        qa, qb = q_r, q_s

        k_table_in, q_table_in = sem("k_table_in"), sem("q_table_in")
        masks_in = sem("masks_in")
        w_raw_in = sem("w_raw_in")
        const_in = sem("const_in")
        half_ok = sem("half_ok")
        const_ok = sem("const_ok")
        w8_step = sem("w8_step")
        w16_hi = sem("w16_hi")
        w16_lo = sem("w16_lo")
        zeros_ok = sem("zeros_ok")
        x_in, ctx_in = sem("x_in"), sem("ctx_in")
        ln_bn, ln_mv, ln_ve, ln_rs, ln_out = (sem(f"ln_{n}") for n in ("bn", "mv", "ve", "rs", "out"))
        rot_q = sem("rot_q")
        rot_k = sem("rot_k")
        v0_hi, v0_lo = sem("v0_hi"), sem("v0_lo")
        tr0, t0_hi, t0_lo = sem("tr0"), sem("t0_hi"), sem("t0_lo")
        st0_out = [sem(f"st0_out{i}") for i in range(2)]
        st0_in = sem("st0_in")
        upd = sem("upd")
        state_ok = sem("state_ok")
        state_hi, state_lo = sem("state_hi"), sem("state_lo")
        r_sc, r_mask, r_hi, r_lo = (sem(f"r_{n}") for n in ("sc", "mask", "hi", "lo"))
        r_out, r_add = sem("r_out"), sem("r_add")
        quant = sem("quant")
        xq_tr, xq_cp = sem("xq_tr"), sem("xq_cp")
        ffn_mm, ffn_y, ffn_b, ffn_x = (sem(f"ffn_{n}") for n in ("mm", "y", "b", "x"))
        tr3, t3_hi, t3_lo = sem("tr3"), sem("t3_hi"), sem("t3_lo")
        c3_hi, c3_lo = sem("c3_hi"), sem("c3_lo")
        qk_mm, qk_hi, qk_lo = sem("qk_mm"), sem("qk_hi"), sem("qk_lo")
        v_mm, v_hi, v_lo = sem("v_mm"), sem("v_hi"), sem("v_lo")
        st1_out = [sem(f"st1_out{i}") for i in range(2)]
        rows_in = sem("rows_in")
        st1_in = [sem(f"st1_in{i}") for i in range(2)]
        m_sc, m_max = sem("m_sc"), sem("m_max")
        m_16 = sem("m_16")
        m_tr, m_cp = sem("m_tr"), sem("m_cp")
        m_out = sem("m_out")
        m_in = [sem(f"m_in{i}") for i in range(2)]
        v_cp = sem("v_cp")
        x_mid = sem("x_mid")
        x_back = sem("x_back")
        s_mm, s_exp = sem("s_mm"), sem("s_exp")
        p_hi = sem("p_hi")
        p_lo = {False: sem("p_lo_pool"), True: sem("p_lo_dve")}
        pv_mm = sem("pv_mm")
        o_take = sem("o_take")
        o_rec, o_sum, o_mul = sem("o_rec"), sem("o_sum"), sem("o_mul")
        o_tr, o_hi, o_lo = sem("o_tr"), sem("o_hi"), sem("o_lo")
        x_bias = sem("x_bias")
        pr_mm, pr_x = sem("pr_mm"), sem("pr_x")
        la_bn, la_mv, la_ve, la_rs, la_out = (sem(f"la_{n}") for n in ("bn", "mv", "ve", "rs", "out"))
        tr4, t4_hi, t4_lo = sem("tr4"), sem("t4_hi"), sem("t4_lo")
        x_out = sem("x_out")

        flat = lambda ap: ap.rearrange("p t d -> p (t d)")
        LAST = B - 1
        SLOTS = 2 * H

        def prep_plan(b):
            yield -2.00, ("stats", b, 0)
            yield -2.20 + 0.01, ("root", b, 0)
            yield -1.90, ("rotate_k", b, 0)
            yield -1.70, ("normalise", b, 0)
            yield -1.60, ("split_ctx", b, 0)
            yield -1.60, ("split_ctx_low", b, 0)
            yield -1.50, ("rotate", b, 0)
            for (half, w), turn, low in (((0, 0), -0.90, -0.40), ((0, 1), -0.70, -0.30), ((1, 0), 0.60, 1.10), ((1, 1), 0.60, 1.20)):
                yield turn, ("turn0", b, (half, w))
                yield turn + 0.05, ("turn0_high", b, (half, w))
                yield low, ("turn0_low", b, (half, w))
            for half, time in ((0, 1.95), (1, 6.00)):
                yield time, ("state", b, half)
                yield time + 0.55, ("state_sum", b, half)
                yield time + 1.00, ("state_low", b, half)
            for n, time in enumerate((2.80, 4.80, 15.50, 15.60)):
                yield time, ("qk", b, n)
                yield time + 0.05, ("qk_high", b, n)
                yield time + 0.50, ("qk_low", b, n)
            for half, first in enumerate((2.30, 5.65)):
                for c in range(T):
                    time = first + 0.75 * c
                    yield time, ("r_scores", b, (half, c))
                    yield time, ("r_mask", b, (half, c))
                    yield time, ("r_high", b, (half, c))
                    yield time + 0.10, ("r_low", b, (half, c))
                    yield time + 1.20, ("r_outs", b, (half, c))
                    yield time + 1.70, ("r_add", b, (half, c))
            yield 4.60, ("stack0", b, 1)
            for u, time in enumerate((7.15, 10.25)):
                yield time, ("v", b, u)
                yield time + 0.15, ("v_high", b, u)
                yield time + 0.50, ("v_low", b, u)
            yield 9.60, ("stats", b, 1)
            yield 9.60 + 0.01, ("root", b, 1)
            yield 10.10, ("normalise", b, 1)
            for i in range(3):
                yield 10.55 + i / 2, ("quantise", b, i)
            yield 12.75, ("turn_q", b, 0)
            yield 13.15, ("copy_q", b, 0)
            yield 13.20, ("linear", b, 0)
            yield 13.50, ("linear_add", b, 0)
            yield 13.80, ("stats", b, 2)
            yield 13.80 + 0.01, ("root", b, 2)
            yield 14.20, ("normalise", b, 2)
            for k in range(KD):
                yield 14.80 + k / 10, ("turn3", b, k)
                yield 14.80 + k / 10 + 0.05, ("turn3_high", b, k)
                yield 15.20 + k / 10, ("turn3_low", b, k)
            yield 16.20, ("stack1", b, 0)
            yield 16.20, ("next_inputs", b, 0)

        def maxima_plan(b, half, first, last, rows):
            n = 2 * HH
            for i in range(n):
                yield first + i * (last - first) / n, ("maxima", b, (half, i // 2, i % 2))
            yield rows, ("max_split", b, half)
            yield rows + 0.30, ("max_turn", b, half)
            yield rows + 0.60, ("max_copy", b, half)

        def out_plan(b):
            yield -3.00, ("x_back", b, 0)
            yield -1.60 - 0.02, ("divide_take", b, 7)
            yield -0.80, ("divide", b, 7)
            yield -0.20, ("x_bias", b, 0)
            for k in range(KD):
                yield -0.20 + k / 20, ("o_turn", b, k)
                yield -0.20 + k / 20 + 0.05, ("o_high", b, k)
                yield 0.30 + k / 20, ("o_low", b, k)
            for u, time in enumerate((1.40, 1.50)):
                yield time, ("o_proj", b, u)
                yield time + 0.50, ("o_add", b, u)
            yield 16.50, ("stats_a", b, 0)
            yield 16.50 + 0.01, ("root_a", b, 0)
            yield 17.25, ("normalise_a", b, 0)
            for k, time in enumerate((17.75, 18.05)):
                yield time, ("turn4", b, k)
                yield time + 0.30, ("turn4_high", b, k)
                yield time + 0.60, ("turn4_low", b, k)
            yield 18.50, ("out_store", b, 0)

        def by_dve(b, h, g):
            return g == 1 and (h >= DVE_SPLITS or isinstance(b, int) and b == LAST)

        def split_done(b, h, g):
            if h < 0:
                return split_done(b - 1, H - 1, g)
            who = by_dve(b, h, g)
            in_batch = sum(by_dve(0, i, j) == who for i in range(H) for j in range(2))
            return p_lo[who], b * in_batch + sum(by_dve(b, i, j) == who for i in range(h + 1) for j in range(2)
                                                 if (i, j) <= (h, g))

        def high_by_dve(b, g):
            return g == 1 and isinstance(b, int) and b == LAST

        def low_of_p(engine, b, arg):
            h, g = arg
            if high_by_dve(b, g):
                engine.wait_ge(p_hi, h + 1)
            else:
                engine.wait_ge(s_exp, b * 64 + h * 4 + 2 * g + 2)
            engine.tensor_tensor(pl[:, h % 2, 2 * g:2 * g + 2, :], p32[:, g], ph[:, h % 2, 2 * g:2 * g + 2, :],
                                 ALU.subtract).then_inc(split_done(b, h, g)[0], 1)

        DVE_SPLITS = 9

        def in_order(*plans):
            yield from (step for _, step in sorted((s for plan in plans for s in plan), key=lambda s: s[0]))

        MAX1, MAX0 = (1.30, 13.55, 14.80), (19.30, 29.90, 30.35)

        def batch_steps(b, before, more):
            def attention():
                yield -2.75, ("banks", b, 0)
                yield -2.90, ("stack1", b, 1)
                for slot in range(SLOTS):
                    h, g = slot // 2, slot % 2
                    yield slot - 0.35, ("score", b, (h, g))
                    yield slot - 0.35 + 0.05, ("exp", b, (h, g))
                    yield slot + 0.70, ("split_p", b, (h, g))
                    if h:
                        yield slot + 0.50, ("values", b, (h - 1, g))
                    elif before:
                        yield slot / 2 - 1.50, ("values", b - 1, (H - 1, g))
                yield 0.05, ("take_v", b, 0)
                for g in range(7):
                    yield 4 * g + 6.65, ("divide_take", b, g)
                    yield 4 * g + 6.90, ("divide", b, g)
            plans = [attention(), maxima_plan(b, 1, *MAX1)]
            if more:
                plans += [prep_plan(b + 1), maxima_plan(b + 1, 0, *MAX0)]
            if before:
                plans.append(out_plan(b - 1))
            return in_order(*plans)

        def end_steps(b):
            for g in range(2):
                yield "values", b, (H - 1, g)
            yield from in_order(out_plan(b))

        def start_steps():
            weights = [(-1.55, ("split_weights", 0, 0)), (0.0, ("split_weights_low", 0, 0)),
                       (3.1, ("quantise_weights", 0, 0))]
            return in_order(prep_plan(0), maxima_plan(0, 0, *MAX0), weights)

        BANKS = {"turn0": ("misc", 1), "state": ("misc", 1), "r_outs": ("misc", 1), "turn_q": ("misc", 2),
                 "linear": ("misc", 2), "turn3": ("misc", 1), "qk": ("misc", 1), "v": ("misc", 1),
                 "o_turn": ("misc", 1), "o_proj": ("misc", 1), "turn4": ("misc", 1),
                 "r_scores": ("sc", 2), "maxima": ("sc", 2), "max_turn": ("sc", 1)}
        READ_IN = {"turn0": "turn0_low", "state": "state_sum", "r_outs": "r_add", "turn_q": "copy_q",
                   "linear": "linear_add", "turn3": "turn3_low", "qk": "qk_low", "v": "v_low", "o_turn": "o_low",
                   "o_proj": "o_add", "turn4": "turn4_low", "r_scores": "r_mask", "maxima": "maxima",
                   "max_turn": "max_copy"}
        bank_no = {}

        def bank(name, arg, i=0):
            pair, n = bank_no[name, arg]
            return (misc if pair == "misc" else sc)[:, (n + i) % 2, :]

        def run(steps, engine, loop=True):
            used = {"misc": 0, "sc": 0}
            unread = {"misc": [], "sc": []}

            def emit(order):
                for name, b, arg in order:
                    for users in unread.values():
                        users[:] = [u for u in users if (READ_IN[u[0]], u[1]) != (name, arg)]
                    if name in BANKS:
                        pair, n = BANKS[name]
                        assert all(u[2] > used[pair] + n - 3 for u in unread[pair]), (name, arg, unread)
                        if READ_IN[name] != name:
                            unread[pair] += [(name, arg, used[pair] + n - 1)]
                        bank_no[name, arg] = (pair, used[pair])
                        used[pair] += n
                    if name in steps:
                        steps[name](b, arg)
            emit(start_steps())
            emit(batch_steps(0, False, True))
            if loop:
                with engine.Fori(1, LAST) as i:
                    emit(batch_steps(i, True, True))
            else:
                for i in range(1, LAST):
                    emit(batch_steps(i, True, True))
            emit(batch_steps(LAST, True, False))
            emit(end_steps(LAST))

        block = ctx.enter_context(nc.Block())

        @block.sync
        def _(sp):
            n_const = [0]

            def const(dst, src):
                sp.dma_start(dst, src).then_inc(const_in, 16)
                n_const[0] += 1

            def load_x(b):
                sp.dma_start(x_p[:], t["x"].rearrange("(b t p) d -> b p t d", b=B, t=T)[b]).then_inc(x_in, 16)

            def load_ctx(b):
                for dst, name in ((ctx_n, "ctx"), (ctx_s, "ctx_swapped")):
                    sp.dma_start(dst[:], t[name].rearrange("(b t p) d -> b p t d", b=B, t=T)[b]).then_inc(ctx_in, 16)
                sp.dma_start(ctx_t[:], t["ctx_t"].rearrange("(k p) (b n) -> b p k n", k=KD, b=B)[b]).then_inc(ctx_in, 16)

            load_x(0)
            load_ctx(0)
            for sem_, pairs in ((k_table_in, ((k_cos, "k_cos"), (k_sin, "k_sin"))),
                                (q_table_in, ((q_cos, "q_cos"), (q_sin, "q_sin"))),
                                (masks_in, ((ident, "ident"), (causal, "causal"), (chunk_decay, "chunk_decay")))):
                for dst, name in pairs:
                    sp.dma_start(dst[:], t[name]).then_inc(sem_, 16)
            for dst, name in ((wkv_raw, "wkv_t"), (wq_raw, "wq_t"), (wp_raw, "wp_t")):
                sp.dma_start(dst, t[name].rearrange("(k p) d -> p k d", k=KD)).then_inc(w_raw_in, 16)
            const(w8_raw[:], t["L0_ffn_kernel"].rearrange("(k p) d -> p k d", k=KD))
            const(s_in[:], t["L0_ffn_input_scale"][None, :].to_broadcast([P, 1]))
            const(s_k[:], t["L0_ffn_kernel_scale"][None, :].to_broadcast([P, 1]))
            const(bias0[:], t["L0_ffn_bias"][None, :].to_broadcast([P, D]))
            const(biasp[:], t["L1_xattn_bproj"][None, :].to_broadcast([P, D]))
            assert n_const[0] == N_CONST
            sp.wait_ge(zeros_ok, 4)
            for i in range(2):
                sp.dma_start(kz1[i][KR:MR].rearrange("p a b n -> p (a b n)"), t["max_rows"][:, i]).then_inc(rows_in, 16)

            def to_stack():
                return [(w, par, j, (0, 0, 1)[j] if w == 0 else (0, 1, 0)[j])
                        for w in range(2) for par in range(2) for j in range(3)]

            def part(stack, w, hl, half, par):
                return stack[w, hl].rearrange("(f q r d) n -> f r d q n", f=2, q=HP, r=2)[half, par]

            def turn0_low(b, arg):
                half, w = arg
                if (half, w) == (0, 0):
                    need(sp, st0_in, b * 2 * 12 * 16)
                sp.wait_ge(t0_lo, b * 4 + 2 * half + w + 1)
                for hl in range(2):
                    sp.dma_start(stack0_d[w, hl].rearrange("(f p) n -> f p n", f=2)[half],
                                 t0[w][hl][:, half, :]).then_inc(st0_out[half], 16)
                if (half, w) == (0, 1):
                    stack0(b, 0)

            def stack0(b, half):
                sp.wait_ge(st0_out[half], (b + 1) * 4 * 16)
                need(sp, r_sc, b * 16 + half * 8)
                for w, par, j, hl in to_stack():
                    row = par * SR + j * HD
                    dst = (sq0 if w == 0 else kz0[par])[row:row + HD]
                    sp.dma_start(dst, part(stack0_d, w, hl, half, par)).then_inc(st0_in, 16)

            def qk_low(b, n):
                if n == 0:
                    for half in range(2):
                        need(sp, st1_in[half], b * 12 * 16)
                w, half = 1 - n // 2, n % 2
                sp.wait_ge(qk_lo, b * 4 + n + 1)
                for hl in range(2):
                    sp.dma_start(stack1_d[w, hl].rearrange("(f p) n -> f p n", f=2)[half],
                                 t1[hl][:, half, :]).then_inc(st1_out[half], 16)

            def stack1(b, half):
                sp.wait_ge(st1_out[half], (b + 1) * 4 * 16)
                need(sp, s_mm, b * 64 - 32 + half * 32)
                for w, par, j, hl in to_stack():
                    row = par * SR + j * HD
                    dst = (sq1 if w == 0 else kz1[par])[row:row + HD, half]
                    sp.dma_start(dst, part(stack1_d, w, hl, half, par)).then_inc(st1_in[half], 16)

            def max_copy(b, half):
                sp.wait_ge(m_cp, b * 2 + half + 1)
                need(sp, m_in[half], b * 16)
                sp.dma_start(max_d[half], max_t[:]).then_inc(m_out, 16)
                sp.wait_ge(m_out, (b * 2 + half + 1) * 16)
                need(sp, s_mm, b * 64 - 32 + half * 32)
                sp.dma_start(sq1[KR:MR, half], max_d[half].rearrange("(r q) n -> r q n", r=4)).then_inc(m_in[half], 16)

            def next_inputs(b, _):
                sp.wait_ge(ffn_x, (b + 1) * 2)
                sp.dma_start(x_d.rearrange("(b t) p d -> b p t d", b=B)[b], x_p[:]).then_inc(x_mid, 16)
                if b < LAST:
                    sp.wait_ge(v0_lo, b + 1)
                    sp.wait_ge(rot_k, (b + 1) * 2)
                    sp.wait_ge(c3_lo, b + 1)
                    sp.wait_ge(upd, (b + 1) * 2)
                    load_ctx(b + 1)
                    sp.wait_ge(ln_out, (b + 1) * 3)
                    sp.wait_ge(x_mid, (b + 1) * 16)
                    load_x(b + 1)
                else:
                    load_w(sp, 0)

            def x_back_(b, _):
                sp.wait_ge(x_mid, (b + 1) * 16)
                if b == 0:
                    sp.wait_ge(w8_step, W8_STEPS)
                need(sp, x_out, b * 3 * 16)
                sp.dma_start(x_a[:], x_d.rearrange("(b t) p d -> b p t d", b=B)[b]).then_inc(x_back, 16)

            def out_store(b, _):
                sp.wait_ge(pr_x, (b + 1) * 2)
                sp.dma_start(x_d.rearrange("(b t) p d -> b p t d", b=B)[b], x_a[:]).then_inc(x_out, 16)
                sp.wait_ge(t4_lo, (b + 1) * 2)
                for hl in range(2):
                    sp.dma_start(xt_d[hl][b], o_t[hl][:]).then_inc(x_out, 16)

            run({"turn0_low": turn0_low, "stack0": stack0, "qk_low": qk_low, "stack1": stack1, "max_copy": max_copy,
                 "next_inputs": next_inputs, "x_back": x_back_, "out_store": out_store}, sp, loop=False)
            sp.wait_ge(x_out, B * 3 * 16)

        @block.gpsimd
        def _(pool):
            pool.memset(half_power[:], -0.5).then_inc(half_ok, 1)
            pool.wait_ge(half_ok, 1)

            def root(ve_t, rs_t, s_ve, s_rs, n):
                pool.wait_ge(s_ve, n)
                pool.tensor_tensor(rs_t[:], ve_t[:], half_power[:], ALU.pow).then_inc(s_rs, 1)

            def root_(b, j):
                root(ve, rstd, ln_ve, ln_rs, b * 3 + j + 1)

            def rotate_k(b, _):
                if isinstance(b, int) and b == 0:
                    pool.wait_ge(k_table_in, 2 * 16)
                pool.wait_ge(ctx_in, (b + 1) * 48)
                need(pool, tr0, b * 4)
                need(pool, upd, b * 2)
                pool.tensor_tensor(k_r[:], ctx_n[:], k_cos[:], ALU.mult)
                pool.tensor_tensor(ctx_s[:], ctx_s[:], k_sin[:], ALU.mult).then_inc(rot_k, 1)
                pool.wait_ge(rot_k, b * 2 + 1)
                pool.tensor_tensor(k_r[:], k_r[:], ctx_s[:], ALU.add).then_inc(rot_k, 1)

            def split_ctx_low(b, _):
                pool.wait_ge(v0_hi, b + 1)
                pool.tensor_tensor(v0[:, :, 1], ctx_n[:], v0[:, :, 0], ALU.subtract).then_inc(v0_lo, 1)
                pool.wait_ge(c3_hi, b + 1)
                pool.tensor_tensor(c3[1][:], ctx_t[:], c3[0][:], ALU.subtract).then_inc(c3_lo, 1)

            def r_low(b, arg):
                half, c = arg
                for g in range(2):
                    n = half * 8 + c * 2 + g
                    pool.wait_ge(r_hi, b * 16 + n + 1)
                    pool.tensor_tensor(rs[1][:, c % 2, 4 * g:4 * g + 4, :], rm[:, n % 2],
                                       rs[0][:, c % 2, 4 * g:4 * g + 4, :], ALU.subtract).then_inc(r_lo, 1)

            def split_p(b, arg):
                if not by_dve(b, *arg):
                    low_of_p(pool, b, arg)

            def root_a(b, _):
                root(ve_a, rstd_a, la_ve, la_rs, b + 1)

            run({"root": root_, "rotate_k": rotate_k, "split_ctx_low": split_ctx_low, "r_low": r_low, "split_p": split_p,
                 "root_a": root_a}, pool)

        @block.scalar
        def _(act):
            def split_weights(b, _):
                act.wait_ge(w_raw_in, 3 * 16)
                for hl, w_raw in ((wkv, wkv_raw), (wq, wq_raw), (wp, wp_raw)):
                    act.activation(hl[0][:], w_raw, ACT.Copy, scale=WS).then_inc(w16_hi, 1)

            def split_ctx(b, _):
                act.wait_ge(ctx_in, (b + 1) * 48)
                need(act, r_out, b * 8)
                act.activation(v0[:, :, 0], ctx_n[:], ACT.Copy).then_inc(v0_hi, 1)
                need(act, v_mm, b * 2)
                act.activation(c3[0][:], ctx_t[:], ACT.Copy).then_inc(c3_hi, 1)

            def turn0_high(b, arg):
                half, w = arg
                if half == 0:
                    need(act, st0_out[0], b * 4 * 16)
                    need(act, st0_out[1], b * 4 * 16)
                    need(act, r_out, b * 8)
                act.wait_ge(tr0, b * 4 + 2 * half + w + 1)
                act.activation(t0[w][0][:, half, :], bank("turn0", arg), ACT.Copy).then_inc(t0_hi, 1)

            def state_low(b, half):
                act.wait_ge(state_ok, (b * 2 + half + 1) * 5)
                need(act, r_out, b * 8 + half * 4)
                act.activation(state_s[0][:], state[:], ACT.Copy).then_inc(state_hi, 1)

            def r_high(b, arg):
                half, c = arg
                for g in range(2):
                    n = half * 8 + c * 2 + g
                    act.wait_ge(r_mask, b * 16 + n + 1)
                    need(act, r_out, b * 8 + half * 4 + c - 1)
                    act.activation(rs[0][:, c % 2, 4 * g:4 * g + 4, :], rm[:, n % 2], ACT.Copy).then_inc(r_hi, 1)

            def turn3_high(b, k):
                act.wait_ge(tr3, b * 2 + k + 1)
                need(act, qk_mm, b * 4)
                act.activation(x3[0][:, k, :], bank("turn3", k), ACT.Copy).then_inc(t3_hi, 1)

            def qk_high(b, n):
                act.wait_ge(qk_mm, b * 4 + n + 1)
                need(act, st1_out[n % 2], (b * 4 + 2 * (n // 2)) * 16)
                act.activation(t1[0][:, n % 2, :], bank("qk", n), ACT.Copy, scale=1 / WS).then_inc(qk_hi, 1)

            def v_high(b, u):
                act.wait_ge(v_mm, b * 2 + u + 1)
                need(act, v_cp, b * 2)
                act.activation(v_next[:, 2 * u:2 * u + 2, :, 0:HD],
                               bank("v", u).rearrange("p (t h d) -> p t h d", t=2, h=H),
                               ACT.Copy, scale=1 / WS).then_inc(v_hi, 1)

            def exp(b, arg):
                h, g = arg
                if not high_by_dve(b, g):
                    need(act, pv_mm, b * 16 + h - 1)
                for kt in range(2 * g, 2 * g + 2):
                    act.wait_ge(s_mm, b * 64 + h * 4 + kt + 1)
                    if not high_by_dve(b, g):
                        act.activation(ph[:, h % 2, kt, :], st[:, kt % 2, :], ACT.Exp, scale=QSCALE)
                    if kt % 2 == 0:
                        need(act, *split_done(b, h - 1, g))
                    act.activation(p32[:, g, kt % 2, :], st[:, kt % 2, :], ACT.Exp, scale=QSCALE).then_inc(s_exp, 1)

            def divide_take(b, g):
                act.wait_ge(pv_mm, b * 16 + 2 * g + 2)
                need(act, o_mul, b * 8 + g)
                o = pv[:, g % 2, 0:2 * T * VW].rearrange("p (h q d) -> p h q d", h=2, q=T)
                act.activation(o_part[:], o[:, :, :, HD + 1:VW], ACT.Copy).then_inc(o_take, 1)

            def o_high(b, k):
                act.wait_ge(x_back, (b + 1) * 16)
                act.wait_ge(o_tr, b * 2 + k + 1)
                act.activation(o_t[0][:, k, :], bank("o_turn", k), ACT.Copy).then_inc(o_hi, 1)

            def turn4_high(b, k):
                act.wait_ge(tr4, b * 2 + k + 1)
                act.wait_ge(pr_mm, (b + 1) * 2)
                act.activation(o_t[0][:, k, :], bank("turn4", k), ACT.Copy).then_inc(t4_hi, 1)

            run({"split_weights": split_weights, "split_ctx": split_ctx, "turn0_high": turn0_high, "state_low": state_low, "r_high": r_high,
                 "turn3_high": turn3_high, "qk_high": qk_high, "v_high": v_high, "exp": exp, "divide_take": divide_take, "o_high": o_high, "turn4_high": turn4_high}, act)

        @block.vector
        def _(dve):
            def steps(sem_):
                count = [0]

                def done(ins):
                    count[0] += 1
                    ins.then_inc(sem_, 1)
                    dve.wait_ge(sem_, count[0])
                return done, count

            def to_e4m3(v, m, dst, done):
                done(dve.tensor_scalar(m.bitcast(I32), v.bitcast(I32), 0x7F800000, None, ALU.bitwise_and))
                done(dve.tensor_scalar(m, m, 2.0 ** -6, 1.5 * 2.0 ** 20, ALU.max, ALU.mult))
                done(dve.tensor_tensor(v, v, m, ALU.add))
                done(dve.tensor_tensor(v, v, m, ALU.subtract))
                done(dve.tensor_scalar(m, v, 1.1 * 2.0 ** 119, 0.0, ALU.mult, ALU.mult))
                return dve.tensor_tensor(dst, v, m, ALU.add)

            for buf in (kz0[0], kz0[1], kz1[0], kz1[1]):
                dve.memset(buf[:], 0.0).then_inc(zeros_ok, 1)
            dve.memset(v_next[:, :, :, HD:HD + 1], 1.0).then_inc(const_ok, 1)

            def split_weights_low(b, _):
                for n, (hl, w_raw) in enumerate(((wkv, wkv_raw), (wq, wq_raw), (wp, wp_raw))):
                    dve.wait_ge(w16_hi, n + 1)
                    dve.scalar_tensor_tensor(hl[1][:], w_raw, WS, hl[0][:], ALU.mult, ALU.subtract).then_inc(w16_lo, 1)
                dve.wait_ge(masks_in, 3 * 16)

            def quantise_weights(b, _):
                dve.tensor_copy(ident16[:], ident[:]).then_inc(const_ok, 1)
                dve.tensor_copy(ident_bf[:], ident[:]).then_inc(const_ok, 1)
                dve.wait_ge(const_in, N_CONST * 16)
                done, count = steps(w8_step)
                dve.reciprocal(r_in[:], s_in[:])
                dve.tensor_tensor(s_both[:], s_in[:], s_k[:], ALU.mult)
                done(dve.reciprocal(r_k[:], s_k[:]))
                done(dve.tensor_scalar(w8a, w8_raw[:].rearrange("p k d -> p (k d)"), r_k[:, 0:1], None, ALU.mult))
                done(to_e4m3(w8a, w8b, w8[:].rearrange("p k d -> p (k d)"), done))
                assert count[0] == W8_STEPS

            def variance(x, bn6_, mv_, ve_, s_bn, s_mv, s_ve, n):
                for i in range(T):
                    ins = dve.bn_stats(bn6_[:, i, :], x[:, i, :])
                ins.then_inc(s_bn, 1)
                dve.wait_ge(s_bn, n)
                mean, diff, dev, sq = (mv_[:, i, :] for i in range(4))
                k = (n - 1) * 3
                dve.tensor_tensor(mean, bn6_[:, :, 1], bn6_[:, :, 4], ALU.add)
                dve.tensor_tensor(diff, bn6_[:, :, 1], bn6_[:, :, 4], ALU.subtract)
                dve.tensor_tensor(dev, bn6_[:, :, 2], bn6_[:, :, 5], ALU.add).then_inc(s_mv, 1)
                dve.wait_ge(s_mv, k + 1)
                dve.tensor_tensor(sq, diff, diff, ALU.mult)
                dve.tensor_scalar(mean, mean, 0.5, None, ALU.mult).then_inc(s_mv, 1)
                dve.wait_ge(s_mv, k + 2)
                dve.scalar_tensor_tensor(dev, sq, D / 4.0, dev, ALU.mult, ALU.add).then_inc(s_mv, 1)
                dve.wait_ge(s_mv, k + 3)
                dve.tensor_scalar(ve_[:], dev, 1.0 / D, EPS, ALU.mult, ALU.add).then_inc(s_ve, 1)

            def centre(x, dst, mv_, rs_, s_rs, s_out, n):
                dve.wait_ge(s_rs, n)
                for i in range(T):
                    ins = dve.tensor_scalar(dst[:, i, :], x[:, i, :], mv_[:, 0, i:i + 1], rs_[:, i:i + 1],
                                            ALU.subtract, ALU.mult)
                ins.then_inc(s_out, 1)

            def stats(b, j):
                if j == 0:
                    dve.wait_ge(x_in, (b + 1) * 16)
                    need(dve, ln_out, b * 3)
                if j == 1:
                    dve.wait_ge(r_add, (b + 1) * 16)
                if j == 2:
                    dve.wait_ge(ffn_x, (b + 1) * 2)
                variance(x_p, bn6, mv, ve, ln_bn, ln_mv, ln_ve, b * 3 + j + 1)

            def normalise(b, j):
                if j == 0:
                    need(dve, tr3, b * 2)
                if j == 2:
                    dve.wait_ge(rot_q, (b + 1) * 2)
                centre(x_p, x_b if j == 1 else x_n, mv, rstd, ln_rs, ln_out, b * 3 + j + 1)

            def rotate(b, _):
                if isinstance(b, int) and b == 0:
                    dve.wait_ge(q_table_in, 2 * 16)
                dve.wait_ge(ln_out, b * 3 + 1)
                need(dve, tr0, b * 4)
                need(dve, quant, b * QUANT_STEPS)
                two = lambda a: a[:].rearrange("p t (i two) -> p (t i) two", two=2)
                dve.tensor_tensor(q_r[:], x_n[:], q_cos[:], ALU.mult)
                for i in range(2):
                    ins = dve.tensor_tensor(two(q_s)[:, :, i], two(x_n)[:, :, 1 - i], two(q_sin)[:, :, i], ALU.mult)
                ins.then_inc(rot_q, 1)
                dve.wait_ge(rot_q, b * 2 + 1)
                dve.tensor_tensor(q_r[:], q_r[:], q_s[:], ALU.add).then_inc(rot_q, 1)

            def turn0_low(b, arg):
                half, w = arg
                dve.wait_ge(t0_hi, b * 4 + 2 * half + w + 1)
                dve.tensor_tensor(t0[w][1][:, half, :], bank("turn0", arg), t0[w][0][:, half, :],
                                  ALU.subtract).then_inc(t0_lo, 1)

            def state_sum(b, half):
                n = (b * 2 + half) * 5
                dve.wait_ge(upd, b * 2 + half + 1)
                need(dve, state_hi, b * 2 + half)
                need(dve, state_lo, b * 2 + half)
                u = bank("state", half).rearrange("p (c n) -> p c n", c=T)
                dve.tensor_tensor(state[:, 0], u[:, 0], chunk_decay[:, half], ALU.mult).then_inc(state_ok, 1)
                for c in range(1, T - 1):
                    dve.wait_ge(state_ok, n + 2 * c - 1)
                    dve.tensor_tensor(state[:, c], u[:, c], state[:, c - 1], ALU.add).then_inc(state_ok, 1)
                    dve.wait_ge(state_ok, n + 2 * c)
                    dve.tensor_tensor(state[:, c], state[:, c], chunk_decay[:, half], ALU.mult).then_inc(state_ok, 1)

            def state_low(b, half):
                dve.wait_ge(state_hi, b * 2 + half + 1)
                dve.tensor_tensor(state_s[1][:], state[:], state_s[0][:], ALU.subtract).then_inc(state_lo, 1)

            def r_mask_(b, arg):
                half, c = arg
                for g in range(2):
                    n = half * 8 + c * 2 + g
                    dve.wait_ge(r_sc, b * 16 + n + 1)
                    need(dve, r_hi, b * 16 + n - 1)
                    need(dve, r_lo, b * 16 + n - 1)
                    dve.tensor_tensor(rm[:, n % 2], bank("r_scores", arg, g).rearrange("p (h n) -> p h n", h=4),
                                      causal[:, None, :].to_broadcast([P, 4, P]), ALU.mult).then_inc(r_mask, 1)

            def r_add_(b, arg):
                half, c = arg
                dve.wait_ge(r_out, b * 8 + half * 4 + c + 1)
                xs = x_p[:, c, half * P:(half + 1) * P]
                for i in range(2):
                    dve.tensor_tensor(xs, bank("r_outs", arg)[:, i * P:(i + 1) * P], xs, ALU.add).then_inc(r_add, 1)
                    dve.wait_ge(r_add, b * 16 + (half * 4 + c) * 2 + i + 1)

            def quantise(b, i):
                count = [(0, 3, 5)[i]]

                def done(ins):
                    count[0] += 1
                    ins.then_inc(quant, 1)
                    dve.wait_ge(quant, b * QUANT_STEPS + count[0])
                v, m = flat(qa[:]), flat(qb[:])
                if i == 0:
                    dve.wait_ge(ln_out, b * 3 + 2)
                    dve.wait_ge(tr0, (b + 1) * 4)
                    done(dve.tensor_scalar(v, flat(x_b[:]), r_in[:, 0:1], None, ALU.mult))
                    done(dve.tensor_scalar(m.bitcast(I32), v.bitcast(I32), 0x7F800000, None, ALU.bitwise_and))
                    done(dve.tensor_scalar(m, m, 2.0 ** -6, 1.5 * 2.0 ** 20, ALU.max, ALU.mult))
                if i == 1:
                    done(dve.tensor_tensor(v, v, m, ALU.add))
                    done(dve.tensor_tensor(v, v, m, ALU.subtract))
                if i == 2:
                    done(dve.tensor_scalar(m, v, 1.1 * 2.0 ** 119, 0.0, ALU.mult, ALU.mult))
                    need(dve, xq_tr, b * 2)
                    done(dve.tensor_tensor(flat(x_q[:]), v, m, ALU.add))
                    assert count[0] == QUANT_STEPS

            def copy_q(b, _):
                for k in range(KD):
                    dve.wait_ge(xq_tr, b * 2 + k + 1)
                    need(dve, ffn_mm, b * 2)
                    dve.tensor_copy(xq_t[:, k, :], bank("turn_q", 0, k)[:, 0:256].bitcast(BF16)).then_inc(xq_cp, 1)

            def linear_add(b, _):
                for u in range(2):
                    n = b * 2 + u + 1
                    dve.wait_ge(ffn_mm, n)
                    need(dve, ffn_b, n - 1)
                    dve.tensor_scalar(y_a[:].rearrange("p t d -> p (t d)"), bank("linear", 0, u),
                                      s_both[:, 0:1], None, ALU.mult).then_inc(ffn_y, 1)
                    dve.wait_ge(ffn_y, n)
                    need(dve, ffn_x, n - 1)
                    dve.tensor_tensor(y_b[:], y_a[:], bias0[:, None, :].to_broadcast([P, 2, D]),
                                      ALU.add).then_inc(ffn_b, 1)
                    dve.wait_ge(ffn_b, n)
                    xs = x_p[:, 2 * u:2 * u + 2, :]
                    dve.tensor_tensor(xs, xs, y_b[:], ALU.add).then_inc(ffn_x, 1)

            def turn3_low(b, k):
                dve.wait_ge(t3_hi, b * 2 + k + 1)
                dve.tensor_tensor(x3[1][:, k, :], bank("turn3", k), x3[0][:, k, :], ALU.subtract).then_inc(t3_lo, 1)

            def qk_low(b, n):
                dve.wait_ge(qk_hi, b * 4 + n + 1)
                dve.scalar_tensor_tensor(t1[1][:, n % 2, :], bank("qk", n), 1 / WS, t1[0][:, n % 2, :],
                                         ALU.mult, ALU.subtract).then_inc(qk_lo, 1)

            def v_low(b, u):
                dve.wait_ge(v_hi, b * 2 + u + 1)
                part = lambda col: v_next[:, 2 * u:2 * u + 2, :, col:col + HD].rearrange("p t h d -> p (t h) d")
                dve.scalar_tensor_tensor(part(HD + 1), bank("v", u).rearrange("p (a d) -> p a d", d=HD), 1 / WS,
                                         part(0), ALU.mult, ALU.subtract).then_inc(v_lo, 1)

            def maxima(b, arg):
                half, h, g = arg
                for i in range(2):
                    qt = 2 * g + i
                    dve.wait_ge(m_sc, b * 64 + half * 32 + h * T + qt + 1)
                    if h == 0 and qt == 0:
                        need(dve, m_16, b * 4 + half * 2)
                    dve.tensor_reduce(neg_max[:, qt, h % 2, h // 2:h // 2 + 1], bank("maxima", arg, i), AX.X,
                                      ALU.max, negate=True).then_inc(m_max, 1)

            def max_split(b, half):
                dve.wait_ge(m_max, b * 64 + half * 32 + 32)
                need(dve, m_tr, b * 2 + half)
                dve.tensor_copy(max16[:, :, :, 0, :], neg_max[:]).then_inc(m_16, 1)
                dve.wait_ge(m_16, b * 4 + half * 2 + 1)
                dve.tensor_tensor(max16[:, :, :, 1, :], neg_max[:], max16[:, :, :, 0, :],
                                  ALU.subtract).then_inc(m_16, 1)

            def max_copy(b, half):
                dve.wait_ge(m_tr, b * 2 + half + 1)
                need(dve, m_out, (b * 2 + half) * 16)
                dve.tensor_copy(max_t[:], bank("max_turn", half)[0:4 * HP, 0:256].bitcast(F16)).then_inc(m_cp, 1)

            def split_p(b, arg):
                if high_by_dve(b, arg[1]):
                    h, g = arg
                    dve.wait_ge(s_exp, b * 64 + h * 4 + 2 * g + 2)
                    need(dve, pv_mm, b * 16 + h - 1)
                    dve.tensor_copy(ph[:, h % 2, 2 * g:2 * g + 2, :], p32[:, g]).then_inc(p_hi, 1)
                if by_dve(b, *arg):
                    low_of_p(dve, b, arg)

            def take_v(b, _):
                need(dve, pv_mm, b * 16)
                dve.wait_ge(v_lo, (b + 1) * 2)
                for tiles in (slice(0, T // 2), slice(T // 2, T)):
                    dve.tensor_copy(v_cur[:, tiles], v_next[:, tiles]).then_inc(v_cp, 1)

            def divide(b, g):
                dve.wait_ge(pv_mm, b * 16 + 2 * g + 2)
                need(dve, o_mul, b * 8 + g)
                o = pv[:, g % 2, 0:2 * T * VW].rearrange("p (h q d) -> p h q d", h=2, q=T)
                dve.wait_ge(o_take, b * 8 + g + 1)
                dve.reciprocal(rden[:], o[:, :, :, HD]).then_inc(o_rec, 1)
                dve.tensor_tensor(o_part[:], o[:, :, :, 0:HD], o_part[:], ALU.add).then_inc(o_sum, 1)
                if g == 0:
                    need(dve, o_tr, b * 2)
                dve.wait_ge(o_rec, b * 8 + g + 1)
                dve.wait_ge(o_sum, b * 8 + g + 1)
                dst = o_n[:].rearrange("p q (g h d) -> p g h q d", g=8, h=2)[:, g]
                dve.tensor_tensor(dst, o_part[:], rden[:, :, :, None].to_broadcast([P, 2, T, HD]),
                                  ALU.mult).then_inc(o_mul, 1)

            def x_bias_(b, _):
                dve.wait_ge(x_back, (b + 1) * 16)
                dve.tensor_tensor(x_a[:], x_a[:], biasp[:, None, :].to_broadcast([P, T, D]), ALU.add).then_inc(x_bias, 1)

            def o_low(b, k):
                dve.wait_ge(o_hi, b * 2 + k + 1)
                dve.tensor_tensor(o_t[1][:, k, :], bank("o_turn", k), o_t[0][:, k, :], ALU.subtract).then_inc(o_lo, 1)

            def o_add(b, u):
                dve.wait_ge(x_bias, b + 1)
                dve.wait_ge(pr_mm, b * 2 + u + 1)
                xs = x_a[:, 2 * u:2 * u + 2, :].rearrange("p t d -> p (t d)")
                dve.scalar_tensor_tensor(xs, bank("o_proj", u), 1 / WS, xs, ALU.mult, ALU.add).then_inc(pr_x, 1)

            def stats_a(b, _):
                dve.wait_ge(pr_x, (b + 1) * 2)
                variance(x_a, bn6_a, mv_a, ve_a, la_bn, la_mv, la_ve, b + 1)

            def normalise_a(b, _):
                if not (isinstance(b, int) and b + 2 > LAST):
                    dve.wait_ge(tr3, (b + 3) * 2)
                centre(x_a, x_n, mv_a, rstd_a, la_rs, la_out, b + 1)

            def turn4_low(b, k):
                dve.wait_ge(t4_hi, b * 2 + k + 1)
                dve.tensor_tensor(o_t[1][:, k, :], bank("turn4", k), o_t[0][:, k, :], ALU.subtract).then_inc(t4_lo, 1)

            run({"split_weights_low": split_weights_low, "quantise_weights": quantise_weights,
                 "stats": stats, "normalise": normalise, "rotate": rotate, "turn0_low": turn0_low,
                 "state_sum": state_sum, "state_low": state_low, "r_mask": r_mask_, "r_add": r_add_,
                 "quantise": quantise, "copy_q": copy_q, "linear_add": linear_add, "turn3_low": turn3_low,
                 "qk_low": qk_low, "v_low": v_low, "maxima": maxima, "max_split": max_split, "max_copy": max_copy,
                 "split_p": split_p, "take_v": take_v, "divide": divide, "x_bias": x_bias_, "o_low": o_low, "o_add": o_add,
                 "stats_a": stats_a, "normalise_a": normalise_a, "turn4_low": turn4_low}, dve)

        @block.tensor
        def _(pe):
            pe.wait_ge(masks_in, 3 * 16)

            def split_weights_low(b, _):
                pe.wait_ge(w16_lo, 3)

            def quantise_weights(b, _):
                pe.wait_ge(const_ok, CONSTS)
                pe.wait_ge(w8_step, W8_STEPS)

            THREE = ((0, 0), (0, 1), (1, 0))

            read = {"misc": [None, None], "sc": [None, None]}

            def take(name, arg, read_by, i=0):
                last = read[bank_no[name, arg][0]]
                if last[0] is not None:
                    pe.wait_ge(*last[0])
                last[:] = [last[1], read_by]
                return bank(name, arg, i)

            def banks(b, _):
                read["misc"][:] = [(qk_lo, b * 4 + 3), (qk_lo, b * 4 + 4)]
                read["sc"][:] = [(m_max, b * 64 + 32), (m_cp, b * 2 + 1)]

            def turn(to, src, col):
                for i in range(T):
                    ins = pe.transpose(to[:, i * P:(i + 1) * P], src[:, i, col * P:(col + 1) * P], ident[:])
                return ins

            def turn0(b, arg):
                half, w = arg
                to = take("turn0", arg, (t0_lo, b * 4 + 2 * half + w + 1))
                pe.wait_ge(rot_q if w == 0 else rot_k, (b + 1) * 2)
                turn(to, q_r if w == 0 else k_r, half).then_inc(tr0, 1)

            def state_(b, half):
                to = take("state", half, (state_ok, (b * 2 + half) * 5 + 5))
                pe.wait_ge(rot_k, (b + 1) * 2)
                for c in range(T - 1):
                    cols = slice(half * P, (half + 1) * P)
                    ins = pe.matmul(to[:, c * P:(c + 1) * P], k_r[:, c, cols], ctx_n[:, c, cols],
                                    start=True, stop=True)
                ins.then_inc(upd, 1)

            def r_scores(b, arg):
                half, c = arg
                if c == 0:
                    pe.wait_ge(st0_in, (b * 2 + half + 1) * 12 * 16)
                tok = slice(c * P, (c + 1) * P)
                for g in range(2):
                    n = half * 8 + c * 2 + g
                    to = take("r_scores", arg, (r_mask, b * 16 + n + 1), g)
                    for i in range(4):
                        pair, par = 2 * g + i // 2, i % 2
                        ins = pe.matmul(to[:, i * P:(i + 1) * P], kz0[par][0:KR, pair, tok], sq0[0:KR, pair, tok],
                                        start=True, stop=True)
                    ins.then_inc(r_sc, 1)

            def r_outs(b, arg):
                half, c = arg
                tok = slice(c * P, (c + 1) * P)
                to = take("r_outs", arg, (r_add, b * 16 + (half * 4 + c) * 2 + 2))
                first = True
                if c:
                    pe.wait_ge(state_lo, b * 2 + half + 1)
                    for qi, si in THREE:
                        pe.matmul(to[:, 0:P], t0[0][qi][:, half, tok], state_s[si][:, c - 1, :],
                                  start=first, stop=False, skip_group_check=True)
                        first = False
                if c == 0 and half == 0:
                    pe.wait_ge(v0_lo, b + 1)
                for h in range(HH):
                    if h % 4 == 0:
                        pe.wait_ge(r_lo, b * 16 + half * 8 + c * 2 + h // 4 + 1)
                    col = half * P + h * HD
                    for si, parts in ((0, 2), (1, 1)):
                        o = to[:, 0:2 * P].rearrange("p (v n) -> p v n", v=2)[:, 0:parts, h * HD:(h + 1) * HD]
                        ins = pe.matmul(o, rs[si][:, c % 2, h, :], v0[:, c, 0:parts, col:col + HD],
                                        start=first, stop=True, skip_group_check=True)
                        first = False
                ins.then_inc(r_out, 1)

            def turn_q(b, _):
                pe.wait_ge(quant, (b + 1) * QUANT_STEPS)
                for k in range(KD):
                    to = take("turn_q", 0, (xq_cp, b * 2 + k + 1), k)
                    for i in range(T):
                        ins = pe.transpose(to[:, i * 64:(i + 1) * 64].bitcast(BF16), x_q[:, i, k * P:(k + 1) * P],
                                           ident_bf[:])
                    ins.then_inc(xq_tr, 1)

            def linear(b, _):
                for u in range(2):
                    to = take("linear", 0, (ffn_y, b * 2 + u + 1), u)
                    pe.wait_ge(xq_cp, (b + 1) * 2)
                    for i in range(2):
                        tok = slice((2 * u + i) * P, (2 * u + i + 1) * P)
                        for k in range(KD):
                            ins = pe.matmul(to[:, i * D:(i + 1) * D], xq_t[:, k, tok], w8[:, k, :],
                                            start=(k == 0), stop=(k == KD - 1))
                    ins.then_inc(ffn_mm, 1)

            def turn3(b, k):
                to = take("turn3", k, (t3_lo, b * 2 + k + 1))
                pe.wait_ge(ln_out, (b + 1) * 3)
                turn(to, x_n, k).then_inc(tr3, 1)

            def qk(b, n):
                w, m = 1 - n // 2, n % 2
                to = take("qk", n, (qk_lo, b * 4 + n + 1))
                pe.wait_ge(*((t3_lo, (b + 1) * 2) if w == 0 else (c3_lo, b + 1)))
                src, wt = (x3, wq) if w == 0 else (c3, wkv)
                for j, (wi, xi) in enumerate(THREE):
                    for k in range(KD):
                        ins = pe.matmul(to, wt[wi][:, k, m * P:(m + 1) * P], src[xi][:, k, :],
                                        start=(j == 0 and k == 0), stop=(j == 2 and k == KD - 1))
                ins.then_inc(qk_mm, 1)

            def v(b, u):
                to = take("v", u, (v_lo, b * 2 + u + 1))
                for i in range(2):
                    tok = slice((2 * u + i) * P, (2 * u + i + 1) * P)
                    for j, (xi, wi) in enumerate(THREE):
                        for k in range(KD):
                            ins = pe.matmul(to[:, i * D:(i + 1) * D], c3[xi][:, k, tok], wkv[wi][:, k, D:2 * D],
                                            start=(j == 0 and k == 0), stop=(j == 2 and k == KD - 1))
                ins.then_inc(v_mm, 1)

            def maxima(b, arg):
                half, h, g = arg
                if h == 0 and g == 0:
                    pe.wait_ge(st1_in[half], (b + 1) * 12 * 16)
                for i in range(2):
                    qt = 2 * g + i
                    to = take("maxima", arg, (m_max, b * 64 + half * 32 + h * T + qt + 1), i)
                    pe.matmul(to, sq1[0:KR, half, h // 2, qt * P:(qt + 1) * P], kz1[h % 2][0:KR, half, h // 2, :],
                              start=True, stop=True).then_inc(m_sc, 1)

            def max_turn(b, half):
                to = take("max_turn", half, (m_cp, b * 2 + half + 1))
                pe.wait_ge(m_16, b * 4 + half * 2 + 2)
                for qt in range(T):
                    ins = pe.transpose(to[0:4 * HP, qt * 64:(qt + 1) * 64].bitcast(F16),
                                       max16[:, qt].rearrange("p r l q -> p (r l q)"), ident16[:])
                ins.then_inc(m_tr, 1)

            def score(b, arg):
                h, g = arg
                half, pair, par = h // HH, (h % HH) // 2, h % 2
                if h % HH == 0 and g == 0:
                    pe.wait_ge(m_in[half], (b + 1) * 16)
                    if half == 0:
                        pe.wait_ge(rows_in, 2 * 16)
                for kt in range(2 * g, 2 * g + 2):
                    need(pe, s_exp, b * 64 + h * 4 + kt - 1)
                    pe.matmul(st[:, kt % 2, :], kz1[par][0:MR, half, pair, kt * P:(kt + 1) * P],
                              sq1[0:MR, half, pair, :], start=True, stop=True).then_inc(s_mm, 1)

            def values(b, arg):
                h, part = arg
                g = h // 2
                if h % 2 == 0 and part == 0:
                    need(pe, o_mul, b * 8 + g - 1)
                if h == 0 and part == 0:
                    pe.wait_ge(v_cp, (b + 1) * 2)
                if part == 0:
                    for g2 in range(2):
                        pe.wait_ge(*split_done(b, h, g2))
                o = pv[:, g % 2, 0:2 * T * VW].rearrange("p (h q d) -> p h q d", h=2, q=T)
                for qt in range(2 * part, 2 * part + 2):
                    for kt in range(T):
                        for p16, cols in ((ph, VW), (pl, HD + 1)):
                            ins = pe.matmul(o[:, h % 2, qt, 0:cols], p16[:, h % 2, kt, qt * P:(qt + 1) * P],
                                            v_cur[:, kt, h, 0:cols], start=(kt == 0 and p16 is ph),
                                            stop=(kt == T - 1), skip_group_check=True)
                if part == 1:
                    ins.then_inc(pv_mm, 1)

            def o_turn(b, k):
                to = take("o_turn", k, (o_lo, b * 2 + k + 1))
                pe.wait_ge(o_mul, (b + 1) * 8)
                turn(to, o_n, k).then_inc(o_tr, 1)

            def o_proj(b, u):
                to = take("o_proj", u, (pr_x, b * 2 + u + 1))
                pe.wait_ge(o_lo, (b + 1) * 2)
                for i in range(2):
                    tok = slice((2 * u + i) * P, (2 * u + i + 1) * P)
                    for j, (oi, wi) in enumerate(THREE):
                        for k in range(KD):
                            ins = pe.matmul(to[:, i * D:(i + 1) * D], o_t[oi][:, k, tok], wp[wi][:, k, :],
                                            start=(j == 0 and k == 0), stop=(j == 2 and k == KD - 1))
                ins.then_inc(pr_mm, 1)

            def turn4(b, k):
                to = take("turn4", k, (t4_lo, b * 2 + k + 1))
                pe.wait_ge(la_out, b + 1)
                turn(to, x_n, k).then_inc(tr4, 1)

            run({"split_weights_low": split_weights_low, "quantise_weights": quantise_weights,
                 "banks": banks, "turn0": turn0, "state": state_, "r_scores": r_scores, "r_outs": r_outs,
                 "turn_q": turn_q, "linear": linear, "turn3": turn3, "qk": qk, "v": v, "maxima": maxima,
                 "max_turn": max_turn, "score": score, "values": values, "o_turn": o_turn, "o_proj": o_proj,
                 "turn4": turn4}, pe)


N_CONST = 5
CONSTS = 3
W8_STEPS = 8
QUANT_STEPS = 7


def phase_m(nc, t, out, x_d, xt_d, raw, raw_b, w_in, load_w):
    with ExitStack() as ctx:
        def sb(name, shape, dt=F32):
            return ctx.enter_context(nc.sbuf_tensor(name, shape, dt))

        def sem(name):
            return ctx.enter_context(nc.semaphore(name))

        N = B * S
        CH = N // 512
        U = CH * IT
        GU, DN = KD * 2 * I, IT * D
        WSTEP = 1024
        WP = (GU + DN) // WSTEP
        LAG = 2
        PE_LAG = 3

        x_all = sb("x_all", [P, NT, D])
        xt = [sb(f"xt{i}", [P, B, KD, S], F16) for i in range(2)]
        ident, before = sb("ident_m", [P, P]), sb("before", [P, E, E])
        wr_raw = sb("wr_raw", [P, KD, E])
        wr = [sb(f"wr{i}", [P, KD, E], F16) for i in range(2)]
        bias_r, bias_d = sb("bias_r", [P, E]), sb("bias_d", [E, D])
        logit = sb("logit", [P, NT, E])
        above, equal = sb("above", [P, NT, E * E]), sb("equal", [P, NT, E * E])
        rank, top, expo = sb("rank", [P, NT, E]), sb("top", [P, NT]), sb("expo", [P, NT, E])
        total, combine = sb("total", [P, NT]), sb("combine", [P, NT, E])
        scaled = sb("scaled", [P, E, NT])
        combine_t = sb("combine_t", [E, N])
        w = [[sb(f"w_{e}{i}", [P, GU + DN], F16) for i in range(2)] for e in range(2)]
        bias16, share = sb("bias16", [P, 2, 8]), sb("share", [P, 2, NT])
        gate, up = sb("gate", [P, 2, 512]), sb("up", [P, 2, 512])
        glu, prod = sb("glu", [P, 2, 512]), sb("prod", [P, 2, 512])
        h16 = [sb(f"h16_{i}", [P, 4, 512], F16) for i in range(2)]

        gu_ps = ctx.enter_context(nc.psum_tensor("gu_ps", [P, 4, 512], F32))
        dn_ps = ctx.enter_context(nc.psum_tensor("dn_ps", [P, 4, 512], F32))

        const_in = sem("m_const_in")
        x_in = [sem(f"m_x_in{b}") for b in range(B)]
        wr_in = sem("wr_in")
        wr_hi, wr_lo = sem("wr_hi"), sem("wr_lo")
        rt_mm = sem("rt_mm")
        rt = sem("rt")
        rt_exp = sem("rt_exp")
        ct_tr, ct_cp = sem("ct_tr"), sem("ct_cp")
        bd_mm, bd_x = sem("bd_mm"), sem("bd_x")
        w_hi, w_lo = sem("w_hi"), sem("w_lo")
        w_bias, w_share = sem("w_bias"), sem("w_share")
        gate_mm, up_mm = sem("gate_mm"), sem("up_mm")
        gate_ok, glu_ok, up_ok, prod_ok = sem("gate_ok"), sem("glu_ok"), sem("up_ok"), sem("prod_ok")
        h_hi, h_lo = sem("h_hi"), sem("h_lo")
        dn_mm, dn_x = sem("dn_mm"), sem("dn_x")
        y_out = sem("y_out")
        N_CONST_M = 5

        def moe(run_expert):
            def emit(engine, loop=True):
                for k in range(2):
                    run_expert(k, k, False)
                if loop:
                    with engine.Fori(1, E // 2 - 1) as i:
                        for k in range(2):
                            run_expert(2 * i + k, k, False)
                else:
                    for e in range(2, E - 2):
                        run_expert(e, e % 2, False)
                for k in range(2):
                    run_expert(E - 2 + k, k, k == 1)
            return emit

        block = ctx.enter_context(nc.Block())

        @block.sync
        def _(sp):
            sp.dma_start(wr_raw[:], t["wr_t"].rearrange("(k p) e -> p k e", k=KD)).then_inc(wr_in, 16)
            for b in range(B):
                for hl in range(2):
                    sp.dma_start(xt[hl][:, b], xt_d[hl, b]).then_inc(x_in[b], 16)
            sp.dma_start(ident[:], t["ident"]).then_inc(const_in, 16)
            sp.dma_start(before[:], t["before"]).then_inc(const_in, 16)
            sp.dma_start(bias_r[:], t["L1_ffn_router_bias"][None, :].to_broadcast([P, E])).then_inc(const_in, 16)
            sp.dma_start(bias_d[:], t["L1_ffn_down_proj_bias"]).then_inc(const_in, 16)
            sp.dma_start(x_all[:], x_d.rearrange("t p d -> p t d")).then_inc(const_in, 16)

            def after(e):
                sp.wait_ge(w_lo, (e + 1) * WP)
                sp.wait_ge(w_bias, (e + 1) * 2)

            def expert(e, k, last):
                if not last:
                    after(e)
                    load_w(sp, e + 1)

            moe(expert)(sp, loop=False)
            for c in range(CH):
                sp.wait_ge(dn_x, (E - 1) * NT + 4 * c + 4)
                sp.dma_start(out.rearrange("(c t p) d -> c p t d", c=CH, t=4)[c],
                             x_all[:, 4 * c:4 * c + 4, :]).then_inc(y_out, 16)
            sp.wait_ge(y_out, CH * 16)

        def pieces():
            return [slice(i * WSTEP, (i + 1) * WSTEP) for i in range(WP)]

        @block.scalar
        def _(act):
            def split(e, k, i):
                if i == 0:
                    act.wait_ge(w_in, (e + 1) * 3 * 16)
                    need(act, dn_mm, (e - 1) * U)
                act.activation(w[k][0][:, pieces()[i]], raw[:, pieces()[i]], ACT.Copy, scale=WS).then_inc(w_hi, 1)

            def unit(e, k, u):
                n = e * U + u
                act.wait_ge(gate_ok, n + 1)
                need(act, prod_ok, n - 1)
                act.activation(glu[:, u % 2, :], gate[:, u % 2, :], ACT.Gelu_apprx_sigmoid,
                               scale=1 / WS).then_inc(glu_ok, 1)
                act.wait_ge(prod_ok, n + 1)
                need(act, dn_mm, n - 3)
                act.activation(h16[0][:, u % 4, :], prod[:, u % 2, :], ACT.Copy).then_inc(h_hi, 1)

            for i in range(WP):
                split(0, 0, i)
            act.wait_ge(wr_in, 16)
            act.activation(wr[0][:], wr_raw[:], ACT.Copy, scale=WS).then_inc(wr_hi, 1)
            for u in range(LAG):
                unit(0, 0, u)
            act.wait_ge(rt, RT_SUB)
            act.activation(expo[:], expo[:], ACT.Exp).then_inc(rt_exp, 1)

            def expert(e, k, last):
                for u in range(U):
                    if not last and u in SPLIT_AT:
                        split(e + 1, 1 - k, SPLIT_AT.index(u))
                    if u + LAG < U:
                        unit(e, k, u + LAG)
                    elif not last:
                        unit(e + 1, 1 - k, u + LAG - U)

            moe(expert)(act)

        @block.gpsimd
        def _(pool):
            def unit(e, k, u):
                n = e * U + u
                pool.wait_ge(h_hi, n + 1)
                pool.tensor_tensor(h16[1][:, u % 4, :], prod[:, u % 2, :], h16[0][:, u % 4, :],
                                   ALU.subtract).then_inc(h_lo, 1)

            for u in range(LAG):
                unit(0, 0, u)

            def expert(e, k, last):
                for u in range(U):
                    if u + LAG < U:
                        unit(e, k, u + LAG)
                    elif not last:
                        unit(e + 1, 1 - k, u + LAG - U)

            moe(expert)(pool)

        @block.vector
        def _(dve):
            count = [0]

            def done(ins):
                count[0] += 1
                ins.then_inc(rt, 1)
                dve.wait_ge(rt, count[0])

            def split(e, k, i):
                dve.wait_ge(w_hi, e * WP + i + 1)
                dve.scalar_tensor_tensor(w[k][1][:, pieces()[i]], raw[:, pieces()[i]], WS, w[k][0][:, pieces()[i]],
                                         ALU.mult, ALU.subtract).then_inc(w_lo, 1)
                if i == 0:
                    need(dve, up_ok, (e - 1) * U)
                    dve.tensor_scalar(bias16[:, k, 0:4], raw_b[:, 0, 0:4], WS, None, ALU.mult).then_inc(w_bias, 1)
                    dve.tensor_scalar(bias16[:, k, 4:8], raw_b[:, 0, 4:8], WS, WS, ALU.mult, ALU.add).then_inc(w_bias, 1)
                    if not (isinstance(e, int) and e == 0):
                        take_share(e, k)

            def take_share(e, k):
                dve.tensor_copy(share[:, k:k + 1, :], scaled[:, bass.ds(e, 1), :]).then_inc(w_share, 1)

            def unit(e, k, u):
                n = e * U + u
                it = u % IT
                dve.wait_ge(gate_mm, n + 1)
                if u == 0:
                    dve.wait_ge(w_bias, (e + 1) * 2)
                need(dve, glu_ok, n - 1)
                dve.tensor_scalar(gate[:, u % 2, :], gu_ps[:, 2 * (u % 2), :], bias16[:, k, it:it + 1], WS * LIMIT,
                                  ALU.add, ALU.min).then_inc(gate_ok, 1)
                dve.wait_ge(up_mm, n + 1)
                dve.tensor_scalar(up[:, u % 2, :], gu_ps[:, 2 * (u % 2) + 1, :], bias16[:, k, 4 + it:5 + it],
                                  WS * (LIMIT + 1), ALU.add, ALU.min).then_inc(up_ok, 1)
                dve.wait_ge(up_ok, n + 1)
                dve.wait_ge(glu_ok, n + 1)
                need(dve, h_hi, n - 1)
                need(dve, h_lo, n - 1)
                dve.scalar_tensor_tensor(prod[:, u % 2, :], up[:, u % 2, :], WS * (1 - LIMIT), glu[:, u % 2, :],
                                         ALU.max, ALU.mult).then_inc(prod_ok, 1)

            def collect(e, k, c):
                dve.wait_ge(dn_mm, e * U + IT * (c + 1))
                if c == 0:
                    dve.wait_ge(w_share, e + 1)
                    need(dve, dn_x, e * NT)
                for i in range(4):
                    tile = 4 * c + i
                    xs = x_all[:, tile, :]
                    dve.scalar_tensor_tensor(xs, dn_ps[:, 2 * (c % 2) + i // 2, (i % 2) * D:(i % 2 + 1) * D],
                                             share[:, k, tile:tile + 1], xs, ALU.mult, ALU.add).then_inc(dn_x, 1)

            for i in range(WP):
                split(0, 0, i)
            dve.wait_ge(wr_hi, 1)
            dve.scalar_tensor_tensor(wr[1][:], wr_raw[:], WS, wr[0][:], ALU.mult, ALU.subtract).then_inc(wr_lo, 1)

            for u in range(LAG):
                unit(0, 0, u)

            dve.wait_ge(const_in, N_CONST_M * 16)
            dve.wait_ge(rt_mm, 1)
            flat = lambda a: a[:].rearrange("p t e -> p (t e)")
            per_expert = lambda a: a[:].to_broadcast([P, NT, E])
            done(dve.tensor_scalar(flat(logit), dn_ps[:, 0, 0:NT * E], 1 / WS, None, ALU.mult))
            done(dve.tensor_tensor(logit[:], logit[:], bias_r[:, None, :].to_broadcast([P, NT, E]), ALU.add))
            square = lambda a: a[:].rearrange("p t (i j) -> p t i j", i=E)
            this, other = logit[:, :, :, None].to_broadcast([P, NT, E, E]), logit[:, :, None, :].to_broadcast([P, NT, E, E])
            dve.tensor_tensor(square(above), other, this, ALU.is_gt)
            done(dve.tensor_tensor(square(equal), other, this, ALU.is_equal))
            done(dve.tensor_tensor(equal[:], equal[:], before[:].rearrange("p i j -> p (i j)")[:, None, :]
                                   .to_broadcast([P, NT, E * E]), ALU.mult))
            done(dve.tensor_tensor(above[:], above[:], equal[:], ALU.add))
            done(dve.tensor_reduce(rank[:], square(above), AX.X, ALU.add))
            dve.tensor_scalar(rank[:], rank[:], TOPK - 0.5, None, ALU.is_lt)
            done(dve.tensor_reduce(top[:], logit[:], AX.X, ALU.max))
            done(dve.tensor_tensor(expo[:], logit[:], top[:, :, None].to_broadcast([P, NT, E]), ALU.subtract))
            assert count[0] == RT_SUB
            dve.wait_ge(rt_exp, 1)
            done(dve.tensor_tensor(expo[:], expo[:], rank[:], ALU.mult))
            done(dve.tensor_reduce(total[:], expo[:], AX.X, ALU.add))
            done(dve.reciprocal(total[:], total[:]))
            done(dve.tensor_tensor(combine[:], expo[:], total[:, :, None].to_broadcast([P, NT, E]), ALU.mult))
            done(dve.tensor_scalar(scaled[:].rearrange("p e t -> p t e"), combine[:], 1 / (WS * WS), None, ALU.mult))
            assert count[0] == RT_STEPS
            for c in range(4):
                dve.wait_ge(ct_tr, c + 1)
                dve.tensor_copy(combine_t[:, c * 512:(c + 1) * 512], dn_ps[0:E, c, :]).then_inc(ct_cp, 1)
            for u in range(NT // 2):
                dve.wait_ge(bd_mm, u + 1)
                xs = x_all[:, 2 * u:2 * u + 2, :].rearrange("p t d -> p (t d)")
                dve.tensor_tensor(xs, dn_ps[:, u % 4, :], xs, ALU.add).then_inc(bd_x, 1)
            dve.wait_ge(bd_x, NT // 2)

            take_share(0, 0)

            def expert(e, k, last):
                for u in range(U):
                    if not last and u in SPLIT_AT:
                        split(e + 1, 1 - k, SPLIT_AT.index(u))
                    if u + LAG < U:
                        unit(e, k, u + LAG)
                    elif not last:
                        unit(e + 1, 1 - k, u + LAG - U)
                    if u % IT == IT - 1:
                        collect(e, k, u // IT)

            moe(expert)(dve)

        @block.tensor
        def _(pe):
            THREE = ((0, 0), (0, 1), (1, 0))
            def gate_up(e, k, u):
                n = e * U + u
                c, it = u // IT, u % IT
                if u == 0:
                    pe.wait_ge(w_lo, (e + 1) * WP)
                for g, (mm, ok) in enumerate(((gate_mm, gate_ok), (up_mm, up_ok))):
                    need(pe, ok, n - 1)
                    for j, (wi, xi) in enumerate(THREE):
                        for kd in range(KD):
                            col = kd * 2 * I + g * I + it * P
                            ins = pe.matmul(gu_ps[:, 2 * (u % 2) + g, :], w[k][wi][:, col:col + P], xt[xi][:, c, kd, :],
                                            start=(j == 0 and kd == 0), stop=(j == 2 and kd == KD - 1))
                    ins.then_inc(mm, 1)

            def down(e, k, u):
                c, it = u // IT, u % IT
                pe.wait_ge(h_lo, e * U + u + 1)
                if it == 0:
                    need(pe, dn_x, e * NT + 4 * (c - 1))
                    if isinstance(e, int) and e == 0 or c == 0:
                        pe.wait_ge(bd_x, NT // 2)
                for i in range(4):
                    for j, (hi, wi) in enumerate(THREE):
                        ins = pe.matmul(dn_ps[:, 2 * (c % 2) + i // 2, (i % 2) * D:(i % 2 + 1) * D],
                                        h16[hi][:, u % 4, i * P:(i + 1) * P],
                                        w[k][wi][:, GU + it * D:GU + (it + 1) * D],
                                        start=(it == 0 and j == 0 and i % 2 == 0), stop=(it == IT - 1 and j == 2),
                                        skip_group_check=True)
                ins.then_inc(dn_mm, 1)

            pe.wait_ge(x_in[0], 2 * 16)
            for u in range(LAG):
                gate_up(0, 0, u)
            for b in range(1, B):
                pe.wait_ge(x_in[b], 2 * 16)
            pe.wait_ge(wr_lo, 1)
            for tile in range(NT):
                b, tok = tile // T, slice((tile % T) * P, (tile % T + 1) * P)
                for j, (xi, wi) in enumerate(THREE):
                    for k in range(KD):
                        ins = pe.matmul(dn_ps[:, 0, tile * E:(tile + 1) * E], xt[xi][:, b, k, tok], wr[wi][:, k, :],
                                        start=(j == 0 and k == 0), stop=(j == 2 and k == KD - 1))
            ins.then_inc(rt_mm, 1)
            for u in range(LAG, PE_LAG):
                gate_up(0, 0, u)
            pe.wait_ge(rt, RT_STEPS)
            for c in range(4):
                for i in range(4):
                    ins = pe.transpose(dn_ps[0:E, c, i * P:(i + 1) * P], combine[:, 4 * c + i, :], ident[:])
                ins.then_inc(ct_tr, 1)
            for u in range(NT // 2):
                if u < 4:
                    pe.wait_ge(ct_cp, 4)
                else:
                    pe.wait_ge(bd_x, u - 3)
                for i in range(2):
                    tile = 2 * u + i
                    ins = pe.matmul(dn_ps[:, u % 4, i * D:(i + 1) * D], combine_t[:, tile * P:(tile + 1) * P], bias_d[:],
                                    start=True, stop=True)
                ins.then_inc(bd_mm, 1)

            def expert(e, k, last):
                for u in range(U):
                    if u + PE_LAG < U:
                        gate_up(e, k, u + PE_LAG)
                    elif not last:
                        gate_up(e + 1, 1 - k, u + PE_LAG - U)
                    down(e, k, u)

            moe(expert)(pe)


RT_SUB, RT_STEPS = 8, 13
SPLIT_AT = [3, 6, 9]


_INS = ["x", "ctx", "ctx_swapped", "ctx_t", "L0_ffn_kernel", "L0_ffn_input_scale", "L0_ffn_kernel_scale",
        "L0_ffn_bias", "wq_t", "wkv_t", "wp_t", "L1_xattn_bproj", "wr_t", "L1_ffn_router_bias", "gate_up_t",
        "gate_up_bias_t", "down_t", "L1_ffn_down_proj_bias"]


def kernel(**inputs):
    import concourse.bacc as bacc
    from concourse.bass_utils import run_bass_kernel_spmd

    a = {k: np.asarray(v) for k, v in inputs.items()}
    flat = a["ctx_1024"].reshape(B * S, D)
    a["x"] = a["x"].reshape(B * S, D)
    a["ctx"] = flat
    a["ctx_swapped"] = flat.reshape(B * S, D // 2, 2)[:, :, ::-1].reshape(B * S, D)
    a["ctx_t"] = flat.T
    a["wq_t"], a["wkv_t"], a["wp_t"] = a["L1_xattn_Wq"].T, a["L1_xattn_Wkv"].T, a["L1_xattn_Wproj"].T
    a["wr_t"] = a["L1_ffn_router_weight"].T
    a["gate_up_t"] = a["L1_ffn_gate_up_proj"].transpose(0, 2, 1)
    a["gate_up_bias_t"] = a["L1_ffn_gate_up_proj_bias"].reshape(E, 8, P).transpose(0, 2, 1)
    a["down_t"] = a["L1_ffn_down_proj"].transpose(0, 2, 1)
    arrays = {name: np.ascontiguousarray(a[name]) for name in _INS}
    arrays.update(tables())
    nc = bacc.Bacc("TRN2", target_bir_lowering=False, num_devices=1)
    aps = {name: nc.dram_tensor(f"in_{name}", v.shape, mybir.dt.from_np(v.dtype), kind="ExternalInput").ap()
           for name, v in arrays.items()}
    out = nc.dram_tensor("out", (B * S, D), F32, kind="ExternalOutput").ap()
    xattn_ffn_moe_kernel(nc, aps, out)
    r = run_bass_kernel_spmd(nc, [{f"in_{name}": v for name, v in arrays.items()}], core_ids=[0])
    return r.results[0]["out"].reshape(B, S, D)
```
